# Optimizing a Trainium2 kernel written in Bass

```python
import numpy as np
import jax
import jax.numpy as jnp

def _softmax(x, axis=-1):
    return jax.nn.softmax(x, axis=axis)

def _gelu(x):
    return jax.nn.gelu(x, approximate=True)

def _silu(x):
    return jax.nn.silu(x)

def _sigmoid(x):
    return jax.nn.sigmoid(x)

def _layernorm(x, axis=-1, eps=1e-05):
    m = jnp.mean(x, axis=axis, keepdims=True)
    v = jnp.var(x, axis=axis, keepdims=True)
    return (x - m) / jnp.sqrt(v + eps)

def _scatter_add(tgt, idx, src, axis=0):
    return tgt.at[idx].add(src)

def _segment_sum(src, seg, n):
    return jax.ops.segment_sum(src, seg, n)
kernel_name = 'mk_adaln_attn_ffn_d1_seqx_r8_47c608'

def setup_inputs(seed: int=0):
    np.random.seed(seed)
    _w = jnp.asarray

    def _rec_inputs():
        import jax
        import jax.numpy as jnp
        _rk = jax.random.key(seed)
        x = -0.0005207 + 1.001 * jax.random.normal(jax.random.fold_in(_rk, 1), (64, 32, 512), jnp.float32)
        _lenS = 32 - jax.random.randint(jax.random.fold_in(_rk, 7), (64,), 0, max(1, 32 // 4) + 1, jnp.int32)
        _lenS2 = 32 - jax.random.randint(jax.random.fold_in(_rk, 8), (64,), 0, max(1, 32 // 4) + 1, jnp.int32)
        itok_Bx16_0_63 = jax.random.randint(jax.random.fold_in(_rk, 11), (64, 16), 0, 64, jnp.int32)
        itok_B_207_1644 = jax.random.randint(jax.random.fold_in(_rk, 12), (64,), 207, 1645, jnp.int32)
        itok_B_0_30 = jax.random.randint(jax.random.fold_in(_rk, 13), (64,), 0, 31, jnp.int32)
        return (x, itok_Bx16_0_63, itok_B_207_1644, itok_B_0_30)
    x, itok_Bx16_0_63, itok_B_207_1644, itok_B_0_30 = _rec_inputs()

    def _L0_cond_setup():
        import jax, jax.numpy as jnp
        import numpy as np
        B, S, HID = (4, 128, 512)
        D, HQ, HK = (128, 32, 8)
        PAGES, PSIZE, NPP = (64, 32, 16)
        THETA = 10000.0
        EPS = 1e-06
        SCALE = 1.0 / float(np.sqrt(D))

        def _rmsnorm(t, w):
            var = jnp.mean(t * t, axis=-1, keepdims=True)
            return t * jax.lax.rsqrt(var + EPS) * w

        def _rope(t, pos):
            inv_freq = 1.0 / THETA ** (jnp.arange(0, D, 2, dtype=jnp.float32) / D)
            freqs = pos[..., None].astype(jnp.float32) * inv_freq
            cos = jnp.cos(freqs)[:, :, None, :]
            sin = jnp.sin(freqs)[:, :, None, :]
            t1, t2 = (t[..., :D // 2], t[..., D // 2:])
            return jnp.concatenate([t1 * cos - t2 * sin, t2 * cos + t1 * sin], axis=-1)
        key = jax.random.key(seed)
        ks = jax.random.split(key, 10)
        x = jax.random.normal(ks[0], (B, S, HID), jnp.float32)
        Wq = jax.random.normal(ks[1], (HQ * D, HID), jnp.float32) * 0.02
        Wk = jax.random.normal(ks[2], (HK * D, HID), jnp.float32) * 0.02
        Wv = jax.random.normal(ks[3], (HK * D, HID), jnp.float32) * 0.02
        Wo = jax.random.normal(ks[4], (HID, HQ * D), jnp.float32) * 0.02
        q_norm_w = jax.random.uniform(ks[5], (D,), jnp.float32)
        k_norm_w = jax.random.uniform(ks[6], (D,), jnp.float32)
        k_cache = jax.random.normal(ks[7], (PAGES, PSIZE, HK, D), jnp.float32)
        v_cache = jax.random.normal(ks[8], (PAGES, PSIZE, HK, D), jnp.float32)
        block_table = jnp.arange(B * NPP, dtype=jnp.int32).reshape(B, NPP)
        cache_seqlens = jax.random.randint(ks[9], (B,), 0, 475).astype(jnp.int32)
        return dict(x=x, Wq=Wq, Wk=Wk, Wv=Wv, Wo=Wo, q_norm_w=q_norm_w, k_norm_w=k_norm_w, k_cache=k_cache, v_cache=v_cache, block_table=block_table, cache_seqlens=cache_seqlens)
    _L0_cond_all = _L0_cond_setup()
    _L0_cond_in = {k: v for k, v in _L0_cond_all.items() if k in ('Wq', 'Wk', 'Wv', 'Wo', 'q_norm_w', 'k_norm_w', 'k_cache', 'v_cache')}
    del _L0_cond_all

    def _L0_attn_setup():
        import jax, jax.numpy as jnp
        import numpy as np
        B, S, EMB = (2, 256, 512)
        NHEADS, KVHEADS, HEAD_D = (32, 8, 128)
        SPLITS = (NHEADS * HEAD_D, KVHEADS * HEAD_D, KVHEADS * HEAD_D)
        key = jax.random.key(seed)
        k1, k2, k3 = jax.random.split(key, 3)
        q = jax.random.normal(k1, (B, S, EMB), dtype=jnp.float32)
        w_qkv = jax.random.normal(k2, (sum(SPLITS), EMB), dtype=jnp.float32) * 0.02
        w_dense = jax.random.normal(k3, (EMB, NHEADS * HEAD_D), dtype=jnp.float32) * 0.02
        return {'q': q, 'w_qkv': w_qkv, 'w_dense': w_dense}
    _L0_attn_all = _L0_attn_setup()
    _L0_attn_in = {k: v for k, v in _L0_attn_all.items() if k in ('w_qkv', 'w_dense')}
    del _L0_attn_all

    def _L0_cond2_setup():
        import jax, jax.numpy as jnp
        import numpy as np
        B, C, D, T, S = (64, 32, 32, 512, 32)
        key = jax.random.key(seed)
        k1, k2, k3 = jax.random.split(key, 3)
        x = jax.random.normal(k1, (B, C, T), dtype=jnp.float32)
        subjects = jax.random.randint(k2, (B,), 0, S, dtype=jnp.int64)
        weights = jax.random.normal(k3, (S, C, D), dtype=jnp.float32) * (1.0 / np.sqrt(C))
        return {'x': x, 'subjects': subjects, 'weights': weights}
    _L0_cond2_all = _L0_cond2_setup()
    _L0_cond2_in = {k: v for k, v in _L0_cond2_all.items() if k in ('weights',)}
    del _L0_cond2_all

    def _L0_ffn_setup():
        import jax, jax.numpy as jnp
        import numpy as np
        BATCH, TOK, DIM, OUT = (4, 256, 512, 512)
        E, R, TOP_K = (8, 16, 2)
        SCALING = 16.0 / R
        key = jax.random.key(seed)
        ks = jax.random.split(key, 6)
        return {'x': jax.random.normal(ks[0], (BATCH, TOK, DIM), dtype=jnp.float32), 'W_base': jax.random.normal(ks[1], (OUT, DIM), dtype=jnp.float32) / np.sqrt(DIM), 'b_base': jax.random.normal(ks[2], (OUT,), dtype=jnp.float32) * 0.01, 'W_gate': jax.random.normal(ks[3], (E, DIM), dtype=jnp.float32) * 0.01, 'A': jax.random.normal(ks[4], (E, R, DIM), dtype=jnp.float32) / np.sqrt(DIM), 'B': jax.random.normal(ks[5], (OUT, OUT // OUT * R * 0 + R), dtype=jnp.float32)[None].repeat(E, 0) * 0.0 + jax.random.normal(ks[5], (E, OUT, R), dtype=jnp.float32) * 0.02}
    _L0_ffn_all = _L0_ffn_setup()
    _L0_ffn_in = {k: v for k, v in _L0_ffn_all.items() if k in ('W_base', 'b_base', 'W_gate', 'A', 'B')}
    del _L0_ffn_all
    return {'x': x, 'itok_Bx16_0_63': itok_Bx16_0_63, 'itok_B_207_1644': itok_B_207_1644, 'itok_B_0_30': itok_B_0_30, 'L0_cond_Wq': _L0_cond_in['Wq'], 'L0_cond_Wk': _L0_cond_in['Wk'], 'L0_cond_Wv': _L0_cond_in['Wv'], 'L0_cond_Wo': _L0_cond_in['Wo'], 'L0_cond_q_norm_w': _L0_cond_in['q_norm_w'], 'L0_cond_k_norm_w': _L0_cond_in['k_norm_w'], 'L0_cond_k_cache': _L0_cond_in['k_cache'], 'L0_cond_v_cache': _L0_cond_in['v_cache'], 'L0_attn_w_qkv': _L0_attn_in['w_qkv'], 'L0_attn_w_dense': _L0_attn_in['w_dense'], 'L0_cond2_weights': _L0_cond2_in['weights'], 'L0_ffn_W_base': _L0_ffn_in['W_base'], 'L0_ffn_b_base': _L0_ffn_in['b_base'], 'L0_ffn_W_gate': _L0_ffn_in['W_gate'], 'L0_ffn_A': _L0_ffn_in['A'], 'L0_ffn_B': _L0_ffn_in['B']}

def reference(x, itok_Bx16_0_63, itok_B_207_1644, itok_B_0_30, L0_cond_Wq, L0_cond_Wk, L0_cond_Wv, L0_cond_Wo, L0_cond_q_norm_w, L0_cond_k_norm_w, L0_cond_k_cache, L0_cond_v_cache, L0_attn_w_qkv, L0_attn_w_dense, L0_cond2_weights, L0_ffn_W_base, L0_ffn_b_base, L0_ffn_W_gate, L0_ffn_A, L0_ffn_B):
    import jax
    import jax.numpy as jnp

    def _L0_cond_ref(x, Wq, Wk, Wv, Wo, q_norm_w, k_norm_w, k_cache, v_cache, block_table, cache_seqlens):
        import jax, jax.numpy as jnp
        import numpy as np
        B, S, HID = (4, 128, 512)
        D, HQ, HK = (128, 32, 8)
        PAGES, PSIZE, NPP = (64, 32, 16)
        THETA = 10000.0
        EPS = 1e-06
        SCALE = 1.0 / float(np.sqrt(D))

        def _rmsnorm(t, w):
            var = jnp.mean(t * t, axis=-1, keepdims=True)
            return t * jax.lax.rsqrt(var + EPS) * w

        def _rope(t, pos):
            inv_freq = 1.0 / THETA ** (jnp.arange(0, D, 2, dtype=jnp.float32) / D)
            freqs = pos[..., None].astype(jnp.float32) * inv_freq
            cos = jnp.cos(freqs)[:, :, None, :]
            sin = jnp.sin(freqs)[:, :, None, :]
            t1, t2 = (t[..., :D // 2], t[..., D // 2:])
            return jnp.concatenate([t1 * cos - t2 * sin, t2 * cos + t1 * sin], axis=-1)
        bsz, seqlen, _ = x.shape
        q = jnp.einsum('bsd,ed->bse', x, Wq).reshape(bsz, seqlen, HQ, D)
        k = jnp.einsum('bsd,ed->bse', x, Wk).reshape(bsz, seqlen, HK, D)
        v = jnp.einsum('bsd,ed->bse', x, Wv).reshape(bsz, seqlen, HK, D)
        q = _rmsnorm(q, q_norm_w)
        k = _rmsnorm(k, k_norm_w)
        pos = cache_seqlens[:, None] + jnp.arange(seqlen)[None, :]
        q = _rope(q, pos)
        k = _rope(k, pos)
        L = NPP * PSIZE
        kc = k_cache[block_table].reshape(bsz, L, HK, D)
        vc = v_cache[block_table].reshape(bsz, L, HK, D)
        k_all = jnp.concatenate([kc, k], axis=1)
        v_all = jnp.concatenate([vc, v], axis=1)
        valid_c = jnp.arange(L)[None, :] < cache_seqlens[:, None]
        valid = jnp.concatenate([valid_c, jnp.ones((bsz, seqlen), dtype=bool)], axis=1)
        rep = HQ // HK
        k_all = jnp.repeat(k_all, rep, axis=2)
        v_all = jnp.repeat(v_all, rep, axis=2)
        scores = jnp.einsum('bqhd,bkhd->bhqk', q, k_all) * SCALE
        scores = jnp.where(valid[:, None, None, :], scores, -1e+30)
        probs = jax.nn.softmax(scores, axis=-1)
        o = jnp.einsum('bhqk,bkhd->bqhd', probs, v_all)
        o = o.reshape(bsz, seqlen, HQ * D)
        return jnp.einsum('bse,de->bsd', o, Wo)

    def _L0_attn_ref(q, w_qkv, w_dense):
        import jax, jax.numpy as jnp
        import numpy as np
        B, S, EMB = (2, 256, 512)
        NHEADS, KVHEADS, HEAD_D = (32, 8, 128)
        SPLITS = (NHEADS * HEAD_D, KVHEADS * HEAD_D, KVHEADS * HEAD_D)
        Bq, Sq, _ = q.shape
        qkv = q @ w_qkv.T
        qs, ks, vs = jnp.split(qkv, np.cumsum(SPLITS)[:-1], axis=-1)
        G = NHEADS // KVHEADS
        qh = qs.reshape(Bq, Sq, KVHEADS, G, HEAD_D)
        kh = ks.reshape(Bq, Sq, KVHEADS, HEAD_D)
        vh = vs.reshape(Bq, Sq, KVHEADS, HEAD_D)
        scale = 1.0 / jnp.sqrt(jnp.float32(HEAD_D))
        scores = jnp.einsum('bskgd,btkd->bkgst', qh, kh) * scale
        causal = jnp.tril(jnp.ones((Sq, Sq), dtype=bool))
        scores = jnp.where(causal, scores, jnp.finfo(scores.dtype).min)
        probs = jax.nn.softmax(scores, axis=-1)
        attn = jnp.einsum('bkgst,btkd->bskgd', probs, vh)
        attn = attn.reshape(Bq, Sq, NHEADS * HEAD_D)
        return attn @ w_dense.T

    def _L0_cond2_ref(x, subjects, weights):
        import jax, jax.numpy as jnp
        import numpy as np
        B, C, D, T, S = (64, 32, 32, 512, 32)
        w = weights[subjects]
        return jnp.einsum('bct,bcd->bdt', x, w)

    def _L0_ffn_ref(x, W_base, b_base, W_gate, A, B):
        import jax, jax.numpy as jnp
        import numpy as np
        BATCH, TOK, DIM, OUT = (4, 256, 512, 512)
        E, R, TOP_K = (8, 16, 2)
        SCALING = 16.0 / R
        result = jnp.einsum('bnd,od->bno', x, W_base) + b_base
        logits = jnp.einsum('bnd,ed->bne', x, W_gate)
        probs = jax.nn.softmax(logits.astype(jnp.float32), axis=-1)
        top_p, top_i = jax.lax.top_k(probs, TOP_K)
        top_p = top_p / jnp.sum(top_p, axis=-1, keepdims=True)
        top_p = top_p.astype(x.dtype)
        route_w = jnp.sum(jax.nn.one_hot(top_i, E, dtype=x.dtype) * top_p[..., None], axis=-2)
        h = jnp.einsum('bnd,erd->bner', x, A)
        hw = h * route_w[..., None]
        delta = jnp.einsum('bner,eor->bno', hw, B)
        return result + delta * SCALING
    x = x + _L0_attn_ref(_L0_cond_ref(x, L0_cond_Wq, L0_cond_Wk, L0_cond_Wv, L0_cond_Wo, L0_cond_q_norm_w, L0_cond_k_norm_w, L0_cond_k_cache, L0_cond_v_cache, itok_Bx16_0_63, itok_B_207_1644), L0_attn_w_qkv, L0_attn_w_dense)
    x = x + _L0_ffn_ref(_L0_cond2_ref(x, itok_B_0_30, L0_cond2_weights), L0_ffn_W_base, L0_ffn_b_base, L0_ffn_W_gate, L0_ffn_A, L0_ffn_B)
    return x

_drawn_inputs = setup_inputs


def setup_inputs(seed=0):
    import zlib

    import numpy as np

    out = dict(_drawn_inputs(seed))
    spreads = {}
    factors = {'L0_cond_Wq': 6.649,
     'L0_cond_Wk': 8.0,
     'L0_cond_Wv': 8.0,
     'L0_cond_q_norm_w': 8.0,
     'L0_cond_k_norm_w': 8.0,
     'L0_cond_k_cache': 6.636,
     'L0_ffn_b_base': 8.0}
    for name, (base, spread) in spreads.items():
        noise = np.random.default_rng([zlib.crc32(name.encode()), seed]).standard_normal(out[name].shape)
        drawn = base * np.exp(spread * noise) if base else spread * noise
        out[name] = jnp.asarray(drawn.astype(out[name].dtype))
    for name, factor in factors.items():
        out[name] = (out[name] * factor).astype(out[name].dtype)
    return out
```

```python
import math
from contextlib import ExitStack

import numpy as np

import concourse.bass as bass
from concourse import mybir

F32 = mybir.dt.float32
F32R = mybir.dt.float32r
BF16 = mybir.dt.bfloat16
I32 = mybir.dt.int32
ACT = mybir.ActivationFunctionType
ALU = mybir.AluOpType
AX = mybir.AxisListType

B, S, HID = 64, 32, 512
TOK = B * S
P = 128
D, HQ, HK = 128, 32, 8
G = HQ // HK
PAGES, PSIZE, NPP = 64, 32, 16
L = PSIZE * NPP
KC = HID // P
TILES = TOK // P
SEQ = P // S
NT = 4
SPAN = TOK // NT
BS = B // NT
E, R = 8, 16
ER = E * R
THETA = 10000.0
EPS = 1e-6
SCALE = 1.0 / math.sqrt(D)
OUT_OF_REACH = -1e30
HALF = D // 2
GS = G * S


def split_product(pe, out, a_hi, a_lo, b_hi, b_lo, start, stop):
    pe.matmul(out, a_hi, b_hi, start=start, stop=False)
    pe.matmul(out, a_hi, b_lo, start=False, stop=False)
    return pe.matmul(out, a_lo, b_hi, start=False, stop=stop)


def stage1(nc, c, a, scratch):
    CB = 12
    UN = TILES // 2
    with ExitStack() as opened:
        hold = opened.enter_context
        x_raw = hold(nc.sbuf_tensor("x_raw", [P, 2, TOK], F32))
        x_hi = hold(nc.sbuf_tensor("x_hi", [P, KC, TOK], F32R))
        x_lo = hold(nc.sbuf_tensor("x_lo", [P, KC, TOK], F32R))
        w_raw = hold(nc.sbuf_tensor("w_raw", [P, 2, KC * 512], F32))
        w_hi = hold(nc.sbuf_tensor("w_hi", [P, 2, KC * 512], F32R))
        w_lo = hold(nc.sbuf_tensor("w_lo", [P, 2, KC * 512], F32R))
        tab_q = hold(nc.sbuf_tensor("tab_q", [P, 2, TILES, D], F32))
        tab_k = hold(nc.sbuf_tensor("tab_k", [P, 2, TILES, D], F32))
        squares = hold(nc.sbuf_tensor("squares", [P, 2, 1024], BF16))
        unit_rows = hold(nc.sbuf_tensor("unit_rows", [P, 1024], F32))
        turning = hold(nc.sbuf_tensor("turning", [P, 2, 1024], F32))
        by_cos = hold(nc.sbuf_tensor("by_cos", [P, 1024], F32))
        by_sin = hold(nc.sbuf_tensor("by_sin", [P, 1024], F32))
        turned = hold(nc.sbuf_tensor("turned", [P, 2, 1024], F32))
        sumsq = hold(nc.sbuf_tensor("sumsq", [P, 2, 8], F32))
        root = hold(nc.sbuf_tensor("root", [P, 2, 8], F32))
        nw = hold(nc.sbuf_tensor("nw", [P, 4, 8], F32))
        eps = hold(nc.sbuf_tensor("eps", [P, 1], F32))
        ps_proj = hold(nc.psum_tensor("ps_proj", [P, 2, 2, 512], F32))
        ps_turn = hold(nc.psum_tensor("ps_turn", [P, 2, 2, 512], F32))
        x_loaded0 = hold(nc.semaphore("x_loaded0"))
        x_loaded1 = hold(nc.semaphore("x_loaded1"))
        x_hi_done = hold(nc.semaphore("x_hi_done"))
        x_lo_done = hold(nc.semaphore("x_lo_done"))
        w_loaded0 = hold(nc.semaphore("w_loaded0"))
        w_loaded1 = hold(nc.semaphore("w_loaded1"))
        w_hi_done = hold(nc.semaphore("w_hi_done"))
        w_lo_done = hold(nc.semaphore("w_lo_done"))
        proj_done = hold(nc.semaphore("proj_done"))
        proj_free = hold(nc.semaphore("proj_free"))
        root_done = hold(nc.semaphore("root_done"))
        dve_step = hold(nc.semaphore("dve_step"))
        halves_done = hold(nc.semaphore("halves_done"))
        rotated = hold(nc.semaphore("rotated"))
        turn_done = hold(nc.semaphore("turn_done"))
        turned_done = hold(nc.semaphore("turned_done"))
        store0_free = hold(nc.semaphore("store0_free"))
        store1_free = hold(nc.semaphore("store1_free"))
        v_copied = hold(nc.semaphore("v_copied"))
        eps_set = hold(nc.semaphore("eps_set"))
        const_loaded = hold(nc.semaphore("const_loaded"))
        pos_ready = hold(nc.semaphore("pos_ready"))
        sines = hold(nc.semaphore("sines"))
        ident_step = hold(nc.semaphore("ident_step"))
        own_set = hold(nc.semaphore("own_set"))
        block = hold(nc.Block())
        x_loaded = [x_loaded0, x_loaded1]
        w_loaded = [w_loaded0, w_loaded1]
        store_free = [store0_free, store1_free]
        angle = turning[:, 0, :].rearrange("p (t f) -> p t f", f=HALF)
        turns = turning[:, 1, :].rearrange("p (t f) -> p t f", f=HALF)
        sin_t = by_cos[:, :].rearrange("p (t f) -> p t f", f=HALF)
        cos_t = by_sin[:, :].rearrange("p (t f) -> p t f", f=HALF)
        freq = turned[:, 0, 0:HALF]
        wq_row = turned[:, 0, 128:256]
        wk_row = turned[:, 0, 256:384]
        len_i = turned[:, 0, 512:512 + TILES].bitcast(I32)
        pos_f = turned[:, 0, 640:640 + TILES]

        @block.sync
        def _(sp):
            sp.sem_inc(store_free[0], 16)
            sp.sem_inc(store_free[1], 16)
            for k in range(2):
                sp.dma_start(x_raw[:, k, :], a["xT"][k * P:(k + 1) * P, :]).then_inc(x_loaded[k], 16)
            for k in range(2):
                sp.dma_start(w_raw[:, k, :], a["w1"][k]).then_inc(w_loaded[k], 16)
            sp.dma_start(freq, a["freq"].to_broadcast([P, HALF])).then_inc(const_loaded, 16)
            sp.dma_start(wq_row, a["qw"].to_broadcast([P, D])).then_inc(const_loaded, 16)
            sp.dma_start(wk_row, a["kw"].to_broadcast([P, D])).then_inc(const_loaded, 16)
            for s in range(SEQ):
                r = slice(s * S, (s + 1) * S)
                sp.dma_start(len_i[r, :], a["lens_t"][s:s + 1, :].to_broadcast([S, TILES])).then_inc(const_loaded, 16)
                sp.dma_start(c["subj"][r, :], a["subj_t"][s:s + 1, :].to_broadcast([S, TILES])).then_inc(const_loaded, 16)
                sp.dma_start(c["vrow"][r, :], a["table_t"][s:s + 1, :].to_broadcast([S, B * 4])).then_inc(const_loaded, 16)
            sp.dma_start(c["len_all"][:, :], a["lens"].to_broadcast([P, B])).then_inc(const_loaded, 16)
            sp.dma_start(c["table"][0:1, :], a["table"]).then_inc(const_loaded, 16)
            for k in range(2, KC):
                sp.wait_ge(x_lo_done, k - 1)
                sp.dma_start(x_raw[:, k % 2, :], a["xT"][k * P:(k + 1) * P, :]).then_inc(x_loaded[k % 2], 16)

            def block_of(i, cb, kind):
                if kind != "v":
                    sp.wait_ge(w_lo_done, i * 2 + cb + 1)
                    sp.dma_start(w_raw[:, cb, :],
                                 a["w1"][bass.ds(i * 2 + cb + 2, 1)].rearrange("o p n -> p (o n)")).then_inc(w_loaded[cb], 16)
                for u in range(UN):
                    n = i * 2 * UN + cb * UN + u
                    b0 = u * 2 * SEQ
                    if kind == "q":
                        dst = scratch["qT"][b0:b0 + 2 * SEQ, :, bass.ds(i * 2 + cb, 1), :].rearrange("b p o n -> p b (o n)")
                    elif kind == "k":
                        dst = scratch["kT"][b0:b0 + 2 * SEQ, :, cb, :].rearrange("b p n -> p b n")
                    else:
                        dst = scratch["v"][u * 2 * P:(u + 1) * 2 * P, cb * 512:(cb + 1) * 512].rearrange("(t p) n -> p t n", p=P)
                    if kind == "v":
                        sp.wait_ge(v_copied, cb * UN + u + 1)
                        src = turned[:, u % 2, :].rearrange("p (t n) -> p t n", t=2)
                    else:
                        sp.wait_ge(turned_done, n + 1)
                        src = turned[:, u % 2, :].rearrange("p (b n) -> p b n", n=GS)
                    sp.dma_start(dst, src).then_inc(store_free[u % 2], 16)

            with sp.Fori(0, 4) as i:
                for cb in range(2):
                    block_of(i, cb, "q")
            for cb in range(2):
                block_of(4, cb, "k")
            for cb in range(2):
                block_of(5, cb, "v")
            for k in range(2):
                sp.wait_ge(store_free[k], 16 + 16 * CB * UN // 2)
            sp.wait_ge(const_loaded, 16 * (5 + 3 * SEQ))

        @block.gpsimd
        def _(pool):
            pool.sem_inc(rotated, 1)
            pool.memset(c["ident"][:, :], 0.0).then_inc(ident_step, 1)
            for s in range(SEQ):
                pool.wait_ge(ident_step, s + 1)
                pool.iota(c["tok_i"][s * S:(s + 1) * S, :], pattern=[[0, 1]], base=0, channel_multiplier=1).then_inc(ident_step, 1)
            pool.wait_ge(ident_step, SEQ + 1)
            pool.iota(c["key_i"][:, :], pattern=[[1, L]], base=0, channel_multiplier=0).then_inc(ident_step, 1)
            pool.wait_ge(ident_step, SEQ + 2)
            pool.affine_select(out=c["ident"][:, :], in_=c["ident"][:, :], compare_op=ALU.not_equal, fill=1.0,
                               base=0, pattern=[[-1, P]], channel_multiplier=1).then_inc(ident_step, 1)
            with pool.Fori(0, 10) as cb:
                for u in range(UN):
                    pool.wait_ge(halves_done, cb * UN + u + 1)
                    pool.tensor_tensor(turning[:, u % 2, :], by_cos[:, :], by_sin[:, :], ALU.add).then_inc(rotated, 1)

        @block.scalar
        def _(act):
            for k in range(KC):
                act.wait_ge(x_loaded[k % 2], 16 * (k // 2 + 1))
                act.activation(x_hi[:, k, :], x_raw[:, k % 2, :], ACT.Copy).then_inc(x_hi_done, 1)
                if k == 0:
                    act.wait_ge(w_loaded[0], 16)
                    act.activation(w_hi[:, 0, :], w_raw[:, 0, :], ACT.Copy).then_inc(w_hi_done, 1)
            act.wait_ge(pos_ready, 1)
            act.activation(sin_t, angle, ACT.Sin).then_inc(sines, 1)
            act.activation(cos_t, angle, ACT.Sin, scale=0.5).then_inc(sines, 1)
            act.wait_ge(eps_set, 1)

            def roots(n, u):
                act.wait_ge(proj_done, n + 1)
                for t in range(2):
                    for g in range(G):
                        h = t * G + g
                        m = act.activation(squares[:, u % 2, h * D:(h + 1) * D], ps_proj[:, u % 2, t, g * D:(g + 1) * D], ACT.Square,
                                           accum_out=sumsq[:, u % 2, h:h + 1])
                m.then_inc(root_done, 1)
                act.wait_ge(root_done, n * 2 + 1)
                act.activation(root[:, u % 2, :], sumsq[:, u % 2, :], ACT.Sqrt, bias=eps[:, 0:1], scale=1.0 / D).then_inc(root_done, 1)

            def turn_copy(n, half, u):
                act.wait_ge(turn_done, n + 1)
                act.wait_ge(store_free[u % 2], half * 16 + 16)
                for t in range(2):
                    src = ps_turn[:, u % 2, t, :].rearrange("p (g b s) -> p g b s", g=G, b=SEQ)
                    dst = turned[:, u % 2, t * 512:(t + 1) * 512].rearrange("p (b g s) -> p g b s", g=G, b=SEQ)
                    m = act.activation(dst, src, ACT.Copy)
                m.then_inc(turned_done, 1)

            def split(slot, load):
                act.wait_ge(w_loaded[slot], load * 16 + 16)
                act.activation(w_hi[:, slot, :], w_raw[:, slot, :], ACT.Copy).then_inc(w_hi_done, 1)

            def block_of(i, cb, kind):
                for u in range(UN):
                    n = i * 2 * UN + cb * UN + u
                    if kind == "v":
                        act.wait_ge(proj_done, n + 1)
                        act.wait_ge(store_free[u % 2], (i * UN + cb * (UN // 2) + u // 2) * 16 + 16)
                        for t in range(2):
                            m = act.activation(turned[:, u % 2, t * 512:(t + 1) * 512], ps_proj[:, u % 2, t, :], ACT.Copy)
                        m.then_inc(v_copied, 1)
                    else:
                        roots(n, u)
                        if u > 0:
                            turn_copy(n - 1, i * UN + cb * (UN // 2) + (u - 1) // 2, u - 1)
                    if u == 3 and not (kind == "v" and cb == 1):
                        split((cb + 1) % 2, i + cb)
                if kind != "v":
                    turn_copy(i * 2 * UN + cb * UN + UN - 1, i * UN + cb * (UN // 2) + UN // 2 - 1, UN - 1)

            with act.Fori(0, 4) as i:
                for cb in range(2):
                    block_of(i, cb, "q")
            for cb in range(2):
                block_of(4, cb, "k")
            for cb in range(2):
                block_of(5, cb, "v")

        @block.vector
        def _(dve):
            steps = [0]

            def step(m):
                steps[0] += 1
                m.then_inc(dve_step, 1)
                dve.wait_ge(dve_step, steps[0])

            dve.sem_inc(proj_free, 2)
            dve.memset(eps[:, :], EPS).then_inc(eps_set, 1)
            for k in range(KC):
                dve.wait_ge(x_hi_done, k + 1)
                dve.tensor_tensor(x_lo[:, k, :], x_raw[:, k % 2, :], x_hi[:, k, :].bitcast(F32), ALU.subtract).then_inc(x_lo_done, 1)
                if k == 0:
                    dve.wait_ge(w_hi_done, 1)
                    dve.tensor_tensor(w_lo[:, 0, :], w_raw[:, 0, :], w_hi[:, 0, :].bitcast(F32), ALU.subtract).then_inc(w_lo_done, 1)
            dve.wait_ge(const_loaded, 16 * (5 + 3 * SEQ))
            dve.wait_ge(ident_step, SEQ + 3)
            step(dve.tensor_copy(c["tok_f"][:, :], c["tok_i"][:, :]))
            step(dve.tensor_copy(c["key_f"][:, :], c["key_i"][:, :]))
            step(dve.tensor_scalar(c["vrow"][:, :], c["vrow"][:, :], float(PSIZE), c["tok_f"][:, 0:1], ALU.mult, ALU.add))
            step(dve.tensor_scalar(c["subj"][:, :], c["subj"][:, :], float(S), c["tok_f"][:, 0:1], ALU.mult, ALU.add))
            step(dve.tensor_copy(c["len_f"][:, :], c["len_all"][:, :]))
            step(dve.tensor_scalar(c["causal"][:, :], c["key_f"][:, 0:S], c["tok_f"][:, 0:1], OUT_OF_REACH, ALU.is_gt, ALU.mult))
            dve.memset(c["own_seq"][:, :], 0.0).then_inc(own_set, 1)
            dve.wait_ge(own_set, 1)
            for s in range(SEQ):
                dve.memset(c["own_seq"][s * S:(s + 1) * S, s:s + 1], 1.0).then_inc(own_set, 1)
            step(dve.tensor_copy(pos_f, len_i))
            step(dve.tensor_scalar(pos_f, pos_f, c["tok_f"][:, 0:1], None, ALU.add))
            step(dve.tensor_tensor(angle, pos_f.rearrange("p (t o) -> p t o", o=1).to_broadcast([P, TILES, HALF]),
                                   freq.rearrange("p (o f) -> p o f", o=1).to_broadcast([P, TILES, HALF]), ALU.mult))
            magic = 1.5 * 2.0 ** 23
            step(dve.tensor_scalar(turns, angle, 1.0 / (2 * math.pi), magic, ALU.mult, ALU.add))
            step(dve.tensor_scalar(turns, turns, magic, None, ALU.subtract))
            c1 = 6.28125
            c2 = math.floor((2 * math.pi - c1) * 2 ** 22) / 2 ** 22
            c3 = 2 * math.pi - c1 - c2
            for part in (c1, c2, c3):
                step(dve.scalar_tensor_tensor(out=angle, in0=turns, scalar=-part, in1=angle, op0=ALU.mult, op1=ALU.add))
            edge = math.pi * (1 - 1e-7)
            dve.tensor_scalar(angle, angle, edge, -edge, ALU.min, ALU.max).then_inc(pos_ready, 1)
            dve.wait_ge(sines, 2)
            step(dve.tensor_tensor(cos_t, cos_t, cos_t, ALU.mult))
            step(dve.tensor_scalar(cos_t, cos_t, -2.0, 1.0, ALU.mult, ALU.add))
            for tab, row in ((tab_q, wq_row), (tab_k, wk_row)):
                for half in range(2):
                    cols = slice(half * HALF, (half + 1) * HALF)
                    other = slice((1 - half) * HALF, (2 - half) * HALF)

                    def w(part):
                        return row[:, part].rearrange("p (o f) -> p o f", o=1).to_broadcast([P, TILES, HALF])
                    step(dve.tensor_tensor(tab[:, 0, :, cols], cos_t, w(cols), ALU.mult))
                    step(dve.tensor_tensor(tab[:, 1, :, cols], sin_t, w(other), ALU.mult))
                step(dve.tensor_scalar(tab[:, 1, :, 0:HALF], tab[:, 1, :, 0:HALF], -1.0, None, ALU.mult))
            before = steps[0]

            def unit(i, cb, u, tab):
                n = i * 2 * UN + cb * UN + u
                m = n * 6 + before
                ss, rt = sumsq[:, u % 2, :], root[:, u % 2, :]
                dve.wait_ge(root_done, n * 2 + 2)
                dve.tensor_scalar(nw[:, 0, :], ss, 1.0 / D, EPS, ALU.mult, ALU.add).then_inc(dve_step, 1)
                dve.reciprocal(nw[:, 1, :], rt).then_inc(dve_step, 1)
                dve.wait_ge(dve_step, m + 2)
                dve.tensor_tensor(nw[:, 2, :], nw[:, 1, :], nw[:, 1, :], ALU.mult).then_inc(dve_step, 1)
                dve.wait_ge(dve_step, m + 3)
                dve.tensor_tensor(nw[:, 2, :], nw[:, 2, :], nw[:, 0, :], ALU.mult).then_inc(dve_step, 1)
                dve.wait_ge(dve_step, m + 4)
                dve.tensor_scalar(nw[:, 2, :], nw[:, 2, :], -0.5, 1.5, ALU.mult, ALU.add).then_inc(dve_step, 1)
                dve.wait_ge(dve_step, m + 5)
                dve.tensor_tensor(nw[:, 3, :], nw[:, 2, :], nw[:, 1, :], ALU.mult).then_inc(dve_step, 1)
                dve.wait_ge(dve_step, m + 6)
                dve.tensor_tensor(unit_rows[:, :].rearrange("p (h d) -> p h d", d=D),
                                  ps_proj[:, u % 2, :, :].rearrange("p t (g d) -> p (t g) d", d=D),
                                  nw[:, 3, :].rearrange("p (h o) -> p h o", o=1).to_broadcast([P, 8, D]),
                                  ALU.mult).then_inc(proj_free, 1)
                dve.wait_ge(proj_free, n + 3)
                dve.wait_ge(rotated, n + 1)
                for t in range(2):
                    q3 = unit_rows[:, t * 512:(t + 1) * 512].rearrange("p (g d) -> p g d", d=D)
                    cos3 = tab[:, 0, 2 * u + t, :].rearrange("p (o d) -> p o d", o=1).to_broadcast([P, G, D])
                    dve.tensor_tensor(by_cos[:, t * 512:(t + 1) * 512].rearrange("p (g d) -> p g d", d=D), q3, cos3, ALU.mult)
                    for half in range(2):
                        cols = slice(half * HALF, (half + 1) * HALF)
                        other = slice((1 - half) * HALF, (2 - half) * HALF)
                        sin3 = tab[:, 1, 2 * u + t, cols].rearrange("p (o d) -> p o d", o=1).to_broadcast([P, G, HALF])
                        k = dve.tensor_tensor(by_sin[:, t * 512:(t + 1) * 512].rearrange("p (g d) -> p g d", d=D)[:, :, cols],
                                              q3[:, :, other], sin3, ALU.mult)
                k.then_inc(halves_done, 1)

            def split(cb, slot):
                dve.wait_ge(w_hi_done, cb + 1)
                dve.tensor_tensor(w_lo[:, slot, :], w_raw[:, slot, :], w_hi[:, slot, :].bitcast(F32), ALU.subtract).then_inc(w_lo_done, 1)

            with dve.Fori(0, 4) as i:
                for cb in range(2):
                    for u in range(UN):
                        unit(i, cb, u, tab_q)
                        if u == 3:
                            split(i * 2 + cb + 1, (cb + 1) % 2)
            for cb in range(2):
                for u in range(UN):
                    unit(4, cb, u, tab_k)
                    if u == 3:
                        split(9 + cb, (cb + 1) % 2)
            split(11, 1)

        @block.tensor
        def _(pe):
            def project(n, blk, slot, u):
                if u == 0:
                    pe.wait_ge(w_lo_done, blk + 1)
                if isinstance(n, int) and n >= 82:
                    pe.wait_ge(v_copied, n - 81)
                else:
                    pe.wait_ge(proj_free, n + 1)
                for t in range(2):
                    cols = slice((2 * u + t) * P, (2 * u + t + 1) * P)
                    for k in range(KC):
                        w = slice(k * 512, (k + 1) * 512)
                        m = split_product(pe, ps_proj[:, u % 2, t, :], x_hi[:, k, cols], x_lo[:, k, cols],
                                          w_hi[:, slot, w], w_lo[:, slot, w], k == 0, k == KC - 1)
                m.then_inc(proj_done, 1)

            def turn(n, u):
                pe.wait_ge(rotated, n + 2)
                for t in range(2):
                    for g in range(G):
                        j = t * G + g
                        m = pe.transpose(ps_turn[:, u % 2, t, g * P:(g + 1) * P], turning[:, u % 2, j * P:(j + 1) * P], c["ident"][:, :])
                m.then_inc(turn_done, 1)

            def block_of(i, cb, kind):
                for u in range(UN):
                    n = i * 2 * UN + cb * UN + u
                    blk = i * 2 + cb
                    if u < UN - 1:
                        project(n + 1, blk, cb, u + 1)
                    elif not (kind == "v" and cb == 1):
                        project(n + 1, blk + 1, 1 - cb, 0)
                    if kind != "v":
                        turn(n, u)

            pe.wait_ge(x_lo_done, KC)
            pe.wait_ge(ident_step, SEQ + 3)
            project(0, 0, 0, 0)
            with pe.Fori(0, 4) as i:
                for cb in range(2):
                    block_of(i, cb, "q")
            for cb in range(2):
                block_of(4, cb, "k")
            for cb in range(2):
                block_of(5, cb, "v")


def stage2(nc, c, a, scratch):
    with ExitStack() as opened:
        hold = opened.enter_context
        k_pool = hold(nc.sbuf_tensor("k_pool", [P, PAGES, HK * PSIZE], F32))
        k_cached = hold(nc.sbuf_tensor("k_cached", [P, 2, NPP, HK * PSIZE], F32))
        v_cached = hold(nc.sbuf_tensor("v_cached", [P, 2, 4, HK * D], F32))
        k_own = hold(nc.sbuf_tensor("k_own", [P, 2, HK * S], F32))
        v_own = hold(nc.sbuf_tensor("v_own", [S, 2, HK * D], F32))
        q_t = hold(nc.sbuf_tensor("q_t", [P, 2, HK, GS], F32))
        reach = hold(nc.sbuf_tensor("reach", [P, 2, L + S], F32))
        masked = hold(nc.sbuf_tensor("masked", [P, 2, L + S], F32))
        probs = hold(nc.sbuf_tensor("probs", [P, 2, L + S], F32))
        weights = hold(nc.sbuf_tensor("weights", [P, 2, L + S], F32))
        weights_t = hold(nc.sbuf_tensor("weights_t", [P, 2, 5 * P], F32))
        o_t = hold(nc.sbuf_tensor("o_t", [P, 2, HK * GS], F32))
        top = hold(nc.sbuf_tensor("top", [P, 4], F32))
        shift = hold(nc.sbuf_tensor("shift", [P, 4], F32))
        total = hold(nc.sbuf_tensor("total", [P, 4], F32))
        inv = hold(nc.sbuf_tensor("inv", [P, 4], F32))
        rows_now = hold(nc.sbuf_tensor("rows_now", [P, 2, 4], I32))
        ps_scores = hold(nc.psum_tensor("ps_scores", [P, 2, 1024], F32))
        ps_turn2 = hold(nc.psum_tensor("ps_turn2", [P, 1024], F32))
        ps_o = hold(nc.psum_tensor("ps_o", [P, 2, 512], F32))
        pool_loaded = hold(nc.semaphore("pool_loaded"))
        own_loaded = [hold(nc.semaphore(f"own_loaded{k}")) for k in range(2)]
        v_loaded = [hold(nc.semaphore(f"v_loaded{k}")) for k in range(2)]
        k_gathered = hold(nc.semaphore("k_gathered"))
        rows_ready = hold(nc.semaphore("rows_ready"))
        scores_done = hold(nc.semaphore("scores_done"))
        top_done = hold(nc.semaphore("top_done"))
        shift_done = hold(nc.semaphore("shift_done"))
        exp_done = hold(nc.semaphore("exp_done"))
        inv_done = hold(nc.semaphore("inv_done"))
        scaled = hold(nc.semaphore("scaled"))
        turns_done = hold(nc.semaphore("turns_done"))
        wt_done = hold(nc.semaphore("wt_done"))
        wt_tail_done = hold(nc.semaphore("wt_tail_done"))
        pv_done = hold(nc.semaphore("pv_done"))
        o_bank_free = hold(nc.semaphore("o_bank_free"))
        o_store_free = [hold(nc.semaphore(f"o_store{k}_free")) for k in range(2)]
        reach_done = hold(nc.semaphore("reach_done"))
        dve_passed = hold(nc.semaphore("dve_passed"))
        pool_passed = hold(nc.semaphore("pool_passed"))
        block = hold(nc.Block())
        LAST = B // 2 - 1

        @block.sync
        def _(sp):
            def load_own(b, slot):
                sp.dma_start(q_t[:, slot, :, :], scratch["qT"][bass.ds(b, 1)].rearrange("o p h n -> p (o h) n")).then_inc(own_loaded[slot], 16)
                sp.dma_start(k_own[:, slot, :], scratch["kT"][bass.ds(b, 1)].rearrange("o p h n -> p (o h n)")).then_inc(own_loaded[slot], 16)
                sp.dma_start(v_own[:, slot, :], scratch["v"][bass.ds(b * S, S), :]).then_inc(own_loaded[slot], 16)

            for k in range(2):
                sp.sem_inc(o_store_free[k], 16)
            for k in range(4):
                pages = slice(k * PAGES // 4, (k + 1) * PAGES // 4)
                cols = slice(k * PAGES // 4 * HK * PSIZE, (k + 1) * PAGES // 4 * HK * PSIZE)
                sp.dma_start(k_pool[:, pages, :].rearrange("p a n -> p (a n)"), a["kpool"][:, cols]).then_inc(pool_loaded, 16)
            load_own(0, 0)

            def pair_of(i, last):
                for j in range(2):
                    b = i * 2 + j
                    if not (last and j == 1):
                        sp.wait_ge(pv_done, b * HK + 1)
                        load_own(b + 1, 1 - j)
                    sp.wait_ge(o_bank_free, b * 2 + 4)
                    sp.dma_start(scratch["oT"][bass.ds(b, 1)].rearrange("o p h n -> p (o h n)"), o_t[:, j, :]).then_inc(o_store_free[j], 16)

            with sp.Fori(0, LAST) as i:
                pair_of(i, False)
            pair_of(LAST, True)
            for k in range(2):
                sp.wait_ge(o_store_free[k], 16 + 16 * (B // 2))

        @block.gpsimd
        def _(pool):
            def gather_v(b, slot):
                pool.tensor_copy(rows_now[:, slot, :], c["vrow"][:, bass.ds(b * 4, 4)]).then_inc(rows_ready, 1)
                pool.wait_ge(rows_ready, b + 1)
                pool.sem_inc(pool_passed)
                for k in range(4):
                    pool.indirect_dma_start(out=v_cached[:, slot, k, :], out_offset=None, in_=a["vpool"],
                                            in_offset=bass.IndirectOffsetOnAxis(ap=rows_now[:, slot, k:k + 1], axis=0)
                                            ).then_inc(v_loaded[slot], 16)

            gather_v(0, 0)

            def pair_of(i, last):
                for k in range(2 * HK):
                    n = i * 2 * HK + k
                    if k % HK == 1 and not (last and k > HK):
                        pool.wait_ge(pv_done, i * 2 * HK + k)
                        gather_v(i * 2 + k // HK + 1, 1 - k // HK)
                    pool.wait_ge(inv_done, n + 1)
                    pool.tensor_tensor(weights[:, k % 2, :], probs[:, k % 2, :], inv[:, k % 4:k % 4 + 1].to_broadcast([P, L + S]),
                                       ALU.mult).then_inc(scaled, 1)

            with pool.Fori(0, LAST) as i:
                pair_of(i, False)
            pair_of(LAST, True)

        @block.scalar
        def _(act):
            act.sem_inc(o_bank_free, 2)

            def gather_k(b, slot, pages, part):
                _, page = nc.values_load_multi_w_load_instructions(
                    c["table"][0:1, bass.ds(b * NPP + part, pages)], engines=(mybir.EngineType.Activation,),
                    min_val=0, max_val=PAGES - 1, skip_runtime_bounds_check_because="the reference's indices lie in the pool")
                for k in range(pages):
                    m = act.activation(k_cached[:, slot, part + k, :],
                                       k_pool[:, bass.ds(page[k], 1), :].rearrange("p o n -> p (o n)"), ACT.Copy)
                if part + pages == NPP:
                    m.then_inc(k_gathered, 1)

            def exps(n, k):
                act.wait_ge(shift_done, n + 1)
                act.activation(probs[:, k % 2, :], masked[:, k % 2, :], ACT.Exp, bias=shift[:, k % 4:k % 4 + 1], scale=SCALE,
                               accum_out=total[:, k % 4:k % 4 + 1]).then_inc(exp_done, 1)

            act.wait_ge(pool_loaded, 64)
            for part in range(0, NPP, 4):
                gather_k(0, 0, 4, part)
            exps(0, 0)
            exps(1, 1)

            def pair_of(i, last):
                for k in range(2 * HK):
                    n = i * 2 * HK + k
                    act.wait_ge(turns_done, n + 1)
                    act.activation(weights_t[0:S, k % 2, 4 * P:5 * P], ps_turn2[0:S, 512:512 + P], ACT.Copy).then_inc(wt_tail_done, 1)
                    if k % HK < 4 and not (last and k >= HK):
                        gather_k(i * 2 + k // HK + 1, 1 - k // HK, 4, 4 * (k % HK))
                    if not (last and k >= 2 * HK - 2):
                        exps(n + 2, k + 2)
                    if k % 4 == 3:
                        act.wait_ge(pv_done, n + 1)
                        if k % HK == 3:
                            act.wait_ge(o_store_free[k // HK], i * 16 + 16)
                        act.activation(o_t[:, k // HK, (k // 4) % 2 * 512:((k // 4) % 2 + 1) * 512], ps_o[:, (k // 4) % 2, :],
                                       ACT.Copy).then_inc(o_bank_free, 1)

            with act.Fori(0, LAST) as i:
                pair_of(i, False)
            pair_of(LAST, True)

        @block.vector
        def _(dve):
            def reach_of(b, slot):
                m = dve.tensor_scalar(reach[:, slot, 0:L], c["key_f"][:, :], c["len_f"][:, bass.ds(b, 1)], OUT_OF_REACH, ALU.is_ge, ALU.mult)
                m.then_inc(reach_done, 1)

            def maximum(n, k, b):
                dve.wait_ge(scores_done, n + 1)
                dve.wait_ge(reach_done, b + 2)
                dve.sem_inc(dve_passed)
                dve.tensor_tensor_reduce(masked[:, k % 2, :], ps_scores[:, k % 2, 0:L + S], reach[:, (k // HK) % 2, :], 1.0,
                                         -3.0e38, ALU.add, ALU.max, top[:, k % 4:k % 4 + 1]).then_inc(top_done, 1)
                dve.wait_ge(top_done, n + 1)
                dve.tensor_scalar(shift[:, k % 4:k % 4 + 1], top[:, k % 4:k % 4 + 1], -SCALE, None, ALU.mult).then_inc(shift_done, 1)

            def inverse(n, k):
                dve.wait_ge(exp_done, n + 1)
                dve.reciprocal(inv[:, k % 4:k % 4 + 1], total[:, k % 4:k % 4 + 1]).then_inc(inv_done, 1)

            dve.memset(reach[:, :, L:L + S], 0.0).then_inc(reach_done, 1)
            reach_of(0, 0)
            maximum(0, 0, 0)
            maximum(1, 1, 0)
            inverse(0, 0)

            def pair_of(i, last):
                for k in range(2 * HK):
                    n = i * 2 * HK + k
                    if not (last and k == 2 * HK - 1):
                        inverse(n + 1, k + 1)
                    if k % HK == 4 and not (last and k > HK):
                        reach_of(i * 2 + k // HK + 1, 1 - k // HK)
                    dve.wait_ge(turns_done, n + 1)
                    dve.tensor_copy(weights_t[:, k % 2, 0:4 * P], ps_turn2[:, 0:512]).then_inc(wt_done, 1)
                    if not (last and k >= 2 * HK - 2):
                        maximum(n + 2, k + 2, i * 2 + (k + 2) // HK)

            with dve.Fori(0, LAST) as i:
                pair_of(i, False)
            pair_of(LAST, True)

        @block.tensor
        def _(pe):
            def scores(n, k, i):
                h, j = k % HK, (k // HK) % 2
                if h == 0:
                    pe.wait_ge(own_loaded[j], (i + k // (2 * HK)) * 48 + 48)
                    pe.wait_ge(k_gathered, i * 2 + k // HK + 1)
                if not isinstance(n, int) or n >= 2:
                    pe.wait_ge(top_done, n - 1)
                pe.matmul(ps_scores[:, k % 2, 0:L], q_t[:, j, h, :], k_cached[:, j, :, h * PSIZE:(h + 1) * PSIZE], start=True, stop=True)
                pe.matmul(ps_scores[:, k % 2, L:L + S], q_t[:, j, h, :], k_own[:, j, h * S:(h + 1) * S],
                          start=True, stop=True).then_inc(scores_done, 1)

            pe.wait_ge(pool_loaded, 64)
            scores(0, 0, 0)
            scores(1, 1, 0)

            def pair_of(i, last):
                for k in range(2 * HK):
                    n = i * 2 * HK + k
                    h, j = k % HK, k // HK
                    pe.wait_ge(scaled, n + 1)
                    for t in range(4):
                        pe.transpose(ps_turn2[:, t * P:(t + 1) * P], weights[:, k % 2, t * P:(t + 1) * P], c["ident"][:, :])
                    pe.transpose(ps_turn2[0:S, 512:512 + P], weights[:, k % 2, L:L + S], c["ident"][:, :]).then_inc(turns_done, 1)
                    if not (last and k >= 2 * HK - 2):
                        scores(n + 2, k + 2, i)
                    if h == 0:
                        pe.wait_ge(v_loaded[j], i * 64 + 64)
                    if k % 4 == 0:
                        pe.wait_ge(o_bank_free, i * 4 + k // 4 + 1)
                    pe.wait_ge(wt_done, n + 1)
                    pe.wait_ge(wt_tail_done, n + 1)
                    bank = ps_o[:, (k // 4) % 2, (k % 4) * P:(k % 4 + 1) * P]
                    for t in range(4):
                        pe.matmul(bank, v_cached[:, j, t, h * D:(h + 1) * D], weights_t[:, k % 2, t * P:(t + 1) * P],
                                  start=(t == 0), stop=False)
                    pe.matmul(bank, v_own[:, j, h * D:(h + 1) * D], weights_t[0:S, k % 2, 4 * P:5 * P],
                              start=False, stop=True).then_inc(pv_done, 1)

            with pe.Fori(0, LAST) as i:
                pair_of(i, False)
            pair_of(LAST, True)


def over_heads(nc, name, w_in, heads, result, tokens_first):
    with ExitStack() as opened:
        hold = opened.enter_context
        w_raw = hold(nc.sbuf_tensor(f"{name}_w_raw", [P, 2, G, HID], F32))
        w_hi = hold(nc.sbuf_tensor(f"{name}_w_hi", [P, 2, G, HID], F32R))
        w_lo = hold(nc.sbuf_tensor(f"{name}_w_lo", [P, 2, G, HID], F32R))
        h_raw = hold(nc.sbuf_tensor(f"{name}_h_raw", [P, 2, BS, GS], F32))
        h_hi = hold(nc.sbuf_tensor(f"{name}_h_hi", [P, 2, G, SPAN], F32R))
        h_lo = hold(nc.sbuf_tensor(f"{name}_h_lo", [P, 2, G, SPAN], F32R))
        ps = hold(nc.psum_tensor(f"{name}_ps", [P, 2, 4, 512], F32))
        w_loaded = [hold(nc.semaphore(f"{name}_w_loaded{k}")) for k in range(2)]
        h_loaded = [hold(nc.semaphore(f"{name}_h_loaded{k}")) for k in range(2)]
        w_hi_done = hold(nc.semaphore(f"{name}_w_hi_done"))
        w_lo_done = hold(nc.semaphore(f"{name}_w_lo_done"))
        h_hi_done = hold(nc.semaphore(f"{name}_h_hi_done"))
        h_lo_done = hold(nc.semaphore(f"{name}_h_lo_done"))
        unit_done = hold(nc.semaphore(f"{name}_unit_done"))
        bank_free = hold(nc.semaphore(f"{name}_bank_free"))
        block = hold(nc.Block())
        UN = 2 * NT
        LAST = HK // 2 - 1

        @block.sync
        def _(sp):
            def load_w(grp, slot):
                sp.dma_start(w_raw[:, slot, :, :],
                             w_in[bass.ds(grp, 1)].rearrange("o p (g n) -> p (o g) n", g=G)).then_inc(w_loaded[slot], 16)

            def load_h(grp, span, slot):
                sp.dma_start(h_raw[:, slot, :, :], heads[span * BS:(span + 1) * BS, :, bass.ds(grp, 1), :]
                             .rearrange("b p o n -> p b (o n)")).then_inc(h_loaded[slot], 16)

            load_w(0, 0)
            load_h(0, 0, 0)
            load_h(0, 1, 1)
            load_w(1, 1)

            def groups(i, last):
                for k in range(UN):
                    if k % NT == 1 and not last:
                        sp.wait_ge(w_lo_done, i * 2 + k // NT + 1)
                        load_w(i * 2 + k // NT + 2, k // NT)
                    if not (last and k >= UN - 2):
                        sp.wait_ge(h_lo_done, i * UN + k + 1)
                        load_h(i * 2 + (k + 2) // NT, (k + 2) % NT, k % 2)

            with sp.Fori(0, LAST) as i:
                groups(i, False)
            groups(LAST, True)

        @block.scalar
        def _(act):
            def split_w(slot, load):
                act.wait_ge(w_loaded[slot], load * 16 + 16)
                act.activation(w_hi[:, slot, :, :], w_raw[:, slot, :, :], ACT.Copy).then_inc(w_hi_done, 1)

            split_w(0, 0)

            def groups(i, last):
                for k in range(UN):
                    n = i * UN + k
                    act.wait_ge(h_loaded[k % 2], i * (UN * 8) + (k // 2) * 16 + 16)
                    if not isinstance(n, int) or n >= 2:
                        act.wait_ge(unit_done, n - 1)
                    act.activation(h_hi[:, k % 2, :, :].rearrange("p g (b s) -> p b g s", s=S),
                                   h_raw[:, k % 2, :, :].rearrange("p b (g s) -> p b g s", s=S), ACT.Copy).then_inc(h_hi_done, 1)
                    if k % NT == 2 and not (last and k > NT):
                        split_w(1 - k // NT, i + k // NT)

            groups(0, False)
            with act.Fori(1, LAST) as i:
                groups(i, False)
            groups(LAST, True)

        @block.vector
        def _(dve):
            dve.sem_inc(bank_free, 2)

            def split_w(grp, slot):
                dve.wait_ge(w_hi_done, grp + 1)
                dve.tensor_tensor(w_lo[:, slot, :, :], w_raw[:, slot, :, :], w_hi[:, slot, :, :].bitcast(F32),
                                  ALU.subtract).then_inc(w_lo_done, 1)

            def split_h(n, slot):
                dve.wait_ge(h_hi_done, n + 1)
                dve.tensor_tensor(h_lo[:, slot, :, :].rearrange("p g (b s) -> p b g s", s=S),
                                  h_raw[:, slot, :, :].rearrange("p b (g s) -> p b g s", s=S),
                                  h_hi[:, slot, :, :].bitcast(F32).rearrange("p g (b s) -> p b g s", s=S),
                                  ALU.subtract).then_inc(h_lo_done, 1)

            split_w(0, 0)
            split_h(0, 0)

            def groups(i, last):
                for k in range(UN):
                    n = i * UN + k
                    if not (last and k == UN - 1):
                        split_h(n + 1, (k + 1) % 2)
                    if k % NT == 2 and not (last and k > NT):
                        split_w(i * 2 + k // NT + 1, 1 - k // NT)
                    dve.wait_ge(unit_done, n + 1)
                    for j in range(4):
                        part = result(k % NT, j)
                        m = dve.tensor_tensor(part, part, ps[:, k % 2, j, :], ALU.add)
                    m.then_inc(bank_free, 1)

            with dve.Fori(0, LAST) as i:
                groups(i, False)
            groups(LAST, True)

        @block.tensor
        def _(pe):
            def groups(i):
                for k in range(UN):
                    n = i * UN + k
                    w, s = k // NT, k % 2
                    if k % NT == 0:
                        pe.wait_ge(w_lo_done, i * 2 + k // NT + 1)
                    pe.wait_ge(h_lo_done, n + 1)
                    pe.wait_ge(bank_free, n + 1)
                    for j in range(4):
                        cols = slice(j * P, (j + 1) * P)
                        for g in range(G):
                            if tokens_first:
                                m = split_product(pe, ps[:, s, j, :], h_hi[:, s, g, cols], h_lo[:, s, g, cols],
                                                  w_hi[:, w, g, :], w_lo[:, w, g, :], g == 0, g == G - 1)
                            else:
                                m = split_product(pe, ps[:, s, j, :], w_hi[:, w, g, cols], w_lo[:, w, g, cols],
                                                  h_hi[:, s, g, :], h_lo[:, s, g, :], g == 0, g == G - 1)
                    m.then_inc(unit_done, 1)

            with pe.Fori(0, HK // 2) as i:
                groups(i)


def load_x(nc, a, x2):
    with ExitStack() as opened:
        x_loaded = opened.enter_context(nc.semaphore("x2_loaded"))
        block = opened.enter_context(nc.Block())

        @block.sync
        def _(sp):
            sp.dma_start(x2[:, :, :], a["x"].rearrange("(t p) n -> p t n", p=P)).then_inc(x_loaded, 16)
            sp.wait_ge(x_loaded, 16)


def split_y(nc, y, y_hi, y_lo):
    with ExitStack() as opened:
        hold = opened.enter_context
        hi_done = hold(nc.semaphore("y_hi_done"))
        block = hold(nc.Block())

        @block.scalar
        def _(act):
            for j in range(KC):
                act.activation(y_hi[:, j, :], y[:, j, :], ACT.Copy).then_inc(hi_done, 1)

        @block.vector
        def _(dve):
            for j in range(KC):
                dve.wait_ge(hi_done, j + 1)
                dve.tensor_tensor(y_lo[:, j, :], y[:, j, :], y_hi[:, j, :].bitcast(F32), ALU.subtract)


def clear(nc, y):
    with ExitStack() as opened:
        block = opened.enter_context(nc.Block())

        @block.vector
        def _(dve):
            dve.memset(y[:, :, :], 0.0)


def stage4(nc, c, a, scratch, y_hi, y_lo):
    with ExitStack() as opened:
        hold = opened.enter_context
        WC = 6 * D
        w_raw = hold(nc.sbuf_tensor("s4_w_raw", [P, KC, WC], F32))
        w_hi = hold(nc.sbuf_tensor("s4_w_hi", [P, 2, KC, WC], F32R))
        w_lo = hold(nc.sbuf_tensor("s4_w_lo", [P, 2, KC, WC], F32R))
        q_t = hold(nc.sbuf_tensor("s4_q_t", [P, 2, BS, G, S], F32))
        k_t = hold(nc.sbuf_tensor("s4_k_t", [P, 2, SPAN], F32))
        v_r = hold(nc.sbuf_tensor("s4_v_r", [P, 2, 4, D], F32))
        scores = hold(nc.sbuf_tensor("s4_scores", [P, BS, S], F32))
        probs = hold(nc.sbuf_tensor("s4_probs", [P, BS, S], F32))
        weights = hold(nc.sbuf_tensor("s4_weights", [P, BS * S], F32))
        weights_t = hold(nc.sbuf_tensor("s4_weights_t", [P, 4, GS], F32))
        o_t = hold(nc.sbuf_tensor("s4_o_t", [P, 2, BS, GS], F32))
        top = hold(nc.sbuf_tensor("s4_top", [P, BS], F32))
        total = hold(nc.sbuf_tensor("s4_total", [P, BS], F32))
        inv = hold(nc.sbuf_tensor("s4_inv", [P, BS], F32))
        ps_proj = hold(nc.psum_tensor("s4_ps_proj", [P, 2, 512], F32))
        ps_scores = hold(nc.psum_tensor("s4_ps_scores", [P, BS, S], F32))
        ps_turn = hold(nc.psum_tensor("s4_ps_turn", [P, 4, GS], F32))
        ps_o = hold(nc.psum_tensor("s4_ps_o", [P, SEQ, 4, GS], F32))
        w_loaded = hold(nc.semaphore("s4_w_loaded"))
        w_hi_done = hold(nc.semaphore("s4_w_hi_done"))
        w_lo_done = hold(nc.semaphore("s4_w_lo_done"))
        proj_done = hold(nc.semaphore("s4_proj_done"))
        proj_free = hold(nc.semaphore("s4_proj_free"))
        scores_done = hold(nc.semaphore("s4_scores_done"))
        soft_step = hold(nc.semaphore("s4_soft_step"))
        exp_done = hold(nc.semaphore("s4_exp_done"))
        turn_done = hold(nc.semaphore("s4_turn_done"))
        pv_done = hold(nc.semaphore("s4_pv_done"))
        o_free = hold(nc.semaphore("s4_o_free"))
        store_free = [hold(nc.semaphore(f"s4_store{k}_free")) for k in range(2)]
        block = hold(nc.Block())
        UN = 2 * NT
        PJ = 6
        STEPS = 7
        LAST = HK // 2 - 1

        @block.sync
        def _(sp):
            for k in range(2):
                sp.sem_inc(store_free[k], 16)
            sp.dma_start(w_raw[:, :, :].rearrange("p k n -> p (k n)"), a["w2"][0]).then_inc(w_loaded, 16)

            def groups(i, last):
                for k in range(UN):
                    n = i * UN + k
                    if k % NT == 0 and not (last and k > 0):
                        sp.wait_ge(w_lo_done, i * 2 + k // NT + 1)
                        sp.dma_start(w_raw[:, :, :].rearrange("p k n -> p (k n)"),
                                     a["w2"][bass.ds(i * 2 + k // NT + 1, 1)].rearrange("o p n -> p (o n)")).then_inc(w_loaded, 16)
                    sp.wait_ge(o_free, n + 2)
                    dst = scratch["aT"][k % NT * BS:(k % NT + 1) * BS, :, bass.ds(i * 2 + k // NT, 1), :]
                    sp.dma_start(dst.rearrange("b p o n -> p b (o n)"), o_t[:, k % 2, :, :]).then_inc(store_free[k % 2], 16)

            with sp.Fori(0, LAST) as i:
                groups(i, False)
            groups(LAST, True)
            for k in range(2):
                sp.wait_ge(store_free[k], 16 + 16 * HK * NT // 2)

        @block.scalar
        def _(act):
            act.sem_inc(o_free, 1)
            act.sem_inc(proj_free, 2)

            def split_w(grp, slot):
                act.wait_ge(w_loaded, grp * 16 + 16)
                act.activation(w_hi[:, slot, :, :], w_raw[:, :, :], ACT.Copy).then_inc(w_hi_done, 1)

            def copies(n, k):
                for r in range(PJ):
                    act.wait_ge(proj_done, n * PJ + r + 1)
                    src = ps_proj[:, r % 2, :]
                    if r < G:
                        m = act.activation(q_t[:, k % 2, :, r, :], src.rearrange("p (b s) -> p b s", s=S), ACT.Copy)
                    elif r == G:
                        m = act.activation(k_t[:, k % 2, :], src, ACT.Copy)
                    else:
                        m = act.activation(v_r[:, k % 2, :, :], src.rearrange("p (j d) -> p j d", d=D), ACT.Copy)
                    m.then_inc(proj_free, 1)

            split_w(0, 0)
            copies(0, 0)

            def groups(i, last):
                for k in range(UN):
                    n = i * UN + k
                    act.wait_ge(soft_step, n * STEPS + 3)
                    act.activation(probs[:, :, :], scores[:, :, :], ACT.Exp, scale=SCALE).then_inc(exp_done, 1)
                    if k % NT == 1 and not (last and k > NT):
                        split_w(i * 2 + k // NT + 1, 1 - k // NT)
                    if not (last and k == UN - 1):
                        copies(n + 1, k + 1)
                    act.wait_ge(pv_done, n + 1)
                    act.wait_ge(store_free[k % 2], i * (UN * 8) + (k // 2) * 16 + 16)
                    for q in range(SEQ):
                        m = act.activation(o_t[:, k % 2, q:BS:SEQ, :], ps_o[:, q, :, :], ACT.Copy)
                    m.then_inc(o_free, 1)

            with act.Fori(0, LAST) as i:
                groups(i, False)
            groups(LAST, True)

        @block.vector
        def _(dve):
            def split_w(grp, slot):
                dve.wait_ge(w_hi_done, grp + 1)
                dve.tensor_tensor(w_lo[:, slot, :, :], w_raw[:, :, :], w_hi[:, slot, :, :].bitcast(F32),
                                  ALU.subtract).then_inc(w_lo_done, 1)

            split_w(0, 0)

            def over_keys(col):
                return col.rearrange("p (b o) -> p b o", o=1).to_broadcast([P, BS, S])

            def groups(i, last):
                for k in range(UN):
                    n = i * UN + k
                    base = n * STEPS
                    causal = c["causal"][:, :].rearrange("p (o s) -> p o s", o=1).to_broadcast([P, BS, S])
                    dve.wait_ge(scores_done, n + 1)
                    dve.tensor_tensor(scores[:, :, :], ps_scores[:, :, :], causal, ALU.add).then_inc(soft_step, 1)
                    dve.wait_ge(soft_step, base + 1)
                    dve.tensor_reduce(top[:, :], scores[:, :, :], AX.X, ALU.max).then_inc(soft_step, 1)
                    dve.wait_ge(soft_step, base + 2)
                    dve.tensor_tensor(scores[:, :, :], scores[:, :, :], over_keys(top[:, :]), ALU.subtract).then_inc(soft_step, 1)
                    dve.wait_ge(exp_done, n + 1)
                    dve.tensor_reduce(total[:, :], probs[:, :, :], AX.X, ALU.add).then_inc(soft_step, 1)
                    dve.wait_ge(soft_step, base + 4)
                    dve.reciprocal(inv[:, :], total[:, :]).then_inc(soft_step, 1)
                    dve.wait_ge(soft_step, base + 5)
                    dve.tensor_tensor(weights[:, :].rearrange("p (b s) -> p b s", s=S), probs[:, :, :], over_keys(inv[:, :]),
                                      ALU.mult).then_inc(soft_step, 1)
                    if k % NT == 1 and not (last and k > NT):
                        split_w(i * 2 + k // NT + 1, 1 - k // NT)
                    dve.wait_ge(turn_done, n + 1)
                    dve.tensor_copy(weights_t[:, :, :], ps_turn[:, :, :]).then_inc(soft_step, 1)

            with dve.Fori(0, LAST) as i:
                groups(i, False)
            groups(LAST, True)

        @block.tensor
        def _(pe):
            def project(n, k, grp):
                w, span = (k // NT) % 2, k % NT
                if span == 0:
                    pe.wait_ge(w_lo_done, grp + 1)
                for r in range(PJ):
                    pe.wait_ge(proj_free, n * PJ + r + 1)
                    if r < PJ - 1:
                        for q in range(KC):
                            cols = slice(r * D, (r + 1) * D)
                            toks = slice(span * SPAN, (span + 1) * SPAN)
                            m = split_product(pe, ps_proj[:, r % 2, :], w_hi[:, w, q, cols], w_lo[:, w, q, cols],
                                              y_hi[:, q, toks], y_lo[:, q, toks], q == 0, q == KC - 1)
                    else:
                        for j in range(4):
                            toks = slice(span * SPAN + j * P, span * SPAN + (j + 1) * P)
                            cols = slice(r * D, (r + 1) * D)
                            for q in range(KC):
                                m = split_product(pe, ps_proj[:, r % 2, j * D:(j + 1) * D], y_hi[:, q, toks], y_lo[:, q, toks],
                                                  w_hi[:, w, q, cols], w_lo[:, w, q, cols], q == 0, q == KC - 1)
                    m.then_inc(proj_done, 1)

            project(0, 0, 0)

            def groups(i, last):
                for k in range(UN):
                    n = i * UN + k
                    s = k % 2
                    pe.wait_ge(proj_free, n * PJ + PJ + 2)
                    for b in range(BS):
                        m = pe.matmul(ps_scores[:, b, :], q_t[:, s, b, :, :].rearrange("p g s -> p (g s)"),
                                      k_t[:, s, b * S:(b + 1) * S], start=True, stop=True)
                    m.then_inc(scores_done, 1)
                    if not (last and k == UN - 1):
                        project(n + 1, k + 1, i * 2 + (k + 1) // NT)
                    pe.wait_ge(soft_step, n * STEPS + 6)
                    for j in range(4):
                        m = pe.transpose(ps_turn[:, j, :], weights[:, j * P:(j + 1) * P], c["ident"][:, :])
                    m.then_inc(turn_done, 1)
                    pe.wait_ge(soft_step, n * STEPS + 7)
                    pe.wait_ge(o_free, n + 1)
                    for j in range(4):
                        for q in range(SEQ):
                            rows = slice(q * S, (q + 1) * S)
                            m = pe.matmul(ps_o[:, q, j, :], v_r[rows, s, j, :], weights_t[rows, j, :], start=True, stop=True)
                    m.then_inc(pv_done, 1)

            with pe.Fori(0, LAST) as i:
                groups(i, False)
            groups(LAST, True)


def stage6(nc, c, a, x2, out):
    with ExitStack() as opened:
        hold = opened.enter_context
        mix = hold(nc.sbuf_tensor("s6_mix", [P, TILES, S], F32))
        mix_bd = hold(nc.sbuf_tensor("s6_mix_bd", [P, TILES, P], F32))
        y_t = hold(nc.sbuf_tensor("s6_y_t", [P, TILES, KC * P], F32))
        wb = hold(nc.sbuf_tensor("s6_wb", [P, KC, HID], F32))
        wga = hold(nc.sbuf_tensor("s6_wga", [P, KC, E + ER], F32))
        lb = hold(nc.sbuf_tensor("s6_lb", [P, HID], F32))
        bias = hold(nc.sbuf_tensor("s6_bias", [P, HID], F32))
        gate_h = hold(nc.sbuf_tensor("s6_gate_h", [P, TILES, E + ER], F32))
        pick = [hold(nc.sbuf_tensor(f"s6_pick{k}", [P, TILES, E], F32)) for k in range(4)]
        best = [hold(nc.sbuf_tensor(f"s6_best{k}", [P, TILES], F32)) for k in range(4)]
        order = hold(nc.sbuf_tensor("s6_order", [P, E], F32))
        order_i = hold(nc.sbuf_tensor("s6_order_i", [P, E], I32))
        hw = hold(nc.sbuf_tensor("s6_hw", [P, TILES, ER], F32))
        hw_t = hold(nc.sbuf_tensor("s6_hw_t", [P, 2, P], F32))
        done = hold(nc.sbuf_tensor("s6_done", [P, 2, HID], F32))
        ps_y = hold(nc.psum_tensor("s6_ps_y", [P, 2, 512], F32))
        ps_g = hold(nc.psum_tensor("s6_ps_g", [P, 2, 512], F32))
        ps_t = hold(nc.psum_tensor("s6_ps_t", [P, 2, 512], F32))
        ps_out = hold(nc.psum_tensor("s6_ps_out", [P, 2, 512], F32))
        loaded = hold(nc.semaphore("s6_loaded"))
        mix_loaded = hold(nc.semaphore("s6_mix_loaded"))
        order_set = hold(nc.semaphore("s6_order_set"))
        step_done = hold(nc.semaphore("s6_step"))
        mix_done = hold(nc.semaphore("s6_mix_done"))
        y_done = hold(nc.semaphore("s6_y_done"))
        y_copied = hold(nc.semaphore("s6_y_copied"))
        g_done = hold(nc.semaphore("s6_g_done"))
        g_copied = hold(nc.semaphore("s6_g_copied"))
        exp_in = hold(nc.semaphore("s6_exp_in"))
        exp_out = hold(nc.semaphore("s6_exp_out"))
        hw_done = hold(nc.semaphore("s6_hw_done"))
        t_done = hold(nc.semaphore("s6_t_done"))
        t_copied = hold(nc.semaphore("s6_t_copied"))
        out_done = hold(nc.semaphore("s6_out_done"))
        added = hold(nc.semaphore("s6_added"))
        stored = [hold(nc.semaphore(f"s6_stored{k}")) for k in range(2)]
        block = hold(nc.Block())

        @block.sync
        def _(sp):
            sp.dma_start(wga[:, :, :].rearrange("p k n -> p (k n)"), a["wga"]).then_inc(loaded, 16)
            sp.dma_start(wb[:, :, :].rearrange("p k n -> p (k n)"), a["wb"]).then_inc(loaded, 16)
            sp.dma_start(lb[:, :], a["lb"]).then_inc(loaded, 16)
            sp.dma_start(bias[:, :], a["bias"].to_broadcast([P, HID])).then_inc(loaded, 16)
            for t in range(TILES):
                sp.wait_ge(added, t + 1)
                sp.dma_start(out[t * P:(t + 1) * P, :], done[:, t % 2, :]).then_inc(stored[t % 2], 16)
            for k in range(2):
                sp.wait_ge(stored[k], 16 * TILES // 2)

        @block.gpsimd
        def _(pool):
            for t in range(TILES):
                pool.indirect_dma_start(out=mix[:, t, :], out_offset=None, in_=a["mix"],
                                        in_offset=bass.IndirectOffsetOnAxis(ap=c["subj"][:, t:t + 1], axis=0)
                                        ).then_inc(mix_loaded, 16)
            pool.iota(order_i[:, :], pattern=[[-1, E]], base=E, channel_multiplier=0).then_inc(order_set, 1)

        @block.scalar
        def _(act):
            for t in range(TILES):
                act.wait_ge(y_done, t + 1)
                act.activation(y_t[:, t, :], ps_y[:, t % 2, :], ACT.Copy).then_inc(y_copied, 1)
            act.wait_ge(exp_in, 1)
            act.activation(best[2][:, :], best[2][:, :], ACT.Exp).then_inc(exp_out, 1)
            for t in range(TILES):
                act.wait_ge(t_done, t + 1)
                act.activation(hw_t[:, t % 2, :], ps_t[:, t % 2, 0:P], ACT.Copy).then_inc(t_copied, 1)

        @block.vector
        def _(dve):
            steps = [0]

            def step(m):
                steps[0] += 1
                m.then_inc(step_done, 1)
                dve.wait_ge(step_done, steps[0])

            dve.wait_ge(mix_loaded, 16 * TILES)
            for s in range(SEQ):
                m = dve.tensor_tensor(mix_bd[:, :, s * S:(s + 1) * S], mix[:, :, :],
                                      c["own_seq"][:, s:s + 1].rearrange("p (o q) -> p o q", o=1).to_broadcast([P, TILES, S]), ALU.mult)
            m.then_inc(mix_done, 1)
            for t in range(TILES):
                dve.wait_ge(g_done, t + 1)
                dve.tensor_copy(gate_h[:, t, :], ps_g[:, t % 2, 0:E + ER]).then_inc(g_copied, 1)
            dve.wait_ge(g_copied, TILES)
            dve.wait_ge(order_set, 1)
            logits = gate_h[:, :, 0:E]

            def wide(col):
                return col[:, :].rearrange("p (t o) -> p t o", o=1).to_broadcast([P, TILES, E])

            step(dve.tensor_copy(order[:, :], order_i[:, :]))
            rank = order[:, :].rearrange("p (o e) -> p o e", o=1).to_broadcast([P, TILES, E])
            for k in range(2):
                src = logits if k == 0 else pick[3][:, :, :]
                step(dve.tensor_reduce(best[k][:, :], src, AX.X, ALU.max))
                step(dve.tensor_tensor(pick[k][:, :, :], src, wide(best[k]), ALU.is_equal))
                step(dve.tensor_tensor(pick[k][:, :, :], pick[k][:, :, :], rank, ALU.mult))
                step(dve.tensor_reduce(best[3][:, :], pick[k][:, :, :], AX.X, ALU.max))
                step(dve.tensor_tensor(pick[k][:, :, :], rank, wide(best[3]), ALU.is_equal))
                if k == 0:
                    step(dve.scalar_tensor_tensor(out=pick[3][:, :, :], in0=pick[0][:, :, :], scalar=OUT_OF_REACH, in1=logits,
                                                  op0=ALU.mult, op1=ALU.add))
            step(dve.tensor_tensor(best[2][:, :], best[1][:, :], best[0][:, :], ALU.subtract))
            dve.sem_inc(exp_in)
            dve.wait_ge(exp_out, 1)
            step(dve.tensor_scalar(best[0][:, :], best[2][:, :], 1.0, None, ALU.add))
            step(dve.reciprocal(best[0][:, :], best[0][:, :]))
            step(dve.tensor_tensor(best[1][:, :], best[0][:, :], best[2][:, :], ALU.mult))
            step(dve.tensor_tensor(pick[0][:, :, :], pick[0][:, :, :], wide(best[0]), ALU.mult))
            step(dve.tensor_tensor(pick[1][:, :, :], pick[1][:, :, :], wide(best[1]), ALU.mult))
            step(dve.tensor_tensor(pick[2][:, :, :], pick[0][:, :, :], pick[1][:, :, :], ALU.add))
            step(dve.tensor_tensor(hw[:, :, :].rearrange("p t (e r) -> p (t e) r", r=R),
                                   gate_h[:, :, E:].rearrange("p t (e r) -> p t e r", r=R),
                                   pick[2][:, :, :].rearrange("p t (e o) -> p t e o", o=1).to_broadcast([P, TILES, E, R]), ALU.mult))
            dve.sem_inc(hw_done)
            dve.wait_ge(loaded, 64)
            for t in range(TILES):
                step(dve.tensor_tensor(x2[:, t, :], x2[:, t, :], bias[:, :], ALU.add))
                dve.wait_ge(out_done, t + 1)
                if t >= 2:
                    dve.wait_ge(stored[t % 2], 16 * (t // 2))
                dve.tensor_tensor(done[:, t % 2, :], x2[:, t, :], ps_out[:, t % 2, :], ALU.add).then_inc(added, 1)

        @block.tensor
        def _(pe):
            pe.wait_ge(mix_done, 1)
            pe.wait_ge(loaded, 64)

            def gate(t):
                pe.wait_ge(y_copied, t + 1)
                if t >= 2:
                    pe.wait_ge(g_copied, t - 1)
                for k in range(KC):
                    m = pe.matmul(ps_g[:, t % 2, 0:E + ER], y_t[:, t, k * P:(k + 1) * P], wga[:, k, :], start=(k == 0), stop=(k == KC - 1))
                m.then_inc(g_done, 1)

            for t in range(TILES):
                if t >= 2:
                    pe.wait_ge(y_copied, t - 1)
                for k in range(KC):
                    m = pe.matmul(ps_y[:, t % 2, k * P:(k + 1) * P], x2[:, t, k * P:(k + 1) * P], mix_bd[:, t, :], start=True, stop=True)
                m.then_inc(y_done, 1)
                if t > 0:
                    gate(t - 1)
            gate(TILES - 1)

            for t in range(TILES):
                if t >= 2:
                    pe.wait_ge(added, t - 1)
                for k in range(KC):
                    pe.matmul(ps_out[:, t % 2, :], y_t[:, t, k * P:(k + 1) * P], wb[:, k, :], start=(k == 0), stop=False)
                if t == 0:
                    pe.wait_ge(hw_done, 1)
                pe.transpose(ps_t[:, t % 2, 0:P], hw[:, t, :], c["ident"][:, :]).then_inc(t_done, 1)
                pe.wait_ge(t_copied, t + 1)
                pe.matmul(ps_out[:, t % 2, :], hw_t[:, t % 2, :], lb[:, :], start=False, stop=True).then_inc(out_done, 1)


def build(nc, a, out, scratch):
    with ExitStack() as opened:
        hold = opened.enter_context
        ident = hold(nc.sbuf_tensor("ident", [P, P], F32))
        tok_i = hold(nc.sbuf_tensor("tok_i", [P, 1], I32))
        tok_f = hold(nc.sbuf_tensor("tok_f", [P, 1], F32))
        key_i = hold(nc.sbuf_tensor("key_i", [P, L], I32))
        key_f = hold(nc.sbuf_tensor("key_f", [P, L], F32))
        vrow = hold(nc.sbuf_tensor("vrow", [P, B * 4], I32))
        subj = hold(nc.sbuf_tensor("subj", [P, TILES], I32))
        len_all = hold(nc.sbuf_tensor("len_all", [P, B], I32))
        len_f = hold(nc.sbuf_tensor("len_f", [P, B], F32))
        table = hold(nc.sbuf_tensor("table", [1, B * NPP], I32))
        causal = hold(nc.sbuf_tensor("causal", [P, S], F32))
        own_seq = hold(nc.sbuf_tensor("own_seq", [P, SEQ], F32))
        c = dict(ident=ident, tok_i=tok_i, tok_f=tok_f, key_i=key_i, key_f=key_f, vrow=vrow, subj=subj,
                 len_all=len_all, len_f=len_f, table=table, causal=causal, own_seq=own_seq)
        stage1(nc, c, a, scratch)
        stage2(nc, c, a, scratch)
        with ExitStack() as parts:
            y_hi = parts.enter_context(nc.sbuf_tensor("y_hi", [P, KC, TOK], F32R))
            y_lo = parts.enter_context(nc.sbuf_tensor("y_lo", [P, KC, TOK], F32R))
            with nc.sbuf_tensor("y", [P, KC, TOK], F32) as y:
                clear(nc, y)
                over_heads(nc, "s3", a["wo"], scratch["oT"],
                           lambda span, j: y[:, j, span * SPAN:(span + 1) * SPAN], tokens_first=False)
                split_y(nc, y, y_hi, y_lo)
            stage4(nc, c, a, scratch, y_hi, y_lo)
        with nc.sbuf_tensor("x2", [P, TILES, HID], F32) as x2:
            load_x(nc, a, x2)
            over_heads(nc, "s5", a["wd"], scratch["aT"], lambda span, j: x2[:, span * 4 + j, :], tokens_first=True)
            stage6(nc, c, a, x2, out)


def kernel(x, itok_Bx16_0_63, itok_B_207_1644, itok_B_0_30, L0_cond_Wq, L0_cond_Wk, L0_cond_Wv, L0_cond_Wo,
           L0_cond_q_norm_w, L0_cond_k_norm_w, L0_cond_k_cache, L0_cond_v_cache, L0_attn_w_qkv, L0_attn_w_dense,
           L0_cond2_weights, L0_ffn_W_base, L0_ffn_b_base, L0_ffn_W_gate, L0_ffn_A, L0_ffn_B):
    import concourse.bacc as bacc
    from concourse.bass_utils import run_bass_kernel_spmd

    def laid(v):
        return np.ascontiguousarray(np.asarray(v))

    x = np.asarray(x).reshape(TOK, HID)
    w1 = np.concatenate([np.asarray(L0_cond_Wq), np.asarray(L0_cond_Wk), np.asarray(L0_cond_Wv)], 0)
    wqkv = np.asarray(L0_attn_w_qkv)
    w2 = np.concatenate([wqkv[:HQ * D].reshape(HK, G * D, HID), wqkv[HQ * D:(HQ + HK) * D].reshape(HK, D, HID),
                         wqkv[(HQ + HK) * D:].reshape(HK, D, HID)], 1)
    arrays = {
        "x": laid(x),
        "xT": laid(x.T),
        "w1": laid(w1.reshape(12, 512, KC, P).transpose(0, 3, 2, 1).reshape(12, P, KC * 512)),
        "freq": (np.float32(1.0) / np.float32(THETA) ** (np.arange(0, D, 2, dtype=np.float32) / np.float32(D))).astype(np.float32).reshape(1, HALF),
        "qw": laid(L0_cond_q_norm_w).reshape(1, D),
        "kw": laid(L0_cond_k_norm_w).reshape(1, D),
        "table": laid(itok_Bx16_0_63).reshape(1, B * NPP),
        "table_t": laid(np.asarray(itok_Bx16_0_63).reshape(B, 4, 4).transpose(2, 0, 1)).reshape(4, B * 4),
        "lens": laid(itok_B_207_1644).reshape(1, B),
        "lens_t": laid(np.asarray(itok_B_207_1644).reshape(TILES, SEQ).T),
        "subj_t": laid(np.asarray(itok_B_0_30).reshape(TILES, SEQ).T),
        "kpool": laid(np.asarray(L0_cond_k_cache).transpose(3, 0, 2, 1)).reshape(D, PAGES * HK * PSIZE),
        "vpool": laid(L0_cond_v_cache).reshape(PAGES * PSIZE, HK * D),
        "wo": laid(np.asarray(L0_cond_Wo).reshape(HID, HK, G, D).transpose(1, 3, 2, 0)).reshape(HK, D, G * HID),
        "w2": laid(w2.reshape(HK, 6 * D, KC, P).transpose(0, 3, 2, 1)).reshape(HK, P, KC * 6 * D),
        "wd": laid(np.asarray(L0_attn_w_dense).reshape(HID, HK, G, D).transpose(1, 3, 2, 0)).reshape(HK, D, G * HID),
        "mix": laid(L0_cond2_weights).reshape(S * S, S),
        "wb": laid(np.asarray(L0_ffn_W_base).reshape(HID, KC, P).transpose(2, 1, 0)).reshape(P, KC * HID),
        "wga": laid(np.concatenate([np.asarray(L0_ffn_W_gate), np.asarray(L0_ffn_A).reshape(ER, HID)], 0)
                    .reshape(E + ER, KC, P).transpose(2, 1, 0)).reshape(P, KC * (E + ER)),
        "lb": laid(np.asarray(L0_ffn_B).transpose(0, 2, 1)).reshape(ER, HID),
        "bias": laid(L0_ffn_b_base).reshape(1, HID),
    }
    nc = bacc.Bacc("TRN2", target_bir_lowering=False, num_devices=1)
    a = {k: nc.dram_tensor(k + "_in", v.shape, mybir.dt.from_np(v.dtype), kind="ExternalInput").ap() for k, v in arrays.items()}
    out = nc.dram_tensor("out", (TOK, HID), F32, kind="ExternalOutput").ap()
    scratch = {
        "qT": nc.dram_tensor("qT_scratch", (B, D, HK, GS), F32).ap(),
        "kT": nc.dram_tensor("kT_scratch", (B, D, 2, GS), F32).ap(),
        "v": nc.dram_tensor("v_scratch", (TOK, HK * D), F32).ap(),
        "oT": nc.dram_tensor("oT_scratch", (B, D, HK, GS), F32).ap(),
        "aT": nc.dram_tensor("aT_scratch", (B, D, HK, GS), F32).ap(),
    }
    build(nc, a, out, scratch)
    r = run_bass_kernel_spmd(nc, [{k + "_in": v for k, v in arrays.items()}], core_ids=[0])
    return r.results[0]["out"].reshape(B, S, HID)
```

```python
import math
from contextlib import ExitStack

import numpy as np

import concourse.bass as bass
from concourse import mybir

F32 = mybir.dt.float32
F32R = mybir.dt.float32r
BF16 = mybir.dt.bfloat16
I32 = mybir.dt.int32
ACT = mybir.ActivationFunctionType
ALU = mybir.AluOpType
AX = mybir.AxisListType

B, S, HID = 64, 32, 512
TOK = B * S
P = 128
D, HQ, HK = 128, 32, 8
G = HQ // HK
PAGES, PSIZE, NPP = 64, 32, 16
L = PSIZE * NPP
KC = HID // P
TILES = TOK // P
SEQ = P // S
NT = 4
SPAN = TOK // NT
BS = B // NT
E, R = 8, 16
ER = E * R
THETA = 10000.0
EPS = 1e-6
SCALE = 1.0 / math.sqrt(D)
OUT_OF_REACH = -1e30
HALF = D // 2
GS = G * S


def split_product(pe, out, a_hi, a_lo, b_hi, b_lo, start, stop):
    pe.matmul(out, a_hi, b_hi, start=start, stop=False)
    pe.matmul(out, a_hi, b_lo, start=False, stop=False)
    return pe.matmul(out, a_lo, b_hi, start=False, stop=stop)


def stage1(nc, c, a, scratch):
    CB = 12
    UN = TILES // 2
    with ExitStack() as opened:
        hold = opened.enter_context
        x_raw = hold(nc.sbuf_tensor("x_raw", [P, 2, TOK], F32))
        x_hi = hold(nc.sbuf_tensor("x_hi", [P, KC, TOK], F32R))
        x_lo = hold(nc.sbuf_tensor("x_lo", [P, KC, TOK], F32R))
        w_raw = hold(nc.sbuf_tensor("w_raw", [P, 2, KC * 512], F32))
        w_hi = hold(nc.sbuf_tensor("w_hi", [P, 2, KC * 512], F32R))
        w_lo = hold(nc.sbuf_tensor("w_lo", [P, 2, KC * 512], F32R))
        tab_q = hold(nc.sbuf_tensor("tab_q", [P, 2, TILES, D], F32))
        tab_k = hold(nc.sbuf_tensor("tab_k", [P, 2, TILES, D], F32))
        squares = hold(nc.sbuf_tensor("squares", [P, 2, 1024], BF16))
        unit_rows = hold(nc.sbuf_tensor("unit_rows", [P, 1024], F32))
        turning = hold(nc.sbuf_tensor("turning", [P, 2, 1024], F32))
        by_cos = hold(nc.sbuf_tensor("by_cos", [P, 1024], F32))
        by_sin = hold(nc.sbuf_tensor("by_sin", [P, 1024], F32))
        turned = hold(nc.sbuf_tensor("turned", [P, 2, 1024], F32))
        sumsq = hold(nc.sbuf_tensor("sumsq", [P, 2, 8], F32))
        root = hold(nc.sbuf_tensor("root", [P, 2, 8], F32))
        nw = hold(nc.sbuf_tensor("nw", [P, 4, 8], F32))
        eps = hold(nc.sbuf_tensor("eps", [P, 1], F32))
        key_i = turned[:, 1, 0:L].bitcast(I32)
        ps_proj = hold(nc.psum_tensor("ps_proj", [P, 2, 2, 512], F32))
        ps_turn = hold(nc.psum_tensor("ps_turn", [P, 2, 2, 512], F32))
        x_loaded0 = hold(nc.semaphore("x_loaded0"))
        x_loaded1 = hold(nc.semaphore("x_loaded1"))
        x_hi_done = hold(nc.semaphore("x_hi_done"))
        x_lo_done = hold(nc.semaphore("x_lo_done"))
        w_loaded0 = hold(nc.semaphore("w_loaded0"))
        w_loaded1 = hold(nc.semaphore("w_loaded1"))
        w_hi_done = hold(nc.semaphore("w_hi_done"))
        w_lo_done = hold(nc.semaphore("w_lo_done"))
        proj_done = hold(nc.semaphore("proj_done"))
        proj_free = hold(nc.semaphore("proj_free"))
        root_done = hold(nc.semaphore("root_done"))
        dve_step = hold(nc.semaphore("dve_step"))
        halves_done = hold(nc.semaphore("halves_done"))
        rotated = hold(nc.semaphore("rotated"))
        turn_done = hold(nc.semaphore("turn_done"))
        turned_done = hold(nc.semaphore("turned_done"))
        store0_free = hold(nc.semaphore("store0_free"))
        store1_free = hold(nc.semaphore("store1_free"))
        v_copied = hold(nc.semaphore("v_copied"))
        eps_set = hold(nc.semaphore("eps_set"))
        const_loaded = hold(nc.semaphore("const_loaded"))
        pos_ready = hold(nc.semaphore("pos_ready"))
        sines = hold(nc.semaphore("sines"))
        ident_step = hold(nc.semaphore("ident_step"))
        own_set = hold(nc.semaphore("own_set"))
        block = hold(nc.Block())
        x_loaded = [x_loaded0, x_loaded1]
        w_loaded = [w_loaded0, w_loaded1]
        store_free = [store0_free, store1_free]
        angle = turning[:, 0, :].rearrange("p (t f) -> p t f", f=HALF)
        turns = turning[:, 1, :].rearrange("p (t f) -> p t f", f=HALF)
        sin_t = by_cos[:, :].rearrange("p (t f) -> p t f", f=HALF)
        cos_t = by_sin[:, :].rearrange("p (t f) -> p t f", f=HALF)
        freq = turned[:, 0, 0:HALF]
        wq_row = turned[:, 0, 128:256]
        wk_row = turned[:, 0, 256:384]
        len_i = turned[:, 0, 512:512 + TILES].bitcast(I32)
        pos_f = turned[:, 0, 640:640 + TILES]

        @block.sync
        def _(sp):
            sp.sem_inc(store_free[0], 16)
            sp.sem_inc(store_free[1], 16)
            for k in range(2):
                sp.dma_start(x_raw[:, k, :], a["xT"][k * P:(k + 1) * P, :]).then_inc(x_loaded[k], 16)
            for k in range(2):
                sp.dma_start(w_raw[:, k, :], a["w1"][k]).then_inc(w_loaded[k], 16)
            sp.dma_start(freq, a["freq"].to_broadcast([P, HALF])).then_inc(const_loaded, 16)
            sp.dma_start(wq_row, a["qw"].to_broadcast([P, D])).then_inc(const_loaded, 16)
            sp.dma_start(wk_row, a["kw"].to_broadcast([P, D])).then_inc(const_loaded, 16)
            for s in range(SEQ):
                r = slice(s * S, (s + 1) * S)
                sp.dma_start(len_i[r, :], a["lens_t"][s:s + 1, :].to_broadcast([S, TILES])).then_inc(const_loaded, 16)
                sp.dma_start(c["subj"][r, :], a["subj_t"][s:s + 1, :].to_broadcast([S, TILES])).then_inc(const_loaded, 16)
                sp.dma_start(c["vrow"][r, :], a["table_t"][s:s + 1, :].to_broadcast([S, B * 4])).then_inc(const_loaded, 16)
            sp.dma_start(c["len_all"][:, :], a["lens"].to_broadcast([P, B])).then_inc(const_loaded, 16)
            sp.dma_start(c["table"][0:1, :], a["table"]).then_inc(const_loaded, 16)
            for k in range(2, KC):
                sp.wait_ge(x_lo_done, k - 1)
                sp.dma_start(x_raw[:, k % 2, :], a["xT"][k * P:(k + 1) * P, :]).then_inc(x_loaded[k % 2], 16)

            def block_of(i, cb, kind):
                if kind != "v":
                    sp.wait_ge(w_lo_done, i * 2 + cb + 1)
                    sp.dma_start(w_raw[:, cb, :],
                                 a["w1"][bass.ds(i * 2 + cb + 2, 1)].rearrange("o p n -> p (o n)")).then_inc(w_loaded[cb], 16)
                for u in range(UN):
                    n = i * 2 * UN + cb * UN + u
                    b0 = u * 2 * SEQ
                    if kind == "q":
                        dst = scratch["qT"][b0:b0 + 2 * SEQ, :, bass.ds(i * 2 + cb, 1), :].rearrange("b p o n -> p b (o n)")
                    elif kind == "k":
                        dst = scratch["kT"][b0:b0 + 2 * SEQ, :, cb, :].rearrange("b p n -> p b n")
                    else:
                        dst = scratch["v"][u * 2 * P:(u + 1) * 2 * P, cb * 512:(cb + 1) * 512].rearrange("(t p) n -> p t n", p=P)
                    if kind == "v":
                        sp.wait_ge(v_copied, cb * UN + u + 1)
                        src = turned[:, u % 2, :].rearrange("p (t n) -> p t n", t=2)
                    else:
                        sp.wait_ge(turned_done, n + 3)
                        src = turned[:, u % 2, :].rearrange("p (b n) -> p b n", n=GS)
                    sp.dma_start(dst, src).then_inc(store_free[u % 2], 16)

            with sp.Fori(0, 4) as i:
                for cb in range(2):
                    block_of(i, cb, "q")
            for cb in range(2):
                block_of(4, cb, "k")
            for cb in range(2):
                block_of(5, cb, "v")
            for k in range(2):
                sp.wait_ge(store_free[k], 16 + 16 * CB * UN // 2)
            sp.wait_ge(const_loaded, 16 * (5 + 3 * SEQ))

        @block.gpsimd
        def _(pool):
            pool.sem_inc(rotated, 1)
            pool.memset(c["ident"][:, :], 0.0).then_inc(ident_step, 1)
            for s in range(SEQ):
                pool.wait_ge(ident_step, s + 1)
                pool.iota(c["tok_i"][s * S:(s + 1) * S, :], pattern=[[0, 1]], base=0, channel_multiplier=1).then_inc(ident_step, 1)
            pool.wait_ge(ident_step, SEQ + 1)
            pool.iota(key_i[:, :], pattern=[[1, L]], base=0, channel_multiplier=0).then_inc(ident_step, 1)
            pool.wait_ge(ident_step, SEQ + 2)
            pool.affine_select(out=c["ident"][:, :], in_=c["ident"][:, :], compare_op=ALU.not_equal, fill=1.0,
                               base=0, pattern=[[-1, P]], channel_multiplier=1).then_inc(ident_step, 1)
            with pool.Fori(0, 10) as cb:
                for u in range(UN):
                    pool.wait_ge(halves_done, cb * UN + u + 1)
                    pool.wait_ge(turn_done, cb * UN + u + 1)
                    pool.tensor_tensor(turning[:, u % 2, :], by_cos[:, :], by_sin[:, :], ALU.add).then_inc(rotated, 1)

        @block.scalar
        def _(act):
            for k in range(KC):
                act.wait_ge(x_loaded[k % 2], 16 * (k // 2 + 1))
                act.activation(x_hi[:, k, :], x_raw[:, k % 2, :], ACT.Copy).then_inc(x_hi_done, 1)
                if k == 0:
                    act.wait_ge(w_loaded[0], 16)
                    act.activation(w_hi[:, 0, :], w_raw[:, 0, :], ACT.Copy).then_inc(w_hi_done, 1)
            act.wait_ge(pos_ready, 1)
            act.activation(sin_t, angle, ACT.Sin).then_inc(sines, 1)
            act.activation(cos_t, angle, ACT.Sin, scale=0.5).then_inc(sines, 1)
            act.wait_ge(eps_set, 1)

            def roots(n, u):
                act.wait_ge(proj_done, n + 1)
                for t in range(2):
                    for g in range(G):
                        h = t * G + g
                        m = act.activation(squares[:, u % 2, h * D:(h + 1) * D], ps_proj[:, u % 2, t, g * D:(g + 1) * D], ACT.Square,
                                           accum_out=sumsq[:, u % 2, h:h + 1])
                m.then_inc(root_done, 1)
                act.wait_ge(root_done, n * 2 + 1)
                act.activation(root[:, u % 2, :], sumsq[:, u % 2, :], ACT.Sqrt, bias=eps[:, 0:1], scale=1.0 / D).then_inc(root_done, 1)

            def turn_copy(n, half, u):
                act.wait_ge(turn_done, n + 3)
                act.wait_ge(store_free[u % 2], half * 16 + 16)
                for t in range(2):
                    src = ps_turn[:, u % 2, t, :].rearrange("p (g b s) -> p g b s", g=G, b=SEQ)
                    dst = turned[:, u % 2, t * 512:(t + 1) * 512].rearrange("p (b g s) -> p g b s", g=G, b=SEQ)
                    m = act.activation(dst, src, ACT.Copy)
                m.then_inc(turned_done, 1)

            def split(slot, load, q):
                part = slice(q * 512, (q + 1) * 512)
                if q == 0:
                    act.wait_ge(w_loaded[slot], load * 16 + 16)
                act.activation(w_hi[:, slot, part], w_raw[:, slot, part], ACT.Copy).then_inc(w_hi_done, 1)

            def block_of(i, cb, kind):
                for u in range(UN):
                    n = i * 2 * UN + cb * UN + u
                    if kind == "v":
                        act.wait_ge(proj_done, n + 1)
                        act.wait_ge(store_free[u % 2], (i * UN + cb * (UN // 2) + u // 2) * 16 + 16)
                        for t in range(2):
                            m = act.activation(turned[:, u % 2, t * 512:(t + 1) * 512], ps_proj[:, u % 2, t, :], ACT.Copy)
                        m.then_inc(v_copied, 1)
                    else:
                        if not (kind == "k" and cb == 1 and u >= UN - 2):
                            roots(n + 2, u)
                        turn_copy(n, i * UN + cb * (UN // 2) + u // 2, u)
                    if u < KC and not (kind == "v" and cb == 1):
                        split((cb + 1) % 2, i + cb, u)

            act.sem_inc(turned_done, 2)
            roots(0, 0)
            roots(1, 1)
            with act.Fori(0, 4) as i:
                for cb in range(2):
                    block_of(i, cb, "q")
            for cb in range(2):
                block_of(4, cb, "k")
            for cb in range(2):
                block_of(5, cb, "v")

        @block.vector
        def _(dve):
            steps = [0]

            def step(m):
                steps[0] += 1
                m.then_inc(dve_step, 1)
                dve.wait_ge(dve_step, steps[0])

            dve.sem_inc(proj_free, 2)
            dve.memset(eps[:, :], EPS).then_inc(eps_set, 1)
            for k in range(KC):
                dve.wait_ge(x_hi_done, k + 1)
                dve.tensor_tensor(x_lo[:, k, :], x_raw[:, k % 2, :], x_hi[:, k, :].bitcast(F32), ALU.subtract).then_inc(x_lo_done, 1)
                if k == 0:
                    dve.wait_ge(w_hi_done, 1)
                    dve.tensor_tensor(w_lo[:, 0, :], w_raw[:, 0, :], w_hi[:, 0, :].bitcast(F32), ALU.subtract).then_inc(w_lo_done, 1)
            dve.wait_ge(const_loaded, 16 * (5 + 3 * SEQ))
            dve.wait_ge(ident_step, SEQ + 3)
            step(dve.tensor_copy(c["tok_f"][:, :], c["tok_i"][:, :]))
            step(dve.tensor_copy(c["key_f"][:, :], key_i[:, :]))
            step(dve.tensor_copy(c["ident_r"][:, :], c["ident"][:, :]))
            step(dve.tensor_scalar(c["vrow"][:, :], c["vrow"][:, :], float(PSIZE), c["tok_f"][:, 0:1], ALU.mult, ALU.add))
            step(dve.tensor_scalar(c["subj"][:, :], c["subj"][:, :], float(S), c["tok_f"][:, 0:1], ALU.mult, ALU.add))
            step(dve.tensor_copy(c["len_f"][:, :], c["len_all"][:, :]))
            step(dve.tensor_scalar(c["causal"][:, :], c["key_f"][:, 0:S], c["tok_f"][:, 0:1], OUT_OF_REACH, ALU.is_gt, ALU.mult))
            dve.memset(c["own_seq"][:, :], 0.0).then_inc(own_set, 1)
            dve.wait_ge(own_set, 1)
            for s in range(SEQ):
                dve.memset(c["own_seq"][s * S:(s + 1) * S, s:s + 1], 1.0).then_inc(own_set, 1)
            step(dve.tensor_copy(pos_f, len_i))
            step(dve.tensor_scalar(pos_f, pos_f, c["tok_f"][:, 0:1], None, ALU.add))
            step(dve.tensor_tensor(angle, pos_f.rearrange("p (t o) -> p t o", o=1).to_broadcast([P, TILES, HALF]),
                                   freq.rearrange("p (o f) -> p o f", o=1).to_broadcast([P, TILES, HALF]), ALU.mult))
            magic = 1.5 * 2.0 ** 23
            step(dve.tensor_scalar(turns, angle, 1.0 / (2 * math.pi), magic, ALU.mult, ALU.add))
            step(dve.tensor_scalar(turns, turns, magic, None, ALU.subtract))
            c1 = 6.28125
            c2 = math.floor((2 * math.pi - c1) * 2 ** 22) / 2 ** 22
            c3 = 2 * math.pi - c1 - c2
            for part in (c1, c2, c3):
                step(dve.scalar_tensor_tensor(out=angle, in0=turns, scalar=-part, in1=angle, op0=ALU.mult, op1=ALU.add))
            edge = math.pi * (1 - 1e-7)
            dve.tensor_scalar(angle, angle, edge, -edge, ALU.min, ALU.max).then_inc(pos_ready, 1)
            dve.wait_ge(sines, 2)
            step(dve.tensor_tensor(cos_t, cos_t, cos_t, ALU.mult))
            step(dve.tensor_scalar(cos_t, cos_t, -2.0, 1.0, ALU.mult, ALU.add))
            for tab, row in ((tab_q, wq_row), (tab_k, wk_row)):
                for half in range(2):
                    cols = slice(half * HALF, (half + 1) * HALF)
                    other = slice((1 - half) * HALF, (2 - half) * HALF)

                    def w(part):
                        return row[:, part].rearrange("p (o f) -> p o f", o=1).to_broadcast([P, TILES, HALF])
                    step(dve.tensor_tensor(tab[:, 0, :, cols], cos_t, w(cols), ALU.mult))
                    step(dve.tensor_tensor(tab[:, 1, :, cols], sin_t, w(other), ALU.mult))
                step(dve.tensor_scalar(tab[:, 1, :, 0:HALF], tab[:, 1, :, 0:HALF], -1.0, None, ALU.mult))
            before = steps[0]

            def unit(i, cb, u, tab):
                n = i * 2 * UN + cb * UN + u
                m = n * 6 + before
                ss, rt = sumsq[:, u % 2, :], root[:, u % 2, :]
                dve.wait_ge(root_done, n * 2 + 2)
                dve.tensor_scalar(nw[:, 0, :], ss, 1.0 / D, EPS, ALU.mult, ALU.add).then_inc(dve_step, 1)
                dve.reciprocal(nw[:, 1, :], rt).then_inc(dve_step, 1)
                dve.wait_ge(dve_step, m + 2)
                dve.tensor_tensor(nw[:, 2, :], nw[:, 1, :], nw[:, 1, :], ALU.mult).then_inc(dve_step, 1)
                dve.wait_ge(dve_step, m + 3)
                dve.tensor_tensor(nw[:, 2, :], nw[:, 2, :], nw[:, 0, :], ALU.mult).then_inc(dve_step, 1)
                dve.wait_ge(dve_step, m + 4)
                dve.tensor_scalar(nw[:, 2, :], nw[:, 2, :], -0.5, 1.5, ALU.mult, ALU.add).then_inc(dve_step, 1)
                dve.wait_ge(dve_step, m + 5)
                dve.tensor_tensor(nw[:, 3, :], nw[:, 2, :], nw[:, 1, :], ALU.mult).then_inc(dve_step, 1)
                dve.wait_ge(dve_step, m + 6)
                dve.tensor_tensor(unit_rows[:, :].rearrange("p (h d) -> p h d", d=D),
                                  ps_proj[:, u % 2, :, :].rearrange("p t (g d) -> p (t g) d", d=D),
                                  nw[:, 3, :].rearrange("p (h o) -> p h o", o=1).to_broadcast([P, 8, D]),
                                  ALU.mult).then_inc(proj_free, 1)
                dve.wait_ge(proj_free, n + 3)
                dve.wait_ge(rotated, n + 1)
                for t in range(2):
                    q3 = unit_rows[:, t * 512:(t + 1) * 512].rearrange("p (g d) -> p g d", d=D)
                    cos3 = tab[:, 0, 2 * u + t, :].rearrange("p (o d) -> p o d", o=1).to_broadcast([P, G, D])
                    dve.tensor_tensor(by_cos[:, t * 512:(t + 1) * 512].rearrange("p (g d) -> p g d", d=D), q3, cos3, ALU.mult)
                    for half in range(2):
                        cols = slice(half * HALF, (half + 1) * HALF)
                        other = slice((1 - half) * HALF, (2 - half) * HALF)
                        sin3 = tab[:, 1, 2 * u + t, cols].rearrange("p (o d) -> p o d", o=1).to_broadcast([P, G, HALF])
                        k = dve.tensor_tensor(by_sin[:, t * 512:(t + 1) * 512].rearrange("p (g d) -> p g d", d=D)[:, :, cols],
                                              q3[:, :, other], sin3, ALU.mult)
                k.then_inc(halves_done, 1)

            def split(cb, slot, q):
                part = slice(q * 512, (q + 1) * 512)
                dve.wait_ge(w_hi_done, (cb - 1) * KC + q + 2)
                m = dve.tensor_tensor(w_lo[:, slot, part], w_raw[:, slot, part], w_hi[:, slot, part].bitcast(F32), ALU.subtract)
                if q == KC - 1:
                    m.then_inc(w_lo_done, 1)

            with dve.Fori(0, 4) as i:
                for cb in range(2):
                    for u in range(UN):
                        unit(i, cb, u, tab_q)
                        if 1 <= u <= KC:
                            split(i * 2 + cb + 1, (cb + 1) % 2, u - 1)
            for cb in range(2):
                for u in range(UN):
                    unit(4, cb, u, tab_k)
                    if 1 <= u <= KC:
                        split(9 + cb, (cb + 1) % 2, u - 1)
            for q in range(KC):
                split(11, 1, q)

        @block.tensor
        def _(pe):
            def project(n, blk, slot, u):
                if u == 0:
                    pe.wait_ge(w_lo_done, blk + 1)
                if isinstance(n, int) and n >= 82:
                    pe.wait_ge(v_copied, n - 81)
                else:
                    pe.wait_ge(proj_free, n + 1)
                for t in range(2):
                    cols = slice((2 * u + t) * P, (2 * u + t + 1) * P)
                    for k in range(KC):
                        w = slice(k * 512, (k + 1) * 512)
                        m = split_product(pe, ps_proj[:, u % 2, t, :], x_hi[:, k, cols], x_lo[:, k, cols],
                                          w_hi[:, slot, w], w_lo[:, slot, w], k == 0, k == KC - 1)
                m.then_inc(proj_done, 1)

            def turn(n, u):
                pe.wait_ge(rotated, n + 2)
                pe.wait_ge(turned_done, n + 1)
                for t in range(2):
                    for g in range(G):
                        j = t * G + g
                        m = pe.transpose(ps_turn[:, u % 2, t, g * P:(g + 1) * P], turning[:, u % 2, j * P:(j + 1) * P], c["ident"][:, :])
                m.then_inc(turn_done, 1)

            def block_of(i, cb, kind):
                for u in range(UN):
                    n = i * 2 * UN + cb * UN + u
                    blk = i * 2 + cb
                    if u < UN - 2:
                        project(n + 2, blk, cb, u + 2)
                    elif not (kind == "v" and cb == 1):
                        project(n + 2, blk + 1, 1 - cb, u + 2 - UN)
                    if kind != "v":
                        turn(n, u)

            pe.sem_inc(turn_done, 2)
            pe.wait_ge(x_lo_done, KC)
            pe.wait_ge(ident_step, SEQ + 3)
            project(0, 0, 0, 0)
            project(1, 0, 0, 1)
            with pe.Fori(0, 4) as i:
                for cb in range(2):
                    block_of(i, cb, "q")
            for cb in range(2):
                block_of(4, cb, "k")
            for cb in range(2):
                block_of(5, cb, "v")


def stage2(nc, c, a, scratch):
    with ExitStack() as opened:
        hold = opened.enter_context
        N2 = 2 * HK
        Q = 4
        DVE_PAGES = 6
        LAST = B // 2 - 1
        k_pool = hold(nc.sbuf_tensor("k_pool", [P, PAGES, HK * PSIZE], F32))
        k_cached = hold(nc.sbuf_tensor("k_cached", [P, 2, NPP, HK * PSIZE], F32))
        v_cached = hold(nc.sbuf_tensor("v_cached", [P, 2, 4, HK * D], F32))
        k_own = hold(nc.sbuf_tensor("k_own", [P, 2, HK * S], F32))
        v_own = hold(nc.sbuf_tensor("v_own", [P, 2, HK, D], F32))
        q_t = hold(nc.sbuf_tensor("q_t", [P, 2, HK, GS], F32))
        reach = hold(nc.sbuf_tensor("reach", [P, 2, L], BF16))
        masked = hold(nc.sbuf_tensor("masked", [P, 2 * Q, L + S], F32))
        probs = hold(nc.sbuf_tensor("probs", [P, 2, L + S], F32))
        w_hi = hold(nc.sbuf_tensor("w_hi2", [P, L + S, Q], F32R))
        w_lo = hold(nc.sbuf_tensor("w_lo2", [P, L + S, Q], F32R))
        weights_t = hold(nc.sbuf_tensor("weights_t", [P, 2, L], F32))
        own_t = hold(nc.sbuf_tensor("own_t", [P, 2, GS], F32))
        o_t = hold(nc.sbuf_tensor("o_t", [P, 2, Q * GS], F32))
        own_top = hold(nc.sbuf_tensor("own_top", [P, 2, Q], F32))
        top = hold(nc.sbuf_tensor("top", [P, 4], F32))
        shift = hold(nc.sbuf_tensor("shift", [P, 4], F32))
        total = hold(nc.sbuf_tensor("total", [P, 4], F32))
        inv = hold(nc.sbuf_tensor("inv", [P, 4], F32))
        rows_now = hold(nc.sbuf_tensor("rows_now", [P, 2, 4], I32))
        ps_scores = hold(nc.psum_tensor("ps_scores", [P, 4, 512], F32))
        ps_own = hold(nc.psum_tensor("ps_own", [P, 512], F32))
        ps_turn2 = hold(nc.psum_tensor("ps_turn2", [P, 512], F32))
        ps_o = hold(nc.psum_tensor("ps_o", [P, 2, 512], F32))
        pool_loaded = hold(nc.semaphore("pool_loaded"))
        own_loaded = [hold(nc.semaphore(f"own_loaded{k}")) for k in range(2)]
        v_loaded = [hold(nc.semaphore(f"v_loaded{k}")) for k in range(2)]
        k_by_dve = hold(nc.semaphore("k_by_dve"))
        k_by_pool = hold(nc.semaphore("k_by_pool"))
        rows_ready = hold(nc.semaphore("rows_ready"))
        v_own_zero = hold(nc.semaphore("v_own_zero"))
        scores_done = hold(nc.semaphore("scores_done"))
        own_scored = hold(nc.semaphore("own_scored"))
        own_read = hold(nc.semaphore("own_read"))
        top_done = hold(nc.semaphore("top_done"))
        shift_done = hold(nc.semaphore("shift_done"))
        exp_done = hold(nc.semaphore("exp_done"))
        inv_done = hold(nc.semaphore("inv_done"))
        w_hi_done = hold(nc.semaphore("w_hi2_done"))
        w_lo_done = hold(nc.semaphore("w_lo2_done"))
        turns_done = hold(nc.semaphore("turns_done"))
        own_turned = hold(nc.semaphore("own_turned"))
        wt_done = hold(nc.semaphore("wt_done"))
        own_t_done = hold(nc.semaphore("own_t_done"))
        pv_done = hold(nc.semaphore("pv_done"))
        group_done = hold(nc.semaphore("group_done"))
        o_bank_free = hold(nc.semaphore("o_bank_free"))
        o_store_free = [hold(nc.semaphore(f"o_store{k}_free")) for k in range(2)]
        reach_done = hold(nc.semaphore("reach_done"))
        dve_passed = hold(nc.semaphore("dve_passed"))
        pool_passed = hold(nc.semaphore("pool_passed"))
        block = hold(nc.Block())

        def pages_of(engine, b, first, count):
            return nc.values_load_multi_w_load_instructions(
                c["table"][0:1, bass.ds(b * NPP + first, count)], engines=(engine,), min_val=0, max_val=PAGES - 1,
                skip_runtime_bounds_check_because="the reference's indices lie in the pool")[1]

        @block.sync
        def _(sp):
            def load_own(b, slot):
                sp.dma_start(q_t[:, slot, :, :], scratch["qT"][bass.ds(b, 1)].rearrange("o p h n -> p (o h) n")).then_inc(own_loaded[slot], 16)
                sp.dma_start(k_own[:, slot, :], scratch["kT"][bass.ds(b, 1)].rearrange("o p h n -> p (o h n)")).then_inc(own_loaded[slot], 16)
                for q in range(Q):
                    sp.dma_start(v_own[q:P:Q, slot, q:HK:Q, :],
                                 scratch["v"][bass.ds(b * S, S), :].rearrange("s (g q d) -> s g q d", q=Q, d=D)[:, :, q, :]
                                 ).then_inc(own_loaded[slot], 16)

            for k in range(2):
                sp.sem_inc(o_store_free[k], 16)
            for k in range(4):
                pages = slice(k * PAGES // 4, (k + 1) * PAGES // 4)
                cols = slice(k * PAGES // 4 * HK * PSIZE, (k + 1) * PAGES // 4 * HK * PSIZE)
                sp.dma_start(k_pool[:, pages, :].rearrange("p a n -> p (a n)"), a["kpool"][:, cols]).then_inc(pool_loaded, 16)
            sp.wait_ge(v_own_zero, 1)
            load_own(0, 0)

            def pair_of(i, last):
                for j in range(2):
                    b = i * 2 + j
                    if not (last and j == 1):
                        sp.wait_ge(pv_done, b * HK + 1)
                        load_own(b + 1, 1 - j)
                    for g in range(2):
                        sp.wait_ge(o_bank_free, b * 2 + g + 3)
                        dst = scratch["oT"][bass.ds(b, 1), :, g * Q:(g + 1) * Q, :]
                        sp.dma_start(dst.rearrange("o p h n -> p (o h n)"), o_t[:, g, :]).then_inc(o_store_free[g], 16)

            with sp.Fori(0, LAST) as i:
                pair_of(i, False)
            pair_of(LAST, True)
            for k in range(2):
                sp.wait_ge(o_store_free[k], 16 + 16 * B)

        @block.gpsimd
        def _(pool):
            def gather_v(b, slot):
                pool.tensor_copy(rows_now[:, slot, :], c["vrow"][:, bass.ds(b * 4, 4)]).then_inc(rows_ready, 1)
                pool.wait_ge(rows_ready, b + 1)
                pool.sem_inc(pool_passed)
                for k in range(4):
                    pool.indirect_dma_start(out=v_cached[:, slot, k, :], out_offset=None, in_=a["vpool"],
                                            in_offset=bass.IndirectOffsetOnAxis(ap=rows_now[:, slot, k:k + 1], axis=0)
                                            ).then_inc(v_loaded[slot], 16)

            def gather_k(b, slot):
                page = pages_of(mybir.EngineType.Pool, b, DVE_PAGES, NPP - DVE_PAGES)
                for k in range(NPP - DVE_PAGES):
                    m = pool.tensor_copy(k_cached[:, slot, DVE_PAGES + k, :], k_pool[:, bass.ds(page[k], 1), :].rearrange("p o n -> p (o n)"))
                m.then_inc(k_by_pool, 1)

            gather_v(0, 0)
            pool.wait_ge(pool_loaded, 64)
            gather_k(0, 0)
            gather_k(1, 1)

            def pair_of(i, last):
                for j in range(2):
                    b = i * 2 + j
                    if not (last and j == 1):
                        pool.wait_ge(pv_done, b * HK + 1)
                        pool.sem_inc(pool_passed)
                        gather_v(b + 1, 1 - j)
                    if not last:
                        pool.wait_ge(scores_done, b * HK + HK)
                        pool.sem_inc(pool_passed)
                        gather_k(b + 2, j)

            with pool.Fori(0, LAST) as i:
                pair_of(i, False)
            pair_of(LAST, True)

        @block.scalar
        def _(act):
            act.sem_inc(o_bank_free, 2)

            def exps(n, k):
                act.wait_ge(shift_done, n + 1)
                act.activation(probs[:, k % 2, :], masked[:, k % 8, :], ACT.Exp, bias=shift[:, k % 4:k % 4 + 1], scale=SCALE,
                               accum_out=total[:, k % 4:k % 4 + 1]).then_inc(exp_done, 1)

            def high(n, k):
                act.wait_ge(inv_done, n + 1)
                act.activation(w_hi[:, :, k % Q], probs[:, k % 2, :], ACT.Copy,
                               scale=inv[:, k % 4:k % 4 + 1]).then_inc(w_hi_done, 1)

            exps(0, 0)
            high(0, 0)
            exps(1, 1)

            def pair_of(i, last):
                for k in range(N2):
                    n = i * N2 + k
                    if k % Q == Q - 1:
                        act.wait_ge(own_turned, i * Q + k // Q + 1)
                    if not (last and k >= N2 - 1):
                        high(n + 1, k + 1)
                    act.wait_ge(turns_done, n + 1)
                    act.activation(weights_t[:, k % 2, :], ps_turn2[:, :], ACT.Copy).then_inc(wt_done, 1)
                    if k % Q == Q - 1:
                        act.activation(own_t[:, k // Q % 2, :], ps_own[:, Q * S:Q * S + GS], ACT.Copy).then_inc(own_t_done, 1)
                    if not (last and k >= N2 - 2):
                        exps(n + 2, k + 2)
                    if k % Q == Q - 1:
                        g = k // Q
                        act.wait_ge(group_done, i * Q + g + 1)
                        act.wait_ge(o_store_free[g % 2], i * 32 + (g // 2) * 16 + 16)
                        act.activation(o_t[:, g % 2, :], ps_o[:, g % 2, :], ACT.Copy).then_inc(o_bank_free, 1)

            with act.Fori(0, LAST) as i:
                pair_of(i, False)
            pair_of(LAST, True)

        @block.vector
        def _(dve):
            def reach_of(b, slot):
                dve.tensor_scalar(reach[:, slot, :], c["key_f"][:, :], c["len_f"][:, bass.ds(b, 1)], OUT_OF_REACH,
                                  ALU.is_ge, ALU.mult).then_inc(reach_done, 1)

            def own_part(grp, slot):
                dve.wait_ge(own_scored, grp + 1)
                src = ps_own[:, 0:Q * S].rearrange("p (h s) -> p h s", s=S)
                dve.tensor_copy(masked[:, slot * Q:(slot + 1) * Q, L:L + S], src)
                dve.tensor_reduce(own_top[:, slot, :], src, AX.X, ALU.max).then_inc(own_read, 1)

            def maximum(n, k, b):
                dve.wait_ge(scores_done, n + 1)
                dve.wait_ge(reach_done, b + 1)
                dve.sem_inc(dve_passed)
                dve.tensor_tensor_reduce(masked[:, k % 8, 0:L], ps_scores[:, k % 4, :], reach[:, (k // HK) % 2, :], 1.0,
                                         -3.0e38, ALU.add, ALU.max, top[:, k % 4:k % 4 + 1]).then_inc(top_done, 1)
                dve.wait_ge(top_done, n + 1)
                if k % Q == 0:
                    dve.wait_ge(own_read, b * 2 + (k // Q) % 2 + 1)
                dve.tensor_scalar(shift[:, k % 4:k % 4 + 1], top[:, k % 4:k % 4 + 1],
                                  own_top[:, (k // Q) % 2, k % Q:k % Q + 1], -SCALE, ALU.max, ALU.mult).then_inc(shift_done, 1)

            def inverse(n, k):
                dve.wait_ge(exp_done, n + 1)
                dve.reciprocal(inv[:, k % 4:k % 4 + 1], total[:, k % 4:k % 4 + 1]).then_inc(inv_done, 1)

            def low(n, k):
                dve.wait_ge(w_hi_done, n + 1)
                dve.scalar_tensor_tensor(out=w_lo[:, :, k % Q], in0=probs[:, k % 2, :],
                                         scalar=inv[:, k % 4:k % 4 + 1], in1=w_hi[:, :, k % Q].bitcast(F32),
                                         op0=ALU.mult, op1=ALU.subtract).then_inc(w_lo_done, 1)

            def gather_k(b, slot, first, count):
                page = pages_of(mybir.EngineType.DVE, b, first, count)
                for k in range(count):
                    m = dve.tensor_copy(k_cached[:, slot, first + k, :], k_pool[:, bass.ds(page[k], 1), :].rearrange("p o n -> p (o n)"))
                if first + count == DVE_PAGES:
                    m.then_inc(k_by_dve, 1)

            dve.memset(v_own[:, :, :, :], 0.0).then_inc(v_own_zero, 1)
            reach_of(0, 0)
            dve.wait_ge(pool_loaded, 64)
            gather_k(0, 0, 0, DVE_PAGES)
            gather_k(1, 1, 0, DVE_PAGES)
            own_part(0, 0)
            maximum(0, 0, 0)
            inverse(0, 0)
            maximum(1, 1, 0)
            low(0, 0)
            inverse(1, 1)
            maximum(2, 2, 0)

            def pair_of(i, last):
                for k in range(N2):
                    n = i * N2 + k
                    if k % HK == 2 and not (last and k > HK):
                        reach_of(i * 2 + k // HK + 1, 1 - k // HK)
                    if not (last and k >= N2 - 1):
                        low(n + 1, k + 1)
                    if not (last and k >= N2 - 3):
                        if (k + 3) % Q == 0:
                            own_part(i * Q + (k + 3) // Q, (k + 3) // Q % 2)
                        maximum(n + 3, k + 3, i * 2 + (k + 3) // HK)
                    if not (last and k >= N2 - 2):
                        inverse(n + 2, k + 2)
                    if k % HK >= 5 and not last:
                        gather_k(i * 2 + k // HK + 2, k // HK, (k % HK - 5) * 2, 2)

            with dve.Fori(0, LAST) as i:
                pair_of(i, False)
            pair_of(LAST, True)

        @block.tensor
        def _(pe):
            def scores(n, k, b, grp):
                h, j = k % HK, (k // HK) % 2
                if h == 0:
                    pe.wait_ge(own_loaded[j], (b - j) * 48 + 96)
                    pe.wait_ge(k_by_dve, b + 1)
                    pe.wait_ge(k_by_pool, b + 1)
                if not isinstance(n, int) or n >= 4:
                    pe.wait_ge(top_done, n - 3)
                pe.matmul(ps_scores[:, k % 4, :], q_t[:, j, h, :], k_cached[:, j, :, h * PSIZE:(h + 1) * PSIZE],
                          start=True, stop=True).then_inc(scores_done, 1)
                if h % Q == 0:
                    if not isinstance(grp, int) or grp >= 2:
                        pe.wait_ge(own_t_done, grp - 1)
                    for q in range(Q):
                        m = pe.matmul(ps_own[:, q * S:(q + 1) * S], q_t[:, j, h + q, :], k_own[:, j, (h + q) * S:(h + q + 1) * S],
                                      start=True, stop=True)
                    m.then_inc(own_scored, 1)

            def turn(out, hi, lo):
                pe.matmul(out, hi, c["ident_r"][:, :], start=True, stop=False)
                return pe.matmul(out, lo, c["ident_r"][:, :], start=False, stop=True)

            for k in range(3):
                scores(k, k, 0, 0)

            def pair_of(i, last):
                for k in range(N2):
                    n = i * N2 + k
                    h, j, g = k % HK, k // HK, k // Q
                    pe.wait_ge(w_lo_done, n + 1)
                    if k % Q == Q - 1:
                        turn(ps_own[:, Q * S:Q * S + GS], w_hi[:, L:L + S, :].rearrange("p s q -> p (s q)"),
                             w_lo[:, L:L + S, :].rearrange("p s q -> p (s q)")).then_inc(own_turned, 1)
                    for t in range(4):
                        m = turn(ps_turn2[:, t * P:(t + 1) * P], w_hi[:, t * P:(t + 1) * P, k % Q], w_lo[:, t * P:(t + 1) * P, k % Q])
                    m.then_inc(turns_done, 1)
                    if not (last and k >= N2 - 3):
                        scores(n + 3, k + 3, i * 2 + (k + 3) // HK, i * Q + (k + 3) // Q)
                    if h == 0:
                        pe.wait_ge(v_loaded[j], i * 64 + 64)
                    if k % Q == 0:
                        pe.wait_ge(o_bank_free, i * Q + g + 1)
                    pe.wait_ge(wt_done, n + 1)
                    bank = ps_o[:, g % 2, :]
                    for t in range(4):
                        m = pe.matmul(bank[:, (k % Q) * GS:(k % Q + 1) * GS], v_cached[:, j, t, h * D:(h + 1) * D],
                                      weights_t[:, k % 2, t * P:(t + 1) * P], start=(k % Q == 0 and t == 0), stop=False,
                                      skip_group_check=True)
                    m.then_inc(pv_done, 1)
                    if k % Q == Q - 1:
                        pe.wait_ge(own_t_done, i * Q + g + 1)
                        for q in range(Q):
                            m = pe.matmul(bank[:, q * GS:(q + 1) * GS], v_own[:, j, h - Q + 1 + q, :], own_t[:, g % 2, :],
                                          start=False, stop=True, skip_group_check=True)
                        m.then_inc(group_done, 1)

            with pe.Fori(0, LAST) as i:
                pair_of(i, False)
            pair_of(LAST, True)


def over_heads(nc, name, w_in, heads, result, tokens_first):
    with ExitStack() as opened:
        hold = opened.enter_context
        w_raw = hold(nc.sbuf_tensor(f"{name}_w_raw", [P, 2, G, HID], F32))
        w_hi = hold(nc.sbuf_tensor(f"{name}_w_hi", [P, 2, G, HID], F32R))
        w_lo = hold(nc.sbuf_tensor(f"{name}_w_lo", [P, 2, G, HID], F32R))
        h_raw = hold(nc.sbuf_tensor(f"{name}_h_raw", [P, 2, BS, GS], F32))
        h_hi = hold(nc.sbuf_tensor(f"{name}_h_hi", [P, 2, G, SPAN], F32R))
        h_lo = hold(nc.sbuf_tensor(f"{name}_h_lo", [P, 2, G, SPAN], F32R))
        ps = hold(nc.psum_tensor(f"{name}_ps", [P, 2, 4, 512], F32))
        w_loaded = [hold(nc.semaphore(f"{name}_w_loaded{k}")) for k in range(2)]
        h_loaded = [hold(nc.semaphore(f"{name}_h_loaded{k}")) for k in range(2)]
        w_hi_done = hold(nc.semaphore(f"{name}_w_hi_done"))
        w_lo_done = hold(nc.semaphore(f"{name}_w_lo_done"))
        h_hi_done = hold(nc.semaphore(f"{name}_h_hi_done"))
        h_lo_done = hold(nc.semaphore(f"{name}_h_lo_done"))
        unit_done = hold(nc.semaphore(f"{name}_unit_done"))
        bank_free = hold(nc.semaphore(f"{name}_bank_free"))
        block = hold(nc.Block())
        UN = 2 * NT
        LAST = HK // 2 - 1

        @block.sync
        def _(sp):
            def load_w(grp, slot):
                sp.dma_start(w_raw[:, slot, :, :],
                             w_in[bass.ds(grp, 1)].rearrange("o p (g n) -> p (o g) n", g=G)).then_inc(w_loaded[slot], 16)

            def load_h(grp, span, slot):
                sp.dma_start(h_raw[:, slot, :, :], heads[span * BS:(span + 1) * BS, :, bass.ds(grp, 1), :]
                             .rearrange("b p o n -> p b (o n)")).then_inc(h_loaded[slot], 16)

            load_w(0, 0)
            load_h(0, 0, 0)
            load_h(0, 1, 1)
            load_w(1, 1)

            def groups(i, last):
                for k in range(UN):
                    if k % NT == 1 and not last:
                        sp.wait_ge(w_lo_done, i * 2 + k // NT + 1)
                        load_w(i * 2 + k // NT + 2, k // NT)
                    if not (last and k >= UN - 2):
                        sp.wait_ge(h_lo_done, i * UN + k + 1)
                        load_h(i * 2 + (k + 2) // NT, (k + 2) % NT, k % 2)

            with sp.Fori(0, LAST) as i:
                groups(i, False)
            groups(LAST, True)

        @block.scalar
        def _(act):
            def split_w(slot, load):
                act.wait_ge(w_loaded[slot], load * 16 + 16)
                act.activation(w_hi[:, slot, :, :], w_raw[:, slot, :, :], ACT.Copy).then_inc(w_hi_done, 1)

            split_w(0, 0)

            def groups(i, last):
                for k in range(UN):
                    n = i * UN + k
                    act.wait_ge(h_loaded[k % 2], i * (UN * 8) + (k // 2) * 16 + 16)
                    if not isinstance(n, int) or n >= 2:
                        act.wait_ge(unit_done, n - 1)
                    act.activation(h_hi[:, k % 2, :, :].rearrange("p g (b s) -> p b g s", s=S),
                                   h_raw[:, k % 2, :, :].rearrange("p b (g s) -> p b g s", s=S), ACT.Copy).then_inc(h_hi_done, 1)
                    if k % NT == 2 and not (last and k > NT):
                        split_w(1 - k // NT, i + k // NT)

            groups(0, False)
            with act.Fori(1, LAST) as i:
                groups(i, False)
            groups(LAST, True)

        @block.vector
        def _(dve):
            dve.sem_inc(bank_free, 2)

            def split_w(grp, slot):
                dve.wait_ge(w_hi_done, grp + 1)
                dve.tensor_tensor(w_lo[:, slot, :, :], w_raw[:, slot, :, :], w_hi[:, slot, :, :].bitcast(F32),
                                  ALU.subtract).then_inc(w_lo_done, 1)

            def split_h(n, slot):
                dve.wait_ge(h_hi_done, n + 1)
                dve.tensor_tensor(h_lo[:, slot, :, :].rearrange("p g (b s) -> p b g s", s=S),
                                  h_raw[:, slot, :, :].rearrange("p b (g s) -> p b g s", s=S),
                                  h_hi[:, slot, :, :].bitcast(F32).rearrange("p g (b s) -> p b g s", s=S),
                                  ALU.subtract).then_inc(h_lo_done, 1)

            split_w(0, 0)
            split_h(0, 0)

            def groups(i, last):
                for k in range(UN):
                    n = i * UN + k
                    if not (last and k == UN - 1):
                        split_h(n + 1, (k + 1) % 2)
                    if k % NT == 2 and not (last and k > NT):
                        split_w(i * 2 + k // NT + 1, 1 - k // NT)
                    dve.wait_ge(unit_done, n + 1)
                    for j in range(4):
                        part = result(k % NT, j)
                        m = dve.tensor_tensor(part, part, ps[:, k % 2, j, :], ALU.add)
                    m.then_inc(bank_free, 1)

            with dve.Fori(0, LAST) as i:
                groups(i, False)
            groups(LAST, True)

        @block.tensor
        def _(pe):
            def groups(i):
                for k in range(UN):
                    n = i * UN + k
                    w, s = k // NT, k % 2
                    if k % NT == 0:
                        pe.wait_ge(w_lo_done, i * 2 + k // NT + 1)
                    pe.wait_ge(h_lo_done, n + 1)
                    pe.wait_ge(bank_free, n + 1)
                    for j in range(4):
                        cols = slice(j * P, (j + 1) * P)
                        for g in range(G):
                            if tokens_first:
                                m = split_product(pe, ps[:, s, j, :], h_hi[:, s, g, cols], h_lo[:, s, g, cols],
                                                  w_hi[:, w, g, :], w_lo[:, w, g, :], g == 0, g == G - 1)
                            else:
                                m = split_product(pe, ps[:, s, j, :], w_hi[:, w, g, cols], w_lo[:, w, g, cols],
                                                  h_hi[:, s, g, :], h_lo[:, s, g, :], g == 0, g == G - 1)
                    m.then_inc(unit_done, 1)

            with pe.Fori(0, HK // 2) as i:
                groups(i)


def load_x(nc, a, x2):
    with ExitStack() as opened:
        x_loaded = opened.enter_context(nc.semaphore("x2_loaded"))
        block = opened.enter_context(nc.Block())

        @block.sync
        def _(sp):
            sp.dma_start(x2[:, :, :], a["x"].rearrange("(t p) n -> p t n", p=P)).then_inc(x_loaded, 16)
            sp.wait_ge(x_loaded, 16)


def values_of_y(nc, a, scratch, y, y_hi, y_lo):
    with ExitStack() as opened:
        hold = opened.enter_context
        BANKS = 6
        w_raw = hold(nc.sbuf_tensor("yv_w_raw", [P, KC, HK * D], F32))
        w_hi = hold(nc.sbuf_tensor("yv_w_hi", [P, KC, HK * D], F32R))
        w_lo = hold(nc.sbuf_tensor("yv_w_lo", [P, KC, HK * D], F32R))
        rows = hold(nc.sbuf_tensor("yv_rows", [P, 3, HK * D], F32))
        ps_v = hold(nc.psum_tensor("yv_ps", [P, BANKS, 512], F32))
        w_loaded = hold(nc.semaphore("yv_w_loaded"))
        w_hi_done = hold(nc.semaphore("yv_w_hi_done"))
        w_lo_done = hold(nc.semaphore("yv_w_lo_done"))
        y_hi_done = hold(nc.semaphore("yv_y_hi_done"))
        y_lo_done = hold(nc.semaphore("yv_y_lo_done"))
        v_done = hold(nc.semaphore("yv_v_done"))
        by_act = hold(nc.semaphore("yv_by_act"))
        by_dve = hold(nc.semaphore("yv_by_dve"))
        stored = [hold(nc.semaphore(f"yv_stored{k}")) for k in range(3)]
        block = hold(nc.Block())

        @block.sync
        def _(sp):
            sp.dma_start(w_raw[:, :, :].rearrange("p k n -> p (k n)"), a["wv2"]).then_inc(w_loaded, 16)
            for t in range(TILES):
                sp.wait_ge(by_act, t + 1)
                sp.wait_ge(by_dve, t + 1)
                sp.dma_start(scratch["v"][t * P:(t + 1) * P, :], rows[:, t % 3, :]).then_inc(stored[t % 3], 16)
            for k in range(3):
                sp.wait_ge(stored[k], 16 * len(range(k, TILES, 3)))

        @block.scalar
        def _(act):
            def y_high(span):
                toks = slice(span * SPAN, (span + 1) * SPAN)
                act.activation(y_hi[:, :, toks], y[:, :, toks], ACT.Copy).then_inc(y_hi_done, 1)

            y_high(0)
            act.wait_ge(w_loaded, 16)
            for half in range(2):
                cols = slice(half * 512, (half + 1) * 512)
                act.activation(w_hi[:, :, cols], w_raw[:, :, cols], ACT.Copy).then_inc(w_hi_done, 1)
            for t in range(TILES):
                if t % 4 == 0 and t // 4 + 1 < NT:
                    y_high(t // 4 + 1)
                act.wait_ge(v_done, t * 2 + 1)
                if t >= 3:
                    act.wait_ge(stored[t % 3], 16 * (t // 3))
                act.activation(rows[:, t % 3, 0:512], ps_v[:, t * 2 % BANKS, :], ACT.Copy).then_inc(by_act, 1)

        @block.vector
        def _(dve):
            def y_low(span):
                toks = slice(span * SPAN, (span + 1) * SPAN)
                dve.wait_ge(y_hi_done, span + 1)
                dve.tensor_tensor(y_lo[:, :, toks], y[:, :, toks], y_hi[:, :, toks].bitcast(F32), ALU.subtract).then_inc(y_lo_done, 1)

            y_low(0)
            for half in range(2):
                cols = slice(half * 512, (half + 1) * 512)
                dve.wait_ge(w_hi_done, half + 1)
                dve.tensor_tensor(w_lo[:, :, cols], w_raw[:, :, cols], w_hi[:, :, cols].bitcast(F32), ALU.subtract).then_inc(w_lo_done, 1)
            for t in range(TILES):
                if t % 4 == 0 and t // 4 + 1 < NT:
                    y_low(t // 4 + 1)
                dve.wait_ge(v_done, t * 2 + 2)
                if t >= 3:
                    dve.wait_ge(stored[t % 3], 16 * (t // 3))
                dve.tensor_copy(rows[:, t % 3, 512:1024], ps_v[:, (t * 2 + 1) % BANKS, :]).then_inc(by_dve, 1)

        @block.tensor
        def _(pe):
            for t in range(TILES):
                toks = slice(t * P, (t + 1) * P)
                if t % 4 == 0:
                    pe.wait_ge(y_lo_done, t // 4 + 1)
                for half in range(2):
                    cols = slice(half * 512, (half + 1) * 512)
                    if t == 0:
                        pe.wait_ge(w_lo_done, half + 1)
                    if t >= 3:
                        pe.wait_ge(by_dve if half else by_act, t - 2)
                    for k in range(KC):
                        m = split_product(pe, ps_v[:, (t * 2 + half) % BANKS, :], y_hi[:, k, toks], y_lo[:, k, toks],
                                          w_hi[:, k, cols], w_lo[:, k, cols], k == 0, k == KC - 1)
                    m.then_inc(v_done, 1)


def clear(nc, y):
    with ExitStack() as opened:
        block = opened.enter_context(nc.Block())

        @block.vector
        def _(dve):
            dve.memset(y[:, :, :], 0.0)


def stage4(nc, c, a, scratch, y_hi, y_lo):
    with ExitStack() as opened:
        hold = opened.enter_context
        WC = 5 * D
        w_raw = hold(nc.sbuf_tensor("s4_w_raw", [P, KC, WC], F32))
        w_hi = hold(nc.sbuf_tensor("s4_w_hi", [P, 2, KC, WC], F32R))
        w_lo = hold(nc.sbuf_tensor("s4_w_lo", [P, 2, KC, WC], F32R))
        q_t = hold(nc.sbuf_tensor("s4_q_t", [P, 2, BS, G, S], F32))
        k_t = hold(nc.sbuf_tensor("s4_k_t", [P, 2, SPAN], F32))
        v_r = hold(nc.sbuf_tensor("s4_v_r", [P, 2, 4, D], F32))
        scores = hold(nc.sbuf_tensor("s4_scores", [P, BS, S], F32))
        probs = hold(nc.sbuf_tensor("s4_probs", [P, BS, S], F32))
        weights = hold(nc.sbuf_tensor("s4_weights", [P, BS * S], F32))
        weights_t = hold(nc.sbuf_tensor("s4_weights_t", [P, 4, GS], F32))
        o_t = hold(nc.sbuf_tensor("s4_o_t", [P, 2, BS, GS], F32))
        top = hold(nc.sbuf_tensor("s4_top", [P, BS], F32))
        total = hold(nc.sbuf_tensor("s4_total", [P, BS], F32))
        inv = hold(nc.sbuf_tensor("s4_inv", [P, BS], F32))
        ps_proj = hold(nc.psum_tensor("s4_ps_proj", [P, 2, 512], F32))
        ps_scores = hold(nc.psum_tensor("s4_ps_scores", [P, BS, S], F32))
        ps_turn = hold(nc.psum_tensor("s4_ps_turn", [P, 4, GS], F32))
        ps_o = hold(nc.psum_tensor("s4_ps_o", [P, SEQ, 4, GS], F32))
        w_loaded = hold(nc.semaphore("s4_w_loaded"))
        v_loaded = [hold(nc.semaphore(f"s4_v{k}_loaded")) for k in range(2)]
        w_hi_done = hold(nc.semaphore("s4_w_hi_done"))
        w_lo_done = hold(nc.semaphore("s4_w_lo_done"))
        proj_done = hold(nc.semaphore("s4_proj_done"))
        proj_free = hold(nc.semaphore("s4_proj_free"))
        scores_done = hold(nc.semaphore("s4_scores_done"))
        soft_step = hold(nc.semaphore("s4_soft_step"))
        exp_done = hold(nc.semaphore("s4_exp_done"))
        turn_done = hold(nc.semaphore("s4_turn_done"))
        pv_done = hold(nc.semaphore("s4_pv_done"))
        o_free = hold(nc.semaphore("s4_o_free"))
        store_free = [hold(nc.semaphore(f"s4_store{k}_free")) for k in range(2)]
        block = hold(nc.Block())
        UN = 2 * NT
        PJ = 5
        STEPS = 7
        LAST = HK // 2 - 1

        @block.sync
        def _(sp):
            for k in range(2):
                sp.sem_inc(store_free[k], 16)
            sp.dma_start(w_raw[:, :, :].rearrange("p k n -> p (k n)"), a["w2"][0]).then_inc(w_loaded, 16)

            def load_v(grp, k):
                src = scratch["v"][k % NT * SPAN:(k % NT + 1) * SPAN, bass.ds(grp * D, D)]
                sp.dma_start(v_r[:, k % 2, :, :], src.rearrange("(j p) d -> p j d", p=P)).then_inc(v_loaded[k % 2], 16)

            load_v(0, 0)
            load_v(0, 1)

            def groups(i, last):
                for k in range(UN):
                    n = i * UN + k
                    if k % NT == 0 and not (last and k > 0):
                        sp.wait_ge(w_lo_done, i * 2 + k // NT + 1)
                        sp.dma_start(w_raw[:, :, :].rearrange("p k n -> p (k n)"),
                                     a["w2"][bass.ds(i * 2 + k // NT + 1, 1)].rearrange("o p n -> p (o n)")).then_inc(w_loaded, 16)
                    sp.wait_ge(o_free, n + 2)
                    if not (last and k >= UN - 2):
                        load_v(i * 2 + (k + 2) // NT, k + 2)
                    dst = scratch["aT"][k % NT * BS:(k % NT + 1) * BS, :, bass.ds(i * 2 + k // NT, 1), :]
                    sp.dma_start(dst.rearrange("b p o n -> p b (o n)"), o_t[:, k % 2, :, :]).then_inc(store_free[k % 2], 16)

            with sp.Fori(0, LAST) as i:
                groups(i, False)
            groups(LAST, True)
            for k in range(2):
                sp.wait_ge(store_free[k], 16 + 16 * HK * NT // 2)

        @block.scalar
        def _(act):
            act.sem_inc(o_free, 1)
            act.sem_inc(proj_free, 2)

            def split_w(grp, slot):
                act.wait_ge(w_loaded, grp * 16 + 16)
                act.activation(w_hi[:, slot, :, :], w_raw[:, :, :], ACT.Copy).then_inc(w_hi_done, 1)

            def copies(n, k):
                for r in range(PJ):
                    act.wait_ge(proj_done, n * PJ + r + 1)
                    src = ps_proj[:, (k * PJ + r) % 2, :]
                    if r < G:
                        m = act.activation(q_t[:, k % 2, :, r, :], src.rearrange("p (b s) -> p b s", s=S), ACT.Copy)
                    else:
                        m = act.activation(k_t[:, k % 2, :], src, ACT.Copy)
                    m.then_inc(proj_free, 1)

            split_w(0, 0)
            copies(0, 0)

            def groups(i, last):
                for k in range(UN):
                    n = i * UN + k
                    act.wait_ge(soft_step, n * STEPS + 3)
                    act.activation(probs[:, :, :], scores[:, :, :], ACT.Exp, scale=SCALE).then_inc(exp_done, 1)
                    if k % NT == 1 and not (last and k > NT):
                        split_w(i * 2 + k // NT + 1, 1 - k // NT)
                    if not (last and k == UN - 1):
                        copies(n + 1, k + 1)
                    act.wait_ge(pv_done, n + 1)
                    act.wait_ge(store_free[k % 2], i * (UN * 8) + (k // 2) * 16 + 16)
                    for q in range(SEQ):
                        m = act.activation(o_t[:, k % 2, q:BS:SEQ, :], ps_o[:, q, :, :], ACT.Copy)
                    m.then_inc(o_free, 1)

            with act.Fori(0, LAST) as i:
                groups(i, False)
            groups(LAST, True)

        @block.vector
        def _(dve):
            def split_w(grp, slot):
                dve.wait_ge(w_hi_done, grp + 1)
                dve.tensor_tensor(w_lo[:, slot, :, :], w_raw[:, :, :], w_hi[:, slot, :, :].bitcast(F32),
                                  ALU.subtract).then_inc(w_lo_done, 1)

            split_w(0, 0)

            def over_keys(col):
                return col.rearrange("p (b o) -> p b o", o=1).to_broadcast([P, BS, S])

            def groups(i, last):
                for k in range(UN):
                    n = i * UN + k
                    base = n * STEPS
                    causal = c["causal"][:, :].rearrange("p (o s) -> p o s", o=1).to_broadcast([P, BS, S])
                    dve.wait_ge(scores_done, n + 1)
                    dve.tensor_tensor(scores[:, :, :], ps_scores[:, :, :], causal, ALU.add).then_inc(soft_step, 1)
                    dve.wait_ge(soft_step, base + 1)
                    dve.tensor_reduce(top[:, :], scores[:, :, :], AX.X, ALU.max).then_inc(soft_step, 1)
                    dve.wait_ge(soft_step, base + 2)
                    dve.tensor_tensor(scores[:, :, :], scores[:, :, :], over_keys(top[:, :]), ALU.subtract).then_inc(soft_step, 1)
                    dve.wait_ge(exp_done, n + 1)
                    dve.tensor_reduce(total[:, :], probs[:, :, :], AX.X, ALU.add).then_inc(soft_step, 1)
                    dve.wait_ge(soft_step, base + 4)
                    dve.reciprocal(inv[:, :], total[:, :]).then_inc(soft_step, 1)
                    dve.wait_ge(soft_step, base + 5)
                    dve.tensor_tensor(weights[:, :].rearrange("p (b s) -> p b s", s=S), probs[:, :, :], over_keys(inv[:, :]),
                                      ALU.mult).then_inc(soft_step, 1)
                    if k % NT == 1 and not (last and k > NT):
                        split_w(i * 2 + k // NT + 1, 1 - k // NT)
                    dve.wait_ge(turn_done, n + 1)
                    dve.tensor_copy(weights_t[:, :, :], ps_turn[:, :, :]).then_inc(soft_step, 1)

            with dve.Fori(0, LAST) as i:
                groups(i, False)
            groups(LAST, True)

        @block.tensor
        def _(pe):
            def project(n, k, grp, heads):
                w, span = (k // NT) % 2, k % NT
                if span == 0:
                    pe.wait_ge(w_lo_done, grp + 1)
                for r in heads:
                    pe.wait_ge(proj_free, n * PJ + r + 1)
                    for q in range(KC):
                        cols = slice(r * D, (r + 1) * D)
                        toks = slice(span * SPAN, (span + 1) * SPAN)
                        m = split_product(pe, ps_proj[:, (k * PJ + r) % 2, :], w_hi[:, w, q, cols], w_lo[:, w, q, cols],
                                          y_hi[:, q, toks], y_lo[:, q, toks], q == 0, q == KC - 1)
                    m.then_inc(proj_done, 1)

            project(0, 0, 0, range(PJ))

            def groups(i, last):
                for k in range(UN):
                    n = i * UN + k
                    s = k % 2
                    pe.wait_ge(proj_free, n * PJ + PJ + 2)
                    for b in range(BS):
                        m = pe.matmul(ps_scores[:, b, :], q_t[:, s, b, :, :].rearrange("p g s -> p (g s)"),
                                      k_t[:, s, b * S:(b + 1) * S], start=True, stop=True)
                    m.then_inc(scores_done, 1)
                    if not (last and k == UN - 1):
                        project(n + 1, k + 1, i * 2 + (k + 1) // NT, range(PJ - 1))
                    pe.wait_ge(soft_step, n * STEPS + 6)
                    for j in range(4):
                        m = pe.transpose(ps_turn[:, j, :], weights[:, j * P:(j + 1) * P], c["ident"][:, :])
                    m.then_inc(turn_done, 1)
                    if not (last and k == UN - 1):
                        project(n + 1, k + 1, i * 2 + (k + 1) // NT, range(PJ - 1, PJ))
                    pe.wait_ge(v_loaded[s], i * (UN * 8) + (k // 2) * 16 + 16)
                    pe.wait_ge(soft_step, n * STEPS + 7)
                    pe.wait_ge(o_free, n + 1)
                    for j in range(4):
                        for q in range(SEQ):
                            rows = slice(q * S, (q + 1) * S)
                            m = pe.matmul(ps_o[:, q, j, :], v_r[rows, s, j, :], weights_t[rows, j, :], start=True, stop=True)
                    m.then_inc(pv_done, 1)

            with pe.Fori(0, LAST) as i:
                groups(i, False)
            groups(LAST, True)


def stage6(nc, c, a, x2, out):
    with ExitStack() as opened:
        hold = opened.enter_context
        mix = hold(nc.sbuf_tensor("s6_mix", [P, TILES, S], F32))
        mix_bd = hold(nc.sbuf_tensor("s6_mix_bd", [P, TILES, P], F32))
        y_t = hold(nc.sbuf_tensor("s6_y_t", [P, TILES, KC * P], F32))
        wb = hold(nc.sbuf_tensor("s6_wb", [P, KC, HID], F32))
        wga = hold(nc.sbuf_tensor("s6_wga", [P, KC, E + ER], F32))
        lb = hold(nc.sbuf_tensor("s6_lb", [P, HID], F32))
        bias = hold(nc.sbuf_tensor("s6_bias", [P, HID], F32))
        gate_h = hold(nc.sbuf_tensor("s6_gate_h", [P, TILES, E + ER], F32))
        pick = [hold(nc.sbuf_tensor(f"s6_pick{k}", [P, TILES, E], F32)) for k in range(4)]
        best = [hold(nc.sbuf_tensor(f"s6_best{k}", [P, TILES], F32)) for k in range(4)]
        order = hold(nc.sbuf_tensor("s6_order", [P, E], F32))
        order_i = hold(nc.sbuf_tensor("s6_order_i", [P, E], I32))
        hw = hold(nc.sbuf_tensor("s6_hw", [P, TILES, ER], F32))
        hw_t = hold(nc.sbuf_tensor("s6_hw_t", [P, 2, P], F32))
        done = hold(nc.sbuf_tensor("s6_done", [P, 2, HID], F32))
        ps_y = hold(nc.psum_tensor("s6_ps_y", [P, 2, 512], F32))
        ps_g = hold(nc.psum_tensor("s6_ps_g", [P, 2, 512], F32))
        ps_t = hold(nc.psum_tensor("s6_ps_t", [P, 2, 512], F32))
        ps_out = hold(nc.psum_tensor("s6_ps_out", [P, 2, 512], F32))
        loaded = hold(nc.semaphore("s6_loaded"))
        mix_loaded = hold(nc.semaphore("s6_mix_loaded"))
        order_set = hold(nc.semaphore("s6_order_set"))
        step_done = hold(nc.semaphore("s6_step"))
        mix_done = hold(nc.semaphore("s6_mix_done"))
        y_done = hold(nc.semaphore("s6_y_done"))
        y_copied = hold(nc.semaphore("s6_y_copied"))
        g_done = hold(nc.semaphore("s6_g_done"))
        g_copied = hold(nc.semaphore("s6_g_copied"))
        exp_in = hold(nc.semaphore("s6_exp_in"))
        exp_out = hold(nc.semaphore("s6_exp_out"))
        hw_done = hold(nc.semaphore("s6_hw_done"))
        t_done = hold(nc.semaphore("s6_t_done"))
        t_copied = hold(nc.semaphore("s6_t_copied"))
        out_done = hold(nc.semaphore("s6_out_done"))
        added = hold(nc.semaphore("s6_added"))
        stored = [hold(nc.semaphore(f"s6_stored{k}")) for k in range(2)]
        block = hold(nc.Block())

        @block.sync
        def _(sp):
            sp.dma_start(wga[:, :, :].rearrange("p k n -> p (k n)"), a["wga"]).then_inc(loaded, 16)
            sp.dma_start(wb[:, :, :].rearrange("p k n -> p (k n)"), a["wb"]).then_inc(loaded, 16)
            sp.dma_start(lb[:, :], a["lb"]).then_inc(loaded, 16)
            sp.dma_start(bias[:, :], a["bias"].to_broadcast([P, HID])).then_inc(loaded, 16)
            for t in range(TILES):
                sp.wait_ge(added, t + 1)
                sp.dma_start(out[t * P:(t + 1) * P, :], done[:, t % 2, :]).then_inc(stored[t % 2], 16)
            for k in range(2):
                sp.wait_ge(stored[k], 16 * TILES // 2)

        @block.gpsimd
        def _(pool):
            for t in range(TILES):
                pool.indirect_dma_start(out=mix[:, t, :], out_offset=None, in_=a["mix"],
                                        in_offset=bass.IndirectOffsetOnAxis(ap=c["subj"][:, t:t + 1], axis=0)
                                        ).then_inc(mix_loaded, 16)
            pool.iota(order_i[:, :], pattern=[[-1, E]], base=E, channel_multiplier=0).then_inc(order_set, 1)

        @block.scalar
        def _(act):
            for t in range(TILES):
                act.wait_ge(y_done, t + 1)
                act.activation(y_t[:, t, :], ps_y[:, t % 2, :], ACT.Copy).then_inc(y_copied, 1)
            act.wait_ge(exp_in, 1)
            act.activation(best[2][:, :], best[2][:, :], ACT.Exp).then_inc(exp_out, 1)
            for t in range(TILES):
                act.wait_ge(t_done, t + 1)
                act.activation(hw_t[:, t % 2, :], ps_t[:, t % 2, 0:P], ACT.Copy).then_inc(t_copied, 1)

        @block.vector
        def _(dve):
            steps = [0]

            def step(m):
                steps[0] += 1
                m.then_inc(step_done, 1)
                dve.wait_ge(step_done, steps[0])

            dve.wait_ge(mix_loaded, 16 * TILES)
            for s in range(SEQ):
                m = dve.tensor_tensor(mix_bd[:, :, s * S:(s + 1) * S], mix[:, :, :],
                                      c["own_seq"][:, s:s + 1].rearrange("p (o q) -> p o q", o=1).to_broadcast([P, TILES, S]), ALU.mult)
            m.then_inc(mix_done, 1)
            for t in range(TILES):
                dve.wait_ge(g_done, t + 1)
                dve.tensor_copy(gate_h[:, t, :], ps_g[:, t % 2, 0:E + ER]).then_inc(g_copied, 1)
            dve.wait_ge(g_copied, TILES)
            dve.wait_ge(order_set, 1)
            logits = gate_h[:, :, 0:E]

            def wide(col):
                return col[:, :].rearrange("p (t o) -> p t o", o=1).to_broadcast([P, TILES, E])

            step(dve.tensor_copy(order[:, :], order_i[:, :]))
            rank = order[:, :].rearrange("p (o e) -> p o e", o=1).to_broadcast([P, TILES, E])
            for k in range(2):
                src = logits if k == 0 else pick[3][:, :, :]
                step(dve.tensor_reduce(best[k][:, :], src, AX.X, ALU.max))
                step(dve.tensor_tensor(pick[k][:, :, :], src, wide(best[k]), ALU.is_equal))
                step(dve.tensor_tensor(pick[k][:, :, :], pick[k][:, :, :], rank, ALU.mult))
                step(dve.tensor_reduce(best[3][:, :], pick[k][:, :, :], AX.X, ALU.max))
                step(dve.tensor_tensor(pick[k][:, :, :], rank, wide(best[3]), ALU.is_equal))
                if k == 0:
                    step(dve.scalar_tensor_tensor(out=pick[3][:, :, :], in0=pick[0][:, :, :], scalar=OUT_OF_REACH, in1=logits,
                                                  op0=ALU.mult, op1=ALU.add))
            step(dve.tensor_tensor(best[2][:, :], best[1][:, :], best[0][:, :], ALU.subtract))
            dve.sem_inc(exp_in)
            dve.wait_ge(exp_out, 1)
            step(dve.tensor_scalar(best[0][:, :], best[2][:, :], 1.0, None, ALU.add))
            step(dve.reciprocal(best[0][:, :], best[0][:, :]))
            step(dve.tensor_tensor(best[1][:, :], best[0][:, :], best[2][:, :], ALU.mult))
            step(dve.tensor_tensor(pick[0][:, :, :], pick[0][:, :, :], wide(best[0]), ALU.mult))
            step(dve.tensor_tensor(pick[1][:, :, :], pick[1][:, :, :], wide(best[1]), ALU.mult))
            step(dve.tensor_tensor(pick[2][:, :, :], pick[0][:, :, :], pick[1][:, :, :], ALU.add))
            step(dve.tensor_tensor(hw[:, :, :].rearrange("p t (e r) -> p (t e) r", r=R),
                                   gate_h[:, :, E:].rearrange("p t (e r) -> p t e r", r=R),
                                   pick[2][:, :, :].rearrange("p t (e o) -> p t e o", o=1).to_broadcast([P, TILES, E, R]), ALU.mult))
            dve.sem_inc(hw_done)
            dve.wait_ge(loaded, 64)
            for t in range(TILES):
                step(dve.tensor_tensor(x2[:, t, :], x2[:, t, :], bias[:, :], ALU.add))
                dve.wait_ge(out_done, t + 1)
                if t >= 2:
                    dve.wait_ge(stored[t % 2], 16 * (t // 2))
                dve.tensor_tensor(done[:, t % 2, :], x2[:, t, :], ps_out[:, t % 2, :], ALU.add).then_inc(added, 1)

        @block.tensor
        def _(pe):
            pe.wait_ge(mix_done, 1)
            pe.wait_ge(loaded, 64)

            def gate(t):
                pe.wait_ge(y_copied, t + 1)
                if t >= 2:
                    pe.wait_ge(g_copied, t - 1)
                for k in range(KC):
                    m = pe.matmul(ps_g[:, t % 2, 0:E + ER], y_t[:, t, k * P:(k + 1) * P], wga[:, k, :], start=(k == 0), stop=(k == KC - 1))
                m.then_inc(g_done, 1)

            for t in range(TILES):
                if t >= 2:
                    pe.wait_ge(y_copied, t - 1)
                for k in range(KC):
                    m = pe.matmul(ps_y[:, t % 2, k * P:(k + 1) * P], x2[:, t, k * P:(k + 1) * P], mix_bd[:, t, :], start=True, stop=True)
                m.then_inc(y_done, 1)
                if t > 0:
                    gate(t - 1)
            gate(TILES - 1)

            for t in range(TILES):
                if t >= 2:
                    pe.wait_ge(added, t - 1)
                for k in range(KC):
                    pe.matmul(ps_out[:, t % 2, :], y_t[:, t, k * P:(k + 1) * P], wb[:, k, :], start=(k == 0), stop=False)
                if t == 0:
                    pe.wait_ge(hw_done, 1)
                pe.transpose(ps_t[:, t % 2, 0:P], hw[:, t, :], c["ident"][:, :]).then_inc(t_done, 1)
                pe.wait_ge(t_copied, t + 1)
                pe.matmul(ps_out[:, t % 2, :], hw_t[:, t % 2, :], lb[:, :], start=False, stop=True).then_inc(out_done, 1)


def build(nc, a, out, scratch):
    with ExitStack() as opened:
        hold = opened.enter_context
        ident = hold(nc.sbuf_tensor("ident", [P, P], F32))
        tok_i = hold(nc.sbuf_tensor("tok_i", [P, 1], I32))
        tok_f = hold(nc.sbuf_tensor("tok_f", [P, 1], F32))
        ident_r = hold(nc.sbuf_tensor("ident_r", [P, P], F32R))
        key_f = hold(nc.sbuf_tensor("key_f", [P, L], F32))
        vrow = hold(nc.sbuf_tensor("vrow", [P, B * 4], I32))
        subj = hold(nc.sbuf_tensor("subj", [P, TILES], I32))
        len_all = hold(nc.sbuf_tensor("len_all", [P, B], I32))
        len_f = hold(nc.sbuf_tensor("len_f", [P, B], F32))
        table = hold(nc.sbuf_tensor("table", [1, B * NPP], I32))
        causal = hold(nc.sbuf_tensor("causal", [P, S], F32))
        own_seq = hold(nc.sbuf_tensor("own_seq", [P, SEQ], F32))
        c = dict(ident=ident, ident_r=ident_r, tok_i=tok_i, tok_f=tok_f, key_f=key_f, vrow=vrow, subj=subj,
                 len_all=len_all, len_f=len_f, table=table, causal=causal, own_seq=own_seq)
        stage1(nc, c, a, scratch)
        stage2(nc, c, a, scratch)
        with ExitStack() as parts:
            y_hi = parts.enter_context(nc.sbuf_tensor("y_hi", [P, KC, TOK], F32R))
            y_lo = parts.enter_context(nc.sbuf_tensor("y_lo", [P, KC, TOK], F32R))
            with nc.sbuf_tensor("y", [P, KC, TOK], F32) as y:
                clear(nc, y)
                over_heads(nc, "s3", a["wo"], scratch["oT"],
                           lambda span, j: y[:, j, span * SPAN:(span + 1) * SPAN], tokens_first=False)
                values_of_y(nc, a, scratch, y, y_hi, y_lo)
            stage4(nc, c, a, scratch, y_hi, y_lo)
        with nc.sbuf_tensor("x2", [P, TILES, HID], F32) as x2:
            load_x(nc, a, x2)
            over_heads(nc, "s5", a["wd"], scratch["aT"], lambda span, j: x2[:, span * 4 + j, :], tokens_first=True)
            stage6(nc, c, a, x2, out)


def kernel(x, itok_Bx16_0_63, itok_B_207_1644, itok_B_0_30, L0_cond_Wq, L0_cond_Wk, L0_cond_Wv, L0_cond_Wo,
           L0_cond_q_norm_w, L0_cond_k_norm_w, L0_cond_k_cache, L0_cond_v_cache, L0_attn_w_qkv, L0_attn_w_dense,
           L0_cond2_weights, L0_ffn_W_base, L0_ffn_b_base, L0_ffn_W_gate, L0_ffn_A, L0_ffn_B):
    import concourse.bacc as bacc
    from concourse.bass_utils import run_bass_kernel_spmd

    def laid(v):
        return np.ascontiguousarray(np.asarray(v))

    x = np.asarray(x).reshape(TOK, HID)
    w1 = np.concatenate([np.asarray(L0_cond_Wq), np.asarray(L0_cond_Wk), np.asarray(L0_cond_Wv)], 0)
    wqkv = np.asarray(L0_attn_w_qkv)
    w2 = np.concatenate([wqkv[:HQ * D].reshape(HK, G * D, HID), wqkv[HQ * D:(HQ + HK) * D].reshape(HK, D, HID)], 1)
    arrays = {
        "x": laid(x),
        "xT": laid(x.T),
        "w1": laid(w1.reshape(12, 512, KC, P).transpose(0, 3, 2, 1).reshape(12, P, KC * 512)),
        "freq": (np.float32(1.0) / np.float32(THETA) ** (np.arange(0, D, 2, dtype=np.float32) / np.float32(D))).astype(np.float32).reshape(1, HALF),
        "qw": laid(L0_cond_q_norm_w).reshape(1, D),
        "kw": laid(L0_cond_k_norm_w).reshape(1, D),
        "table": laid(itok_Bx16_0_63).reshape(1, B * NPP),
        "table_t": laid(np.asarray(itok_Bx16_0_63).reshape(B, 4, 4).transpose(2, 0, 1)).reshape(4, B * 4),
        "lens": laid(itok_B_207_1644).reshape(1, B),
        "lens_t": laid(np.asarray(itok_B_207_1644).reshape(TILES, SEQ).T),
        "subj_t": laid(np.asarray(itok_B_0_30).reshape(TILES, SEQ).T),
        "kpool": laid(np.asarray(L0_cond_k_cache).transpose(3, 0, 2, 1)).reshape(D, PAGES * HK * PSIZE),
        "vpool": laid(L0_cond_v_cache).reshape(PAGES * PSIZE, HK * D),
        "wo": laid(np.asarray(L0_cond_Wo).reshape(HID, HK, G, D).transpose(1, 3, 2, 0)).reshape(HK, D, G * HID),
        "w2": laid(w2.reshape(HK, 5 * D, KC, P).transpose(0, 3, 2, 1)).reshape(HK, P, KC * 5 * D),
        "wv2": laid(wqkv[(HQ + HK) * D:].reshape(HK * D, KC, P).transpose(2, 1, 0)).reshape(P, KC * HK * D),
        "wd": laid(np.asarray(L0_attn_w_dense).reshape(HID, HK, G, D).transpose(1, 3, 2, 0)).reshape(HK, D, G * HID),
        "mix": laid(L0_cond2_weights).reshape(S * S, S),
        "wb": laid(np.asarray(L0_ffn_W_base).reshape(HID, KC, P).transpose(2, 1, 0)).reshape(P, KC * HID),
        "wga": laid(np.concatenate([np.asarray(L0_ffn_W_gate), np.asarray(L0_ffn_A).reshape(ER, HID)], 0)
                    .reshape(E + ER, KC, P).transpose(2, 1, 0)).reshape(P, KC * (E + ER)),
        "lb": laid(np.asarray(L0_ffn_B).transpose(0, 2, 1)).reshape(ER, HID),
        "bias": laid(L0_ffn_b_base).reshape(1, HID),
    }
    nc = bacc.Bacc("TRN2", target_bir_lowering=False, num_devices=1)
    a = {k: nc.dram_tensor(k + "_in", v.shape, mybir.dt.from_np(v.dtype), kind="ExternalInput").ap() for k, v in arrays.items()}
    out = nc.dram_tensor("out", (TOK, HID), F32, kind="ExternalOutput").ap()
    scratch = {
        "qT": nc.dram_tensor("qT_scratch", (B, D, HK, GS), F32).ap(),
        "kT": nc.dram_tensor("kT_scratch", (B, D, 2, GS), F32).ap(),
        "v": nc.dram_tensor("v_scratch", (TOK, HK * D), F32).ap(),
        "oT": nc.dram_tensor("oT_scratch", (B, D, HK, GS), F32).ap(),
        "aT": nc.dram_tensor("aT_scratch", (B, D, HK, GS), F32).ap(),
    }
    build(nc, a, out, scratch)
    r = run_bass_kernel_spmd(nc, [{k + "_in": v for k, v in arrays.items()}], core_ids=[0])
    return r.results[0]["out"].reshape(B, S, HID)
```

```python
import math
from contextlib import ExitStack

import numpy as np

import concourse.bass as bass
from concourse import mybir

F32 = mybir.dt.float32
F32R = mybir.dt.float32r
BF16 = mybir.dt.bfloat16
I32 = mybir.dt.int32
ACT = mybir.ActivationFunctionType
ALU = mybir.AluOpType
AX = mybir.AxisListType

B, S, HID = 64, 32, 512
TOK = B * S
P = 128
D, HQ, HK = 128, 32, 8
G = HQ // HK
PAGES, PSIZE, NPP = 64, 32, 16
L = PSIZE * NPP
KC = HID // P
TILES = TOK // P
SEQ = P // S
NT = 4
SPAN = TOK // NT
BS = B // NT
E, R = 8, 16
ER = E * R
THETA = 10000.0
EPS = 1e-6
SCALE = 1.0 / math.sqrt(D)
OUT_OF_REACH = -1e30
HALF = D // 2
GS = G * S


def split_product(pe, out, a_hi, a_lo, b_hi, b_lo, start, stop):
    pe.matmul(out, a_hi, b_hi, start=start, stop=False)
    pe.matmul(out, a_hi, b_lo, start=False, stop=False)
    return pe.matmul(out, a_lo, b_hi, start=False, stop=stop)


def stage1(nc, c, a, scratch):
    CB = 12
    UN = TILES // 2
    with ExitStack() as opened:
        hold = opened.enter_context
        k_pool = c["k_pool"]
        quarter = PAGES // 4 * HK * PSIZE
        x_raw = k_pool[:, 0:quarter].rearrange("p (k n) -> p k n", k=2)
        x_hi = hold(nc.sbuf_tensor("x_hi", [P, KC, TOK], F32R))
        x_lo = hold(nc.sbuf_tensor("x_lo", [P, KC, TOK], F32R))
        w_raw = hold(nc.sbuf_tensor("w_raw", [P, 2, KC * 512], F32))
        w_hi = hold(nc.sbuf_tensor("w_hi", [P, 2, KC * 512], F32R))
        w_lo = hold(nc.sbuf_tensor("w_lo", [P, 2, KC * 512], F32R))
        tab_q = k_pool[:, quarter:2 * quarter].rearrange("p (k t d) -> p k t d", k=2, d=D)
        tab_k = k_pool[:, 2 * quarter:3 * quarter].rearrange("p (k t d) -> p k t d", k=2, d=D)
        squares = hold(nc.sbuf_tensor("squares", [P, 2, 1024], BF16))
        unit_rows = k_pool[:, 3 * quarter:3 * quarter + 1024]
        turning = hold(nc.sbuf_tensor("turning", [P, 2, 1024], F32))
        by_cos = k_pool[:, 3 * quarter + 1024:3 * quarter + 2048]
        by_sin = k_pool[:, 3 * quarter + 2048:3 * quarter + 3072]
        turned = hold(nc.sbuf_tensor("turned", [P, 2, 1024], F32))
        sumsq = hold(nc.sbuf_tensor("sumsq", [P, 2, 8], F32))
        root = hold(nc.sbuf_tensor("root", [P, 2, 8], F32))
        nw = hold(nc.sbuf_tensor("nw", [P, 4, 8], F32))
        eps = hold(nc.sbuf_tensor("eps", [P, 1], F32))
        key_i = turned[:, 1, 0:L].bitcast(I32)
        ps_proj = hold(nc.psum_tensor("ps_proj", [P, 2, 2, 512], F32))
        ps_turn = hold(nc.psum_tensor("ps_turn", [P, 2, 2, 512], F32))
        x_loaded0 = hold(nc.semaphore("x_loaded0"))
        x_loaded1 = hold(nc.semaphore("x_loaded1"))
        x_hi_done = hold(nc.semaphore("x_hi_done"))
        x_lo_done = hold(nc.semaphore("x_lo_done"))
        w_loaded0 = hold(nc.semaphore("w_loaded0"))
        w_loaded1 = hold(nc.semaphore("w_loaded1"))
        w_hi_done = hold(nc.semaphore("w_hi_done"))
        w_lo_done = hold(nc.semaphore("w_lo_done"))
        proj_done = hold(nc.semaphore("proj_done"))
        proj_free = hold(nc.semaphore("proj_free"))
        root_done = hold(nc.semaphore("root_done"))
        dve_step = hold(nc.semaphore("dve_step"))
        halves_done = hold(nc.semaphore("halves_done"))
        rotated = hold(nc.semaphore("rotated"))
        turn_done = hold(nc.semaphore("turn_done"))
        turned_done = hold(nc.semaphore("turned_done"))
        store0_free = hold(nc.semaphore("store0_free"))
        store1_free = hold(nc.semaphore("store1_free"))
        v_copied = hold(nc.semaphore("v_copied"))
        eps_set = hold(nc.semaphore("eps_set"))
        const_loaded = hold(nc.semaphore("const_loaded"))
        pos_ready = hold(nc.semaphore("pos_ready"))
        sines = hold(nc.semaphore("sines"))
        ident_step = hold(nc.semaphore("ident_step"))
        own_set = hold(nc.semaphore("own_set"))
        block = hold(nc.Block())
        x_loaded = [x_loaded0, x_loaded1]
        w_loaded = [w_loaded0, w_loaded1]
        store_free = [store0_free, store1_free]
        angle = turning[:, 0, :].rearrange("p (t f) -> p t f", f=HALF)
        turns = turning[:, 1, :].rearrange("p (t f) -> p t f", f=HALF)
        sin_t = by_cos[:, :].rearrange("p (t f) -> p t f", f=HALF)
        cos_t = by_sin[:, :].rearrange("p (t f) -> p t f", f=HALF)
        freq = turned[:, 0, 0:HALF]
        wq_row = turned[:, 0, 128:256]
        wk_row = turned[:, 0, 256:384]
        len_i = turned[:, 0, 512:512 + TILES].bitcast(I32)
        pos_f = turned[:, 0, 640:640 + TILES]

        @block.sync
        def _(sp):
            sp.sem_inc(store_free[0], 16)
            sp.sem_inc(store_free[1], 16)
            for k in range(2):
                sp.dma_start(x_raw[:, k, :], a["xT"][k * P:(k + 1) * P, :]).then_inc(x_loaded[k], 16)
            for k in range(2):
                sp.dma_start(w_raw[:, k, :], a["w1"][k]).then_inc(w_loaded[k], 16)
            sp.dma_start(freq, a["freq"].to_broadcast([P, HALF])).then_inc(const_loaded, 16)
            sp.dma_start(wq_row, a["qw"].to_broadcast([P, D])).then_inc(const_loaded, 16)
            sp.dma_start(wk_row, a["kw"].to_broadcast([P, D])).then_inc(const_loaded, 16)
            for s in range(SEQ):
                r = slice(s * S, (s + 1) * S)
                sp.dma_start(len_i[r, :], a["lens_t"][s:s + 1, :].to_broadcast([S, TILES])).then_inc(const_loaded, 16)
                sp.dma_start(c["subj"][r, :], a["subj_t"][s:s + 1, :].to_broadcast([S, TILES])).then_inc(const_loaded, 16)
                sp.dma_start(c["vrow"][r, :], a["table_t"][s:s + 1, :].to_broadcast([S, B * 4])).then_inc(const_loaded, 16)
            sp.dma_start(c["len_all"][:, :], a["lens"].to_broadcast([P, B])).then_inc(const_loaded, 16)
            sp.dma_start(c["table"][0:1, :], a["table"]).then_inc(const_loaded, 16)
            for k in range(2, KC):
                sp.wait_ge(x_lo_done, k - 1)
                sp.dma_start(x_raw[:, k % 2, :], a["xT"][k * P:(k + 1) * P, :]).then_inc(x_loaded[k % 2], 16)

            def load_pool(first, last):
                cols = slice(first * quarter // 4, last * quarter // 4)
                sp.dma_start(k_pool[:, cols], a["kpool"][:, cols]).then_inc(c["pool_loaded"], 16)

            sp.wait_ge(x_lo_done, KC)
            load_pool(0, 4)

            def block_of(i, cb, kind):
                if kind != "v":
                    sp.wait_ge(w_lo_done, i * 2 + cb + 1)
                    sp.dma_start(w_raw[:, cb, :],
                                 a["w1"][bass.ds(i * 2 + cb + 2, 1)].rearrange("o p n -> p (o n)")).then_inc(w_loaded[cb], 16)
                for u in range(UN):
                    n = i * 2 * UN + cb * UN + u
                    b0 = u * 2 * SEQ
                    if kind == "q":
                        dst = scratch["qT"][b0:b0 + 2 * SEQ, :, bass.ds(i * 2 + cb, 1), :].rearrange("b p o n -> p b (o n)")
                    elif kind == "k":
                        dst = scratch["kT"][b0:b0 + 2 * SEQ, :, cb, :].rearrange("b p n -> p b n")
                    else:
                        dst = scratch["v"][u * 2 * P:(u + 1) * 2 * P, cb * 512:(cb + 1) * 512].rearrange("(t p) n -> p t n", p=P)
                    if kind == "v":
                        sp.wait_ge(v_copied, cb * UN + u + 1)
                        src = turned[:, u % 2, :].rearrange("p (t n) -> p t n", t=2)
                    else:
                        sp.wait_ge(turned_done, n + 3)
                        src = turned[:, u % 2, :].rearrange("p (b n) -> p b n", n=GS)
                    sp.dma_start(dst, src).then_inc(store_free[u % 2], 16)
                    if kind == "v" and cb * UN + u < 12:
                        load_pool(4 + cb * UN + u, 5 + cb * UN + u)

            with sp.Fori(0, 4) as i:
                for cb in range(2):
                    block_of(i, cb, "q")
            for cb in range(2):
                block_of(4, cb, "k")
            sp.wait_ge(rotated, 1 + 10 * UN)
            for cb in range(2):
                block_of(5, cb, "v")
            for k in range(2):
                sp.wait_ge(store_free[k], 16 + 16 * CB * UN // 2)
            sp.wait_ge(const_loaded, 16 * (5 + 3 * SEQ))

        @block.gpsimd
        def _(pool):
            pool.sem_inc(rotated, 1)
            pool.memset(c["ident"][:, :], 0.0).then_inc(ident_step, 1)
            for s in range(SEQ):
                pool.wait_ge(ident_step, s + 1)
                pool.iota(c["tok_i"][s * S:(s + 1) * S, :], pattern=[[0, 1]], base=0, channel_multiplier=1).then_inc(ident_step, 1)
            pool.wait_ge(ident_step, SEQ + 1)
            pool.iota(key_i[:, :], pattern=[[1, L]], base=0, channel_multiplier=0).then_inc(ident_step, 1)
            pool.wait_ge(ident_step, SEQ + 2)
            pool.affine_select(out=c["ident"][:, :], in_=c["ident"][:, :], compare_op=ALU.not_equal, fill=1.0,
                               base=0, pattern=[[-1, P]], channel_multiplier=1).then_inc(ident_step, 1)
            pool.wait_ge(x_hi_done, KC)
            pool.tensor_tensor(x_lo[:, KC - 1, :], x_raw[:, (KC - 1) % 2, :], x_hi[:, KC - 1, :].bitcast(F32), ALU.subtract).then_inc(x_lo_done, 1)
            with pool.Fori(0, 10) as cb:
                for u in range(UN):
                    pool.wait_ge(halves_done, cb * UN + u + 1)
                    pool.wait_ge(turn_done, cb * UN + u + 1)
                    pool.tensor_tensor(turning[:, u % 2, :], by_cos[:, :], by_sin[:, :], ALU.add).then_inc(rotated, 1)

        @block.scalar
        def _(act):
            for k in range(KC):
                act.wait_ge(x_loaded[k % 2], 16 * (k // 2 + 1))
                act.activation(x_hi[:, k, :], x_raw[:, k % 2, :], ACT.Copy).then_inc(x_hi_done, 1)
                if k == 0:
                    act.wait_ge(w_loaded[0], 16)
                    act.activation(w_hi[:, 0, :], w_raw[:, 0, :], ACT.Copy).then_inc(w_hi_done, 1)
            act.wait_ge(pos_ready, 1)
            act.activation(sin_t, angle, ACT.Sin).then_inc(sines, 1)
            act.activation(cos_t, angle, ACT.Sin, scale=0.5).then_inc(sines, 1)
            act.wait_ge(eps_set, 1)

            def roots(n, u):
                act.wait_ge(proj_done, n + 1)
                for t in range(2):
                    for g in range(G):
                        h = t * G + g
                        m = act.activation(squares[:, u % 2, h * D:(h + 1) * D], ps_proj[:, u % 2, t, g * D:(g + 1) * D], ACT.Square,
                                           accum_out=sumsq[:, u % 2, h:h + 1])
                m.then_inc(root_done, 1)
                act.wait_ge(root_done, n * 2 + 1)
                act.activation(root[:, u % 2, :], sumsq[:, u % 2, :], ACT.Sqrt, bias=eps[:, 0:1], scale=1.0 / D).then_inc(root_done, 1)

            def turn_copy(n, half, u):
                act.wait_ge(turn_done, n + 3)
                act.wait_ge(store_free[u % 2], half * 16 + 16)
                for t in range(2):
                    src = ps_turn[:, u % 2, t, :].rearrange("p (g b s) -> p g b s", g=G, b=SEQ)
                    dst = turned[:, u % 2, t * 512:(t + 1) * 512].rearrange("p (b g s) -> p g b s", g=G, b=SEQ)
                    m = act.activation(dst, src, ACT.Copy)
                m.then_inc(turned_done, 1)

            def split(slot, load, q):
                part = slice(q * 512, (q + 1) * 512)
                if q == 0:
                    act.wait_ge(w_loaded[slot], load * 16 + 16)
                act.activation(w_hi[:, slot, part], w_raw[:, slot, part], ACT.Copy).then_inc(w_hi_done, 1)

            def block_of(i, cb, kind):
                for u in range(UN):
                    n = i * 2 * UN + cb * UN + u
                    if kind == "v":
                        act.wait_ge(proj_done, n + 1)
                        act.wait_ge(store_free[u % 2], (i * UN + cb * (UN // 2) + u // 2) * 16 + 16)
                        for t in range(2):
                            m = act.activation(turned[:, u % 2, t * 512:(t + 1) * 512], ps_proj[:, u % 2, t, :], ACT.Copy)
                        m.then_inc(v_copied, 1)
                    else:
                        if not (kind == "k" and cb == 1 and u >= UN - 2):
                            roots(n + 2, u)
                        turn_copy(n, i * UN + cb * (UN // 2) + u // 2, u)
                    if u < KC and not (kind == "v" and cb == 1):
                        split((cb + 1) % 2, i + cb, u)

            act.sem_inc(turned_done, 2)
            roots(0, 0)
            roots(1, 1)
            with act.Fori(0, 4) as i:
                for cb in range(2):
                    block_of(i, cb, "q")
            for cb in range(2):
                block_of(4, cb, "k")
            for cb in range(2):
                block_of(5, cb, "v")

        @block.vector
        def _(dve):
            steps = [0]

            def step(m):
                steps[0] += 1
                m.then_inc(dve_step, 1)
                dve.wait_ge(dve_step, steps[0])

            dve.sem_inc(proj_free, 2)
            dve.memset(eps[:, :], EPS).then_inc(eps_set, 1)
            for k in range(KC - 1):
                dve.wait_ge(x_hi_done, k + 1)
                dve.tensor_tensor(x_lo[:, k, :], x_raw[:, k % 2, :], x_hi[:, k, :].bitcast(F32), ALU.subtract).then_inc(x_lo_done, 1)
                if k == 0:
                    dve.wait_ge(w_hi_done, 1)
                    dve.tensor_tensor(w_lo[:, 0, :], w_raw[:, 0, :], w_hi[:, 0, :].bitcast(F32), ALU.subtract).then_inc(w_lo_done, 1)
            dve.wait_ge(const_loaded, 16 * (5 + 3 * SEQ))
            dve.wait_ge(ident_step, SEQ + 3)
            step(dve.tensor_copy(c["tok_f"][:, :], c["tok_i"][:, :]))
            step(dve.tensor_copy(c["key_f"][:, :], key_i[:, :]))
            step(dve.tensor_scalar(c["vrow"][:, :], c["vrow"][:, :], float(PSIZE), c["tok_f"][:, 0:1], ALU.mult, ALU.add))
            step(dve.tensor_scalar(c["subj"][:, :], c["subj"][:, :], float(S), c["tok_f"][:, 0:1], ALU.mult, ALU.add))
            step(dve.tensor_copy(c["len_f"][:, :], c["len_all"][:, :]))
            step(dve.tensor_scalar(c["causal"][:, :], c["key_f"][:, 0:S], c["tok_f"][:, 0:1], OUT_OF_REACH, ALU.is_gt, ALU.mult))
            dve.memset(c["own_seq"][:, :], 0.0).then_inc(own_set, 1)
            dve.wait_ge(own_set, 1)
            for s in range(SEQ):
                dve.memset(c["own_seq"][s * S:(s + 1) * S, s:s + 1], 1.0).then_inc(own_set, 1)
            step(dve.tensor_copy(pos_f, len_i))
            step(dve.tensor_scalar(pos_f, pos_f, c["tok_f"][:, 0:1], None, ALU.add))
            step(dve.tensor_tensor(angle, pos_f.rearrange("p (t o) -> p t o", o=1).to_broadcast([P, TILES, HALF]),
                                   freq.rearrange("p (o f) -> p o f", o=1).to_broadcast([P, TILES, HALF]), ALU.mult))
            magic = 1.5 * 2.0 ** 23
            step(dve.tensor_scalar(turns, angle, 1.0 / (2 * math.pi), magic, ALU.mult, ALU.add))
            step(dve.tensor_scalar(turns, turns, magic, None, ALU.subtract))
            c1 = 6.28125
            c2 = math.floor((2 * math.pi - c1) * 2 ** 22) / 2 ** 22
            c3 = 2 * math.pi - c1 - c2
            for part in (c1, c2, c3):
                step(dve.scalar_tensor_tensor(out=angle, in0=turns, scalar=-part, in1=angle, op0=ALU.mult, op1=ALU.add))
            edge = math.pi * (1 - 1e-7)
            dve.tensor_scalar(angle, angle, edge, -edge, ALU.min, ALU.max).then_inc(pos_ready, 1)
            dve.wait_ge(sines, 2)
            step(dve.tensor_tensor(cos_t, cos_t, cos_t, ALU.mult))
            step(dve.tensor_scalar(cos_t, cos_t, -2.0, 1.0, ALU.mult, ALU.add))
            for tab, row in ((tab_q, wq_row), (tab_k, wk_row)):
                for half in range(2):
                    cols = slice(half * HALF, (half + 1) * HALF)
                    other = slice((1 - half) * HALF, (2 - half) * HALF)

                    def w(part):
                        return row[:, part].rearrange("p (o f) -> p o f", o=1).to_broadcast([P, TILES, HALF])
                    step(dve.tensor_tensor(tab[:, 0, :, cols], cos_t, w(cols), ALU.mult))
                    step(dve.tensor_tensor(tab[:, 1, :, cols], sin_t, w(other), ALU.mult))
                step(dve.tensor_scalar(tab[:, 1, :, 0:HALF], tab[:, 1, :, 0:HALF], -1.0, None, ALU.mult))
            before = steps[0]

            def unit(i, cb, u, tab):
                n = i * 2 * UN + cb * UN + u
                m = n * 6 + before
                ss, rt = sumsq[:, u % 2, :], root[:, u % 2, :]
                dve.wait_ge(root_done, n * 2 + 2)
                dve.tensor_scalar(nw[:, 0, :], ss, 1.0 / D, EPS, ALU.mult, ALU.add).then_inc(dve_step, 1)
                dve.reciprocal(nw[:, 1, :], rt).then_inc(dve_step, 1)
                dve.wait_ge(dve_step, m + 2)
                dve.tensor_tensor(nw[:, 2, :], nw[:, 1, :], nw[:, 1, :], ALU.mult).then_inc(dve_step, 1)
                dve.wait_ge(dve_step, m + 3)
                dve.tensor_tensor(nw[:, 2, :], nw[:, 2, :], nw[:, 0, :], ALU.mult).then_inc(dve_step, 1)
                dve.wait_ge(dve_step, m + 4)
                dve.tensor_scalar(nw[:, 2, :], nw[:, 2, :], -0.5, 1.5, ALU.mult, ALU.add).then_inc(dve_step, 1)
                dve.wait_ge(dve_step, m + 5)
                dve.tensor_tensor(nw[:, 3, :], nw[:, 2, :], nw[:, 1, :], ALU.mult).then_inc(dve_step, 1)
                dve.wait_ge(dve_step, m + 6)
                dve.tensor_tensor(unit_rows[:, :].rearrange("p (h d) -> p h d", d=D),
                                  ps_proj[:, u % 2, :, :].rearrange("p t (g d) -> p (t g) d", d=D),
                                  nw[:, 3, :].rearrange("p (h o) -> p h o", o=1).to_broadcast([P, 8, D]),
                                  ALU.mult).then_inc(proj_free, 1)
                dve.wait_ge(proj_free, n + 3)
                dve.wait_ge(rotated, n + 1)
                for t in range(2):
                    q3 = unit_rows[:, t * 512:(t + 1) * 512].rearrange("p (g d) -> p g d", d=D)
                    cos3 = tab[:, 0, 2 * u + t, :].rearrange("p (o d) -> p o d", o=1).to_broadcast([P, G, D])
                    dve.tensor_tensor(by_cos[:, t * 512:(t + 1) * 512].rearrange("p (g d) -> p g d", d=D), q3, cos3, ALU.mult)
                    for half in range(2):
                        cols = slice(half * HALF, (half + 1) * HALF)
                        other = slice((1 - half) * HALF, (2 - half) * HALF)
                        sin3 = tab[:, 1, 2 * u + t, cols].rearrange("p (o d) -> p o d", o=1).to_broadcast([P, G, HALF])
                        k = dve.tensor_tensor(by_sin[:, t * 512:(t + 1) * 512].rearrange("p (g d) -> p g d", d=D)[:, :, cols],
                                              q3[:, :, other], sin3, ALU.mult)
                k.then_inc(halves_done, 1)

            def split(cb, slot, q):
                part = slice(q * 512, (q + 1) * 512)
                dve.wait_ge(w_hi_done, (cb - 1) * KC + q + 2)
                m = dve.tensor_tensor(w_lo[:, slot, part], w_raw[:, slot, part], w_hi[:, slot, part].bitcast(F32), ALU.subtract)
                if q == KC - 1:
                    m.then_inc(w_lo_done, 1)

            with dve.Fori(0, 4) as i:
                for cb in range(2):
                    for u in range(UN):
                        unit(i, cb, u, tab_q)
                        if 1 <= u <= KC:
                            split(i * 2 + cb + 1, (cb + 1) % 2, u - 1)
            for cb in range(2):
                for u in range(UN):
                    unit(4, cb, u, tab_k)
                    if 1 <= u <= KC:
                        split(9 + cb, (cb + 1) % 2, u - 1)
            for q in range(KC):
                split(11, 1, q)

        @block.tensor
        def _(pe):
            def project(n, blk, slot, u):
                if u == 0:
                    pe.wait_ge(w_lo_done, blk + 1)
                if isinstance(n, int) and n >= 82:
                    pe.wait_ge(v_copied, n - 81)
                else:
                    pe.wait_ge(proj_free, n + 1)
                for t in range(2):
                    cols = slice((2 * u + t) * P, (2 * u + t + 1) * P)
                    for k in range(KC):
                        w = slice(k * 512, (k + 1) * 512)
                        m = split_product(pe, ps_proj[:, u % 2, t, :], x_hi[:, k, cols], x_lo[:, k, cols],
                                          w_hi[:, slot, w], w_lo[:, slot, w], k == 0, k == KC - 1)
                m.then_inc(proj_done, 1)

            def turn(n, u):
                pe.wait_ge(rotated, n + 2)
                pe.wait_ge(turned_done, n + 1)
                for t in range(2):
                    for g in range(G):
                        j = t * G + g
                        m = pe.transpose(ps_turn[:, u % 2, t, g * P:(g + 1) * P], turning[:, u % 2, j * P:(j + 1) * P], c["ident"][:, :])
                m.then_inc(turn_done, 1)

            def block_of(i, cb, kind):
                for u in range(UN):
                    n = i * 2 * UN + cb * UN + u
                    blk = i * 2 + cb
                    if u < UN - 2:
                        project(n + 2, blk, cb, u + 2)
                    elif not (kind == "v" and cb == 1):
                        project(n + 2, blk + 1, 1 - cb, u + 2 - UN)
                    if kind != "v":
                        turn(n, u)

            pe.sem_inc(turn_done, 2)
            pe.wait_ge(x_lo_done, KC)
            pe.wait_ge(ident_step, SEQ + 3)
            project(0, 0, 0, 0)
            project(1, 0, 0, 1)
            with pe.Fori(0, 4) as i:
                for cb in range(2):
                    block_of(i, cb, "q")
            for cb in range(2):
                block_of(4, cb, "k")
            for cb in range(2):
                block_of(5, cb, "v")


def stage2(nc, c, a, scratch):
    with ExitStack() as opened:
        hold = opened.enter_context
        N2 = 2 * HK
        Q = 4
        DVE_PAGES = 9
        LAST = B // 2 - 1
        k_pool = c["k_pool"][:, :].rearrange("p (a n) -> p a n", a=PAGES)
        k_cached = hold(nc.sbuf_tensor("k_cached", [P, 2, NPP, HK * PSIZE], F32))
        v_cached = hold(nc.sbuf_tensor("v_cached", [P, 2, 4, HK * D], F32))
        k_own = hold(nc.sbuf_tensor("k_own", [P, 2, HK * S], F32))
        v_own = hold(nc.sbuf_tensor("v_own", [P, 2, HK // Q, D], F32))
        q_t = hold(nc.sbuf_tensor("q_t", [P, 2, HK, GS], F32))
        reach = hold(nc.sbuf_tensor("reach", [P, 2, L], BF16))
        masked = hold(nc.sbuf_tensor("masked", [P, 2 * Q, L + S], F32))
        probs = hold(nc.sbuf_tensor("probs", [P, 2, L + S], F32))
        weights = hold(nc.sbuf_tensor("weights", [P, 2, L], F32))
        own_w = hold(nc.sbuf_tensor("own_w", [P, 2, Q * S], F32))
        weights_t = hold(nc.sbuf_tensor("weights_t", [P, 2, L], F32))
        own_t = hold(nc.sbuf_tensor("own_t", [P, 2, GS], F32))
        o_t = hold(nc.sbuf_tensor("o_t", [P, 2, Q * GS], F32))
        own_top = hold(nc.sbuf_tensor("own_top", [P, 2, Q], F32))
        top = hold(nc.sbuf_tensor("top", [P, 4], F32))
        shift = hold(nc.sbuf_tensor("shift", [P, 4], F32))
        total = hold(nc.sbuf_tensor("total", [P, 4], F32))
        inv = hold(nc.sbuf_tensor("inv", [P, 4], F32))
        rows_now = hold(nc.sbuf_tensor("rows_now", [P, 2, 4], I32))
        ps_scores = hold(nc.psum_tensor("ps_scores", [P, 2, 512], F32))
        ps_own = hold(nc.psum_tensor("ps_own", [P, 512], F32))
        ps_turn2 = hold(nc.psum_tensor("ps_turn2", [P, 512], F32))
        ps_o = hold(nc.psum_tensor("ps_o", [P, Q, 512], F32))
        pool_loaded = c["pool_loaded"]
        own_loaded = [hold(nc.semaphore(f"own_loaded{k}")) for k in range(2)]
        v_loaded = [hold(nc.semaphore(f"v_loaded{k}")) for k in range(2)]
        k_by_dve = hold(nc.semaphore("k_by_dve"))
        k_by_pool = hold(nc.semaphore("k_by_pool"))
        rows_ready = hold(nc.semaphore("rows_ready"))
        scores_done = hold(nc.semaphore("scores_done"))
        own_scored = hold(nc.semaphore("own_scored"))
        own_read = hold(nc.semaphore("own_read"))
        top_done = hold(nc.semaphore("top_done"))
        shift_done = hold(nc.semaphore("shift_done"))
        exp_done = hold(nc.semaphore("exp_done"))
        inv_done = hold(nc.semaphore("inv_done"))
        w_done = hold(nc.semaphore("w_done"))
        turns_done = hold(nc.semaphore("turns_done"))
        own_turned = hold(nc.semaphore("own_turned"))
        wt_done = hold(nc.semaphore("wt_done"))
        own_t_done = hold(nc.semaphore("own_t_done"))
        pv_done = hold(nc.semaphore("pv_done"))
        group_done = hold(nc.semaphore("group_done"))
        o_bank_free = hold(nc.semaphore("o_bank_free"))
        o_store_free = [hold(nc.semaphore(f"o_store{k}_free")) for k in range(2)]
        reach_done = hold(nc.semaphore("reach_done"))
        dve_passed = hold(nc.semaphore("dve_passed"))
        pool_passed = hold(nc.semaphore("pool_passed"))
        block = hold(nc.Block())

        def pages_of(engine, b, first, count):
            return nc.values_load_multi_w_load_instructions(
                c["table"][0:1, bass.ds(b * NPP + first, count)], engines=(engine,), min_val=0, max_val=PAGES - 1,
                skip_runtime_bounds_check_because="the reference's indices lie in the pool")[1]

        @block.sync
        def _(sp):
            def load_own(b, slot):
                sp.dma_start(q_t[:, slot, :, :], scratch["qT"][bass.ds(b, 1)].rearrange("o p h n -> p (o h) n")).then_inc(own_loaded[slot], 16)
                sp.dma_start(k_own[:, slot, :], scratch["kT"][bass.ds(b, 1)].rearrange("o p h n -> p (o h n)")).then_inc(own_loaded[slot], 16)
                for q in range(Q):
                    sp.dma_start(v_own[q * S:(q + 1) * S, slot, :, :],
                                 scratch["v"][bass.ds(b * S, S), :].rearrange("s (g q d) -> s g q d", q=Q, d=D)[:, :, q, :]
                                 ).then_inc(own_loaded[slot], 16)

            for k in range(2):
                sp.sem_inc(o_store_free[k], 16)
            load_own(0, 0)

            def pair_of(i, last):
                for j in range(2):
                    b = i * 2 + j
                    if not (last and j == 1):
                        sp.wait_ge(pv_done, b * HK + 1)
                        load_own(b + 1, 1 - j)
                    for g in range(2):
                        sp.wait_ge(o_bank_free, b * 2 + g + 3)
                        dst = scratch["oT"][bass.ds(b, 1), :, g * Q:(g + 1) * Q, :]
                        sp.dma_start(dst.rearrange("o p h n -> p (o h n)"), o_t[:, g, :]).then_inc(o_store_free[g], 16)

            with sp.Fori(0, LAST) as i:
                pair_of(i, False)
            pair_of(LAST, True)
            for k in range(2):
                sp.wait_ge(o_store_free[k], 16 + 16 * B)

        @block.gpsimd
        def _(pool):
            def gather_v(b, slot):
                pool.tensor_copy(rows_now[:, slot, :], c["vrow"][:, bass.ds(b * 4, 4)]).then_inc(rows_ready, 1)
                pool.wait_ge(rows_ready, b + 1)
                pool.sem_inc(pool_passed)
                for k in range(4):
                    pool.indirect_dma_start(out=v_cached[:, slot, k, :], out_offset=None, in_=a["vpool"],
                                            in_offset=bass.IndirectOffsetOnAxis(ap=rows_now[:, slot, k:k + 1], axis=0)
                                            ).then_inc(v_loaded[slot], 16)

            def gather_k(b, slot):
                page = pages_of(mybir.EngineType.Pool, b, DVE_PAGES, NPP - DVE_PAGES)
                for k in range(NPP - DVE_PAGES):
                    m = pool.tensor_copy(k_cached[:, slot, DVE_PAGES + k, :], k_pool[:, bass.ds(page[k], 1), :].rearrange("p o n -> p (o n)"))
                m.then_inc(k_by_pool, 1)

            gather_v(0, 0)
            pool.wait_ge(pool_loaded, 16 * 13)
            gather_k(0, 0)
            gather_k(1, 1)

            def pair_of(i, last):
                for j in range(2):
                    b = i * 2 + j
                    if not (last and j == 1):
                        pool.wait_ge(pv_done, b * HK + 1)
                        pool.sem_inc(pool_passed)
                        gather_v(b + 1, 1 - j)
                    if not last:
                        pool.wait_ge(scores_done, b * HK + HK)
                        pool.sem_inc(pool_passed)
                        gather_k(b + 2, j)

            with pool.Fori(0, LAST) as i:
                pair_of(i, False)
            pair_of(LAST, True)

        @block.scalar
        def _(act):
            act.sem_inc(o_bank_free, 2)

            def exps(n, k):
                act.wait_ge(shift_done, n + 1)
                act.activation(probs[:, k % 2, :], masked[:, k % 8, :], ACT.Exp, bias=shift[:, k % 4:k % 4 + 1], scale=SCALE,
                               accum_out=total[:, k % 4:k % 4 + 1]).then_inc(exp_done, 1)

            exps(0, 0)
            exps(1, 1)

            def pair_of(i, last):
                for k in range(N2):
                    n = i * N2 + k
                    act.wait_ge(turns_done, n + 1)
                    act.activation(weights_t[:, k % 2, :], ps_turn2[:, :], ACT.Copy).then_inc(wt_done, 1)
                    if k % Q == Q - 1:
                        act.wait_ge(own_turned, i * Q + k // Q + 1)
                        act.activation(own_t[:, k // Q % 2, :], ps_own[:, Q * S:Q * S + GS], ACT.Copy).then_inc(own_t_done, 1)
                    if not (last and k >= N2 - 2):
                        exps(n + 2, k + 2)
                    if k % Q == Q - 1:
                        g = k // Q
                        act.wait_ge(group_done, i * Q + g + 1)
                        act.wait_ge(o_store_free[g % 2], i * 32 + (g // 2) * 16 + 16)
                        act.activation(o_t[:, g % 2, :].rearrange("p (q n) -> p q n", q=Q), ps_o[:, :, (g % 2) * GS:(g % 2 + 1) * GS], ACT.Copy).then_inc(o_bank_free, 1)

            with act.Fori(0, LAST) as i:
                pair_of(i, False)
            pair_of(LAST, True)

        @block.vector
        def _(dve):
            def reach_of(b, slot):
                dve.tensor_scalar(reach[:, slot, :], c["key_f"][:, :], c["len_f"][:, bass.ds(b, 1)], OUT_OF_REACH,
                                  ALU.is_ge, ALU.mult).then_inc(reach_done, 1)

            def own_part(grp, slot):
                dve.wait_ge(own_scored, grp + 1)
                src = ps_own[:, 0:Q * S].rearrange("p (h s) -> p h s", s=S)
                dve.tensor_copy(masked[:, slot * Q:(slot + 1) * Q, L:L + S], src)
                dve.tensor_reduce(own_top[:, slot, :], src, AX.X, ALU.max).then_inc(own_read, 1)

            def maximum(n, k, b):
                dve.wait_ge(scores_done, n + 1)
                dve.wait_ge(reach_done, b + 1)
                dve.sem_inc(dve_passed)
                dve.tensor_tensor_reduce(masked[:, k % 8, 0:L], ps_scores[:, k % 2, :], reach[:, (k // HK) % 2, :], 1.0,
                                         -3.0e38, ALU.add, ALU.max, top[:, k % 4:k % 4 + 1]).then_inc(top_done, 1)
                dve.wait_ge(top_done, n + 1)
                if k % Q == 0:
                    dve.wait_ge(own_read, b * 2 + (k // Q) % 2 + 1)
                dve.tensor_scalar(shift[:, k % 4:k % 4 + 1], top[:, k % 4:k % 4 + 1],
                                  own_top[:, (k // Q) % 2, k % Q:k % Q + 1], -SCALE, ALU.max, ALU.mult).then_inc(shift_done, 1)

            def normalise(n, k):
                dve.wait_ge(exp_done, n + 1)
                dve.reciprocal(inv[:, k % 4:k % 4 + 1], total[:, k % 4:k % 4 + 1]).then_inc(inv_done, 1)
                dve.wait_ge(inv_done, n + 1)
                dve.tensor_scalar(weights[:, k % 2, :], probs[:, k % 2, 0:L], inv[:, k % 4:k % 4 + 1], None, ALU.mult)
                dve.tensor_scalar(own_w[:, k // Q % 2, k % Q * S:(k % Q + 1) * S], probs[:, k % 2, L:L + S],
                                  inv[:, k % 4:k % 4 + 1], None, ALU.mult).then_inc(w_done, 1)

            def gather_k(b, slot, first, count):
                page = pages_of(mybir.EngineType.DVE, b, first, count)
                for k in range(count):
                    m = dve.tensor_copy(k_cached[:, slot, first + k, :], k_pool[:, bass.ds(page[k], 1), :].rearrange("p o n -> p (o n)"))
                if first + count == DVE_PAGES:
                    m.then_inc(k_by_dve, 1)

            reach_of(0, 0)
            dve.wait_ge(pool_loaded, 16 * 13)
            gather_k(0, 0, 0, DVE_PAGES)
            gather_k(1, 1, 0, DVE_PAGES)
            own_part(0, 0)
            maximum(0, 0, 0)
            maximum(1, 1, 0)
            normalise(0, 0)
            maximum(2, 2, 0)

            def pair_of(i, last):
                for k in range(N2):
                    n = i * N2 + k
                    if k % HK == 2 and not (last and k > HK):
                        reach_of(i * 2 + k // HK + 1, 1 - k // HK)
                    if not (last and k >= N2 - 1):
                        normalise(n + 1, k + 1)
                    if not (last and k >= N2 - 3):
                        if (k + 3) % Q == 0:
                            own_part(i * Q + (k + 3) // Q, (k + 3) // Q % 2)
                        maximum(n + 3, k + 3, i * 2 + (k + 3) // HK)
                    if k % HK >= 5 and not last:
                        gather_k(i * 2 + k // HK + 2, k // HK, (k % HK - 5) * (DVE_PAGES // 3), DVE_PAGES // 3)

            with dve.Fori(0, LAST) as i:
                pair_of(i, False)
            pair_of(LAST, True)

        @block.tensor
        def _(pe):
            def scores(n, k, b, grp):
                h, j = k % HK, (k // HK) % 2
                if h == 0:
                    pe.wait_ge(own_loaded[j], (b - j) * 48 + 96)
                    pe.wait_ge(k_by_dve, b + 1)
                    pe.wait_ge(k_by_pool, b + 1)
                if not isinstance(n, int) or n >= 2:
                    pe.wait_ge(top_done, n - 1)
                pe.matmul(ps_scores[:, k % 2, :], q_t[:, j, h, :], k_cached[:, j, :, h * PSIZE:(h + 1) * PSIZE],
                          start=True, stop=True).then_inc(scores_done, 1)
                if h % Q == 0:
                    if not isinstance(grp, int) or grp >= 2:
                        pe.wait_ge(own_t_done, grp - 1)
                    for q in range(Q):
                        m = pe.matmul(ps_own[:, q * S:(q + 1) * S], q_t[:, j, h + q, :], k_own[:, j, (h + q) * S:(h + q + 1) * S],
                                      start=True, stop=True)
                    m.then_inc(own_scored, 1)

            for k in range(3):
                scores(k, k, 0, 0)

            def pair_of(i, last):
                for k in range(N2):
                    n = i * N2 + k
                    h, j, g = k % HK, k // HK, k // Q
                    pe.wait_ge(w_done, n + 1)
                    for t in range(4):
                        m = pe.transpose(ps_turn2[:, t * P:(t + 1) * P], weights[:, k % 2, t * P:(t + 1) * P], c["ident"][:, :])
                    m.then_inc(turns_done, 1)
                    if k % Q == Q - 1:
                        pe.transpose(ps_own[:, Q * S:Q * S + GS], own_w[:, g % 2, :], c["ident"][:, :]).then_inc(own_turned, 1)
                    if not (last and k >= N2 - 3):
                        scores(n + 3, k + 3, i * 2 + (k + 3) // HK, i * Q + (k + 3) // Q)
                    if h == 0:
                        pe.wait_ge(v_loaded[j], i * 64 + 64)
                    if k % Q == 0:
                        pe.wait_ge(o_bank_free, i * Q + g + 1)
                    pe.wait_ge(wt_done, n + 1)
                    rows_of = slice((g % 2) * GS, (g % 2 + 1) * GS)
                    for t in range(4):
                        m = pe.matmul(ps_o[:, k % Q, rows_of], v_cached[:, j, t, h * D:(h + 1) * D],
                                      weights_t[:, k % 2, t * P:(t + 1) * P], start=t == 0, stop=False, skip_group_check=True)
                    m.then_inc(pv_done, 1)
                    if k % Q == Q - 1:
                        pe.wait_ge(own_t_done, i * Q + g + 1)
                        for q in range(Q):
                            own = slice(q * S, (q + 1) * S)
                            m = pe.matmul(ps_o[:, q, rows_of], v_own[own, j, g % 2, :], own_t[own, g % 2, :],
                                          start=False, stop=True, skip_group_check=True)
                        m.then_inc(group_done, 1)

            with pe.Fori(0, LAST) as i:
                pair_of(i, False)
            pair_of(LAST, True)


def over_heads(nc, name, w_in, heads, result, tokens_first, ready, loads, beside):
    with ExitStack() as opened:
        hold = opened.enter_context
        w_raw = hold(nc.sbuf_tensor(f"{name}_w_raw", [P, 2, G, HID], F32))
        w_hi = hold(nc.sbuf_tensor(f"{name}_w_hi", [P, 2, G, HID], F32R))
        w_lo = hold(nc.sbuf_tensor(f"{name}_w_lo", [P, 2, G, HID], F32R))
        h_raw = hold(nc.sbuf_tensor(f"{name}_h_raw", [P, 2, BS, GS], F32))
        h_hi = hold(nc.sbuf_tensor(f"{name}_h_hi", [P, 2, G, SPAN], F32R))
        h_lo = hold(nc.sbuf_tensor(f"{name}_h_lo", [P, 2, G, SPAN], F32R))
        ps = hold(nc.psum_tensor(f"{name}_ps", [P, 2, 4, 512], F32))
        w_loaded = [hold(nc.semaphore(f"{name}_w_loaded{k}")) for k in range(2)]
        h_loaded = [hold(nc.semaphore(f"{name}_h_loaded{k}")) for k in range(2)]
        w_hi_done = hold(nc.semaphore(f"{name}_w_hi_done"))
        w_lo_done = hold(nc.semaphore(f"{name}_w_lo_done"))
        h_hi_done = hold(nc.semaphore(f"{name}_h_hi_done"))
        h_lo_done = hold(nc.semaphore(f"{name}_h_lo_done"))
        unit_done = hold(nc.semaphore(f"{name}_unit_done"))
        bank_free = hold(nc.semaphore(f"{name}_bank_free"))
        block = hold(nc.Block())
        UN = 2 * NT
        LAST = HK // 2 - 1

        @block.sync
        def _(sp):
            def load_w(grp, slot):
                sp.dma_start(w_raw[:, slot, :, :],
                             w_in[bass.ds(grp, 1)].rearrange("o p (g n) -> p (o g) n", g=G)).then_inc(w_loaded[slot], 16)

            def load_h(grp, span, slot):
                sp.dma_start(h_raw[:, slot, :, :], heads[span * BS:(span + 1) * BS, :, bass.ds(grp, 1), :]
                             .rearrange("b p o n -> p b (o n)")).then_inc(h_loaded[slot], 16)

            load_w(0, 0)
            load_h(0, 0, 0)
            load_h(0, 1, 1)
            loads(sp)
            load_w(1, 1)

            def groups(i, last):
                for k in range(UN):
                    if k % NT == 1 and not last:
                        sp.wait_ge(w_lo_done, i * 2 + k // NT + 1)
                        load_w(i * 2 + k // NT + 2, k // NT)
                    if not (last and k >= UN - 2):
                        sp.wait_ge(h_lo_done, i * UN + k + 1)
                        load_h(i * 2 + (k + 2) // NT, (k + 2) % NT, k % 2)

            with sp.Fori(0, LAST) as i:
                groups(i, False)
            groups(LAST, True)

        @block.gpsimd
        def _(pool):
            beside(pool)

        @block.scalar
        def _(act):
            def split_w(slot, load):
                act.wait_ge(w_loaded[slot], load * 16 + 16)
                act.activation(w_hi[:, slot, :, :], w_raw[:, slot, :, :], ACT.Copy).then_inc(w_hi_done, 1)

            split_w(0, 0)

            def groups(i, last):
                for k in range(UN):
                    n = i * UN + k
                    act.wait_ge(h_loaded[k % 2], i * (UN * 8) + (k // 2) * 16 + 16)
                    if not isinstance(n, int) or n >= 2:
                        act.wait_ge(unit_done, n - 1)
                    act.activation(h_hi[:, k % 2, :, :].rearrange("p g (b s) -> p b g s", s=S),
                                   h_raw[:, k % 2, :, :].rearrange("p b (g s) -> p b g s", s=S), ACT.Copy).then_inc(h_hi_done, 1)
                    if k % NT == 2 and not (last and k > NT):
                        split_w(1 - k // NT, i + k // NT)

            groups(0, False)
            with act.Fori(1, LAST) as i:
                groups(i, False)
            groups(LAST, True)

        @block.vector
        def _(dve):
            dve.sem_inc(bank_free, 2)

            def split_w(grp, slot):
                dve.wait_ge(w_hi_done, grp + 1)
                dve.tensor_tensor(w_lo[:, slot, :, :], w_raw[:, slot, :, :], w_hi[:, slot, :, :].bitcast(F32),
                                  ALU.subtract).then_inc(w_lo_done, 1)

            def split_h(n, slot):
                dve.wait_ge(h_hi_done, n + 1)
                dve.tensor_tensor(h_lo[:, slot, :, :].rearrange("p g (b s) -> p b g s", s=S),
                                  h_raw[:, slot, :, :].rearrange("p b (g s) -> p b g s", s=S),
                                  h_hi[:, slot, :, :].bitcast(F32).rearrange("p g (b s) -> p b g s", s=S),
                                  ALU.subtract).then_inc(h_lo_done, 1)

            split_w(0, 0)
            split_h(0, 0)

            def groups(i, last):
                for k in range(UN):
                    n = i * UN + k
                    if not (last and k == UN - 1):
                        split_h(n + 1, (k + 1) % 2)
                    if k % NT == 2 and not (last and k > NT):
                        split_w(i * 2 + k // NT + 1, 1 - k // NT)
                    if isinstance(n, int) and n == 0:
                        dve.wait_ge(*ready)
                    dve.wait_ge(unit_done, n + 1)
                    for j in range(4):
                        part = result(k % NT, j)
                        m = dve.tensor_tensor(part, part, ps[:, k % 2, j, :], ALU.add)
                    m.then_inc(bank_free, 1)

            groups(0, False)
            with dve.Fori(1, LAST) as i:
                groups(i, False)
            groups(LAST, True)

        @block.tensor
        def _(pe):
            def groups(i):
                for k in range(UN):
                    n = i * UN + k
                    w, s = k // NT, k % 2
                    if k % NT == 0:
                        pe.wait_ge(w_lo_done, i * 2 + k // NT + 1)
                    pe.wait_ge(h_lo_done, n + 1)
                    pe.wait_ge(bank_free, n + 1)
                    for j in range(4):
                        cols = slice(j * P, (j + 1) * P)
                        for g in range(G):
                            if tokens_first:
                                m = split_product(pe, ps[:, s, j, :], h_hi[:, s, g, cols], h_lo[:, s, g, cols],
                                                  w_hi[:, w, g, :], w_lo[:, w, g, :], g == 0, g == G - 1)
                            else:
                                m = split_product(pe, ps[:, s, j, :], w_hi[:, w, g, cols], w_lo[:, w, g, cols],
                                                  h_hi[:, s, g, :], h_lo[:, s, g, :], g == 0, g == G - 1)
                    m.then_inc(unit_done, 1)

            with pe.Fori(0, HK // 2) as i:
                groups(i)


def values_of_y(nc, a, scratch, y, y_hi, y_lo, first_w):
    with ExitStack() as opened:
        hold = opened.enter_context
        BANKS = 6
        w_raw = hold(nc.sbuf_tensor("yv_w_raw", [P, KC, HK * D], F32))
        w_hi = hold(nc.sbuf_tensor("yv_w_hi", [P, KC, HK * D], F32R))
        w_lo = hold(nc.sbuf_tensor("yv_w_lo", [P, KC, HK * D], F32R))
        rows = hold(nc.sbuf_tensor("yv_rows", [P, 3, HK * D], F32))
        ps_v = hold(nc.psum_tensor("yv_ps", [P, BANKS, 512], F32))
        w_loaded = [hold(nc.semaphore(f"yv_w_loaded{k}")) for k in range(2)]
        w_hi_done = hold(nc.semaphore("yv_w_hi_done"))
        w_lo_done = hold(nc.semaphore("yv_w_lo_done"))
        y_hi_done = hold(nc.semaphore("yv_y_hi_done"))
        y_lo_done = hold(nc.semaphore("yv_y_lo_done"))
        v_done = hold(nc.semaphore("yv_v_done"))
        by_act = hold(nc.semaphore("yv_by_act"))
        by_dve = hold(nc.semaphore("yv_by_dve"))
        stored = [hold(nc.semaphore(f"yv_stored{k}")) for k in range(3)]
        block = hold(nc.Block())

        @block.sync
        def _(sp):
            for half in range(2):
                cols = slice(half * 512, (half + 1) * 512)
                sp.dma_start(w_raw[:, :, cols], a["wv2"].rearrange("p (k n) -> p k n", k=KC)[:, :, cols]).then_inc(w_loaded[half], 16)
            sp.dma_start(first_w[0][:, :, :].rearrange("p k n -> p (k n)"), a["w2"][0]).then_inc(first_w[1], 16)
            for t in range(TILES):
                sp.wait_ge(by_act, t + 1)
                sp.wait_ge(by_dve, t + 1)
                sp.dma_start(scratch["v"][t * P:(t + 1) * P, :], rows[:, t % 3, :]).then_inc(stored[t % 3], 16)
            for k in range(3):
                sp.wait_ge(stored[k], 16 * len(range(k, TILES, 3)))

        @block.scalar
        def _(act):
            def y_high(span):
                toks = slice(span * SPAN, (span + 1) * SPAN)
                act.activation(y_hi[:, :, toks], y[:, :, toks], ACT.Copy).then_inc(y_hi_done, 1)

            y_high(0)
            for half in range(2):
                cols = slice(half * 512, (half + 1) * 512)
                act.wait_ge(w_loaded[half], 16)
                act.activation(w_hi[:, :, cols], w_raw[:, :, cols], ACT.Copy).then_inc(w_hi_done, 1)
            for t in range(TILES):
                if t % 4 == 0 and t // 4 + 1 < NT:
                    y_high(t // 4 + 1)
                act.wait_ge(v_done, t * 2 + 1)
                if t >= 3:
                    act.wait_ge(stored[t % 3], 16 * (t // 3))
                act.activation(rows[:, t % 3, 0:512], ps_v[:, t * 2 % BANKS, :], ACT.Copy).then_inc(by_act, 1)

        @block.vector
        def _(dve):
            def y_low(span):
                toks = slice(span * SPAN, (span + 1) * SPAN)
                dve.wait_ge(y_hi_done, span + 1)
                dve.tensor_tensor(y_lo[:, :, toks], y[:, :, toks], y_hi[:, :, toks].bitcast(F32), ALU.subtract).then_inc(y_lo_done, 1)

            y_low(0)
            for half in range(2):
                cols = slice(half * 512, (half + 1) * 512)
                dve.wait_ge(w_hi_done, half + 1)
                dve.tensor_tensor(w_lo[:, :, cols], w_raw[:, :, cols], w_hi[:, :, cols].bitcast(F32), ALU.subtract).then_inc(w_lo_done, 1)
            for t in range(TILES):
                if t % 4 == 0 and t // 4 + 1 < NT:
                    y_low(t // 4 + 1)
                dve.wait_ge(v_done, t * 2 + 2)
                if t >= 3:
                    dve.wait_ge(stored[t % 3], 16 * (t // 3))
                dve.tensor_copy(rows[:, t % 3, 512:1024], ps_v[:, (t * 2 + 1) % BANKS, :]).then_inc(by_dve, 1)

        @block.tensor
        def _(pe):
            for t in range(TILES):
                toks = slice(t * P, (t + 1) * P)
                if t % 4 == 0:
                    pe.wait_ge(y_lo_done, t // 4 + 1)
                for half in range(2):
                    cols = slice(half * 512, (half + 1) * 512)
                    if t == 0:
                        pe.wait_ge(w_lo_done, half + 1)
                    if t >= 3:
                        pe.wait_ge(by_dve if half else by_act, t - 2)
                    for k in range(KC):
                        m = split_product(pe, ps_v[:, (t * 2 + half) % BANKS, :], y_hi[:, k, toks], y_lo[:, k, toks],
                                          w_hi[:, k, cols], w_lo[:, k, cols], k == 0, k == KC - 1)
                    m.then_inc(v_done, 1)


def stage4(nc, c, a, scratch, y_hi, y_lo, w_raw, w_loaded, residual):
    with ExitStack() as opened:
        hold = opened.enter_context
        WC = 5 * D
        w_hi = hold(nc.sbuf_tensor("s4_w_hi", [P, 2, KC, WC], F32R))
        w_lo = hold(nc.sbuf_tensor("s4_w_lo", [P, 2, KC, WC], F32R))
        q_t = hold(nc.sbuf_tensor("s4_q_t", [P, 2, BS, G, S], F32))
        k_t = hold(nc.sbuf_tensor("s4_k_t", [P, 2, SPAN], F32))
        v_r = hold(nc.sbuf_tensor("s4_v_r", [P, 2, 4, D], F32))
        scores = hold(nc.sbuf_tensor("s4_scores", [P, BS, S], F32))
        probs = hold(nc.sbuf_tensor("s4_probs", [P, BS, S], F32))
        weights = hold(nc.sbuf_tensor("s4_weights", [P, BS * S], F32))
        weights_t = hold(nc.sbuf_tensor("s4_weights_t", [P, 4, GS], F32))
        o_t = hold(nc.sbuf_tensor("s4_o_t", [P, 2, BS, GS], F32))
        top = hold(nc.sbuf_tensor("s4_top", [P, BS], F32))
        total = hold(nc.sbuf_tensor("s4_total", [P, BS], F32))
        inv = hold(nc.sbuf_tensor("s4_inv", [P, BS], F32))
        ps_proj = hold(nc.psum_tensor("s4_ps_proj", [P, 2, 512], F32))
        ps_scores = hold(nc.psum_tensor("s4_ps_scores", [P, BS, S], F32))
        ps_turn = hold(nc.psum_tensor("s4_ps_turn", [P, 4, GS], F32))
        ps_o = hold(nc.psum_tensor("s4_ps_o", [P, SEQ, 4, GS], F32))
        v_loaded = [hold(nc.semaphore(f"s4_v{k}_loaded")) for k in range(2)]
        w_hi_done = hold(nc.semaphore("s4_w_hi_done"))
        w_lo_done = hold(nc.semaphore("s4_w_lo_done"))
        proj_done = hold(nc.semaphore("s4_proj_done"))
        proj_free = hold(nc.semaphore("s4_proj_free"))
        scores_done = hold(nc.semaphore("s4_scores_done"))
        soft_step = hold(nc.semaphore("s4_soft_step"))
        exp_done = hold(nc.semaphore("s4_exp_done"))
        turn_done = hold(nc.semaphore("s4_turn_done"))
        pv_done = hold(nc.semaphore("s4_pv_done"))
        o_free = hold(nc.semaphore("s4_o_free"))
        store_free = [hold(nc.semaphore(f"s4_store{k}_free")) for k in range(2)]
        block = hold(nc.Block())
        UN = 2 * NT
        PJ = 5
        STEPS = 7
        LAST = HK // 2 - 1

        @block.sync
        def _(sp):
            for k in range(2):
                sp.sem_inc(store_free[k], 16)
            def load_v(grp, k):
                src = scratch["v"][k % NT * SPAN:(k % NT + 1) * SPAN, bass.ds(grp * D, D)]
                sp.dma_start(v_r[:, k % 2, :, :], src.rearrange("(j p) d -> p j d", p=P)).then_inc(v_loaded[k % 2], 16)

            load_v(0, 0)
            load_v(0, 1)
            sp.dma_start(residual[0][:, :, :], a["x"].rearrange("(t p) n -> p t n", p=P)).then_inc(residual[1], 16)

            def groups(i, last):
                for k in range(UN):
                    n = i * UN + k
                    if k % NT == 0 and not (last and k > 0):
                        sp.wait_ge(w_lo_done, i * 2 + k // NT + 1)
                        sp.dma_start(w_raw[:, :, :].rearrange("p k n -> p (k n)"),
                                     a["w2"][bass.ds(i * 2 + k // NT + 1, 1)].rearrange("o p n -> p (o n)")).then_inc(w_loaded, 16)
                    sp.wait_ge(o_free, n + 2)
                    if not (last and k >= UN - 2):
                        load_v(i * 2 + (k + 2) // NT, k + 2)
                    dst = scratch["aT"][k % NT * BS:(k % NT + 1) * BS, :, bass.ds(i * 2 + k // NT, 1), :]
                    sp.dma_start(dst.rearrange("b p o n -> p b (o n)"), o_t[:, k % 2, :, :]).then_inc(store_free[k % 2], 16)

            with sp.Fori(0, LAST) as i:
                groups(i, False)
            groups(LAST, True)
            for k in range(2):
                sp.wait_ge(store_free[k], 16 + 16 * HK * NT // 2)

        @block.scalar
        def _(act):
            act.sem_inc(o_free, 1)
            act.sem_inc(proj_free, 2)

            def split_w(grp, slot):
                act.wait_ge(w_loaded, grp * 16 + 16)
                act.activation(w_hi[:, slot, :, :], w_raw[:, :, :], ACT.Copy).then_inc(w_hi_done, 1)

            def copies(n, k, heads):
                for r in heads:
                    act.wait_ge(proj_done, n * PJ + r + 1)
                    src = ps_proj[:, (k * PJ + r) % 2, :]
                    if r < G:
                        m = act.activation(q_t[:, k % 2, :, r, :], src.rearrange("p (b s) -> p b s", s=S), ACT.Copy)
                    else:
                        m = act.activation(k_t[:, k % 2, :], src, ACT.Copy)
                    m.then_inc(proj_free, 1)

            split_w(0, 0)
            copies(0, 0, range(PJ))

            def groups(i, last):
                for k in range(UN):
                    n = i * UN + k
                    if not (last and k == UN - 1):
                        copies(n + 1, k + 1, range(1))
                    act.wait_ge(soft_step, n * STEPS + 3)
                    act.activation(probs[:, :, :], scores[:, :, :], ACT.Exp, scale=SCALE).then_inc(exp_done, 1)
                    if k % NT == 1 and not (last and k > NT):
                        split_w(i * 2 + k // NT + 1, 1 - k // NT)
                    if not (last and k == UN - 1):
                        copies(n + 1, k + 1, range(1, PJ))
                    act.wait_ge(pv_done, n + 1)
                    act.wait_ge(store_free[k % 2], i * (UN * 8) + (k // 2) * 16 + 16)
                    for q in range(SEQ):
                        m = act.activation(o_t[:, k % 2, q:BS:SEQ, :], ps_o[:, q, :, :], ACT.Copy)
                    m.then_inc(o_free, 1)

            with act.Fori(0, LAST) as i:
                groups(i, False)
            groups(LAST, True)

        @block.vector
        def _(dve):
            def split_w(grp, slot):
                dve.wait_ge(w_hi_done, grp + 1)
                dve.tensor_tensor(w_lo[:, slot, :, :], w_raw[:, :, :], w_hi[:, slot, :, :].bitcast(F32),
                                  ALU.subtract).then_inc(w_lo_done, 1)

            split_w(0, 0)

            def over_keys(col):
                return col.rearrange("p (b o) -> p b o", o=1).to_broadcast([P, BS, S])

            def groups(i, last):
                for k in range(UN):
                    n = i * UN + k
                    base = n * STEPS
                    causal = c["causal"][:, :].rearrange("p (o s) -> p o s", o=1).to_broadcast([P, BS, S])
                    dve.wait_ge(scores_done, n + 1)
                    dve.tensor_tensor(scores[:, :, :], ps_scores[:, :, :], causal, ALU.add).then_inc(soft_step, 1)
                    dve.wait_ge(soft_step, base + 1)
                    dve.tensor_reduce(top[:, :], scores[:, :, :], AX.X, ALU.max).then_inc(soft_step, 1)
                    dve.wait_ge(soft_step, base + 2)
                    dve.tensor_tensor(scores[:, :, :], scores[:, :, :], over_keys(top[:, :]), ALU.subtract).then_inc(soft_step, 1)
                    dve.wait_ge(exp_done, n + 1)
                    dve.tensor_reduce(total[:, :], probs[:, :, :], AX.X, ALU.add).then_inc(soft_step, 1)
                    dve.wait_ge(soft_step, base + 4)
                    dve.reciprocal(inv[:, :], total[:, :]).then_inc(soft_step, 1)
                    dve.wait_ge(soft_step, base + 5)
                    dve.tensor_tensor(weights[:, :].rearrange("p (b s) -> p b s", s=S), probs[:, :, :], over_keys(inv[:, :]),
                                      ALU.mult).then_inc(soft_step, 1)
                    if k % NT == 1 and not (last and k > NT):
                        split_w(i * 2 + k // NT + 1, 1 - k // NT)
                    dve.wait_ge(turn_done, n + 1)
                    dve.tensor_copy(weights_t[:, :, :], ps_turn[:, :, :]).then_inc(soft_step, 1)

            with dve.Fori(0, LAST) as i:
                groups(i, False)
            groups(LAST, True)

        @block.tensor
        def _(pe):
            def project(n, k, grp, heads):
                w, span = (k // NT) % 2, k % NT
                if span == 0:
                    pe.wait_ge(w_lo_done, grp + 1)
                for r in heads:
                    pe.wait_ge(proj_free, n * PJ + r + 1)
                    for q in range(KC):
                        cols = slice(r * D, (r + 1) * D)
                        toks = slice(span * SPAN, (span + 1) * SPAN)
                        m = split_product(pe, ps_proj[:, (k * PJ + r) % 2, :], w_hi[:, w, q, cols], w_lo[:, w, q, cols],
                                          y_hi[:, q, toks], y_lo[:, q, toks], q == 0, q == KC - 1)
                    m.then_inc(proj_done, 1)

            project(0, 0, 0, range(PJ))

            def groups(i, last):
                for k in range(UN):
                    n = i * UN + k
                    s = k % 2
                    pe.wait_ge(proj_free, n * PJ + PJ + 2)
                    more = not (last and k == UN - 1)
                    following = (n + 1, k + 1, i * 2 + (k + 1) // NT)
                    for first, end in ((0, BS // 4), (BS // 4, BS)):
                        for b in range(first, end):
                            m = pe.matmul(ps_scores[:, b, :], q_t[:, s, b, :, :].rearrange("p g s -> p (g s)"),
                                          k_t[:, s, b * S:(b + 1) * S], start=True, stop=True)
                        if end == BS:
                            m.then_inc(scores_done, 1)
                        if more:
                            project(*following, range(1) if first == 0 else range(1, 3))
                    pe.wait_ge(soft_step, n * STEPS + 6)
                    for j in range(4):
                        m = pe.transpose(ps_turn[:, j, :], weights[:, j * P:(j + 1) * P], c["ident"][:, :])
                    m.then_inc(turn_done, 1)
                    if more:
                        project(*following, range(3, 4))
                    pe.wait_ge(v_loaded[s], i * (UN * 8) + (k // 2) * 16 + 16)
                    pe.wait_ge(soft_step, n * STEPS + 7)
                    pe.wait_ge(o_free, n + 1)
                    for j in range(4):
                        if j == 3 and more:
                            project(*following, range(4, PJ))
                        for q in range(SEQ):
                            rows = slice(q * S, (q + 1) * S)
                            m = pe.matmul(ps_o[:, q, j, :], v_r[rows, s, j, :], weights_t[rows, j, :], start=True, stop=True)
                    m.then_inc(pv_done, 1)

            with pe.Fori(0, LAST) as i:
                groups(i, False)
            groups(LAST, True)


def stage6(nc, c, a, x2, f, out):
    with ExitStack() as opened:
        hold = opened.enter_context
        y_t = hold(nc.sbuf_tensor("s6_y_t", [P, TILES, KC * P], F32))
        mix_bd, wb, wga, lb, bias, order_i = f["mix_bd"], f["wb"], f["wga"], f["lb"], f["bias"], f["order_i"]
        loaded, mix_done, order_set = f["loaded"], f["mix_done"], f["order_set"]
        gate_h = hold(nc.sbuf_tensor("s6_gate_h", [P, TILES, E + ER], F32))
        pick = [hold(nc.sbuf_tensor(f"s6_pick{k}", [P, TILES, E], F32)) for k in range(4)]
        best = [hold(nc.sbuf_tensor(f"s6_best{k}", [P, TILES], F32)) for k in range(4)]
        order = hold(nc.sbuf_tensor("s6_order", [P, E], F32))
        hw = hold(nc.sbuf_tensor("s6_hw", [P, TILES, ER], F32))
        hw_t = hold(nc.sbuf_tensor("s6_hw_t", [P, 2, P], F32))
        done = hold(nc.sbuf_tensor("s6_done", [P, 2, HID], F32))
        ps_y = hold(nc.psum_tensor("s6_ps_y", [P, 2, 512], F32))
        ps_g = hold(nc.psum_tensor("s6_ps_g", [P, 2, 512], F32))
        ps_t = hold(nc.psum_tensor("s6_ps_t", [P, 2, 512], F32))
        ps_out = hold(nc.psum_tensor("s6_ps_out", [P, 2, 512], F32))

        def out_bank(t):
            return ps_out[:, t % 2, :] if t % 4 < 2 else ps_y[:, t % 2, :]

        step_done = hold(nc.semaphore("s6_step"))
        y_done = hold(nc.semaphore("s6_y_done"))
        y_copied = hold(nc.semaphore("s6_y_copied"))
        g_done = hold(nc.semaphore("s6_g_done"))
        g_copied = hold(nc.semaphore("s6_g_copied"))
        exp_in = hold(nc.semaphore("s6_exp_in"))
        exp_out = hold(nc.semaphore("s6_exp_out"))
        hw_done = hold(nc.semaphore("s6_hw_done"))
        t_done = hold(nc.semaphore("s6_t_done"))
        t_copied = hold(nc.semaphore("s6_t_copied"))
        out_done = hold(nc.semaphore("s6_out_done"))
        added = hold(nc.semaphore("s6_added"))
        stored = [hold(nc.semaphore(f"s6_stored{k}")) for k in range(2)]
        block = hold(nc.Block())

        @block.sync
        def _(sp):
            for t in range(TILES):
                sp.wait_ge(added, t + 1)
                sp.dma_start(out[t * P:(t + 1) * P, :], done[:, t % 2, :]).then_inc(stored[t % 2], 16)
            for k in range(2):
                sp.wait_ge(stored[k], 16 * TILES // 2)

        @block.scalar
        def _(act):
            for t in range(TILES):
                act.wait_ge(y_done, t + 1)
                act.activation(y_t[:, t, :], ps_y[:, t % 2, :], ACT.Copy).then_inc(y_copied, 1)
            act.wait_ge(exp_in, 1)
            act.activation(best[2][:, :], best[2][:, :], ACT.Exp).then_inc(exp_out, 1)
            for t in range(TILES):
                act.wait_ge(t_done, t + 1)
                act.activation(hw_t[:, t % 2, :], ps_t[:, t % 2, 0:P], ACT.Copy).then_inc(t_copied, 1)

        @block.vector
        def _(dve):
            steps = [0]

            def step(m):
                steps[0] += 1
                m.then_inc(step_done, 1)
                dve.wait_ge(step_done, steps[0])

            for t in range(TILES):
                dve.wait_ge(g_done, t + 1)
                dve.tensor_copy(gate_h[:, t, :], ps_g[:, t % 2, 0:E + ER]).then_inc(g_copied, 1)
            dve.wait_ge(g_copied, TILES)
            dve.wait_ge(order_set, 1)
            logits = gate_h[:, :, 0:E]

            def wide(col):
                return col[:, :].rearrange("p (t o) -> p t o", o=1).to_broadcast([P, TILES, E])

            step(dve.tensor_copy(order[:, :], order_i[:, :]))
            rank = order[:, :].rearrange("p (o e) -> p o e", o=1).to_broadcast([P, TILES, E])
            for k in range(2):
                src = logits if k == 0 else pick[3][:, :, :]
                step(dve.tensor_reduce(best[k][:, :], src, AX.X, ALU.max))
                step(dve.tensor_tensor(pick[k][:, :, :], src, wide(best[k]), ALU.is_equal))
                step(dve.tensor_tensor(pick[k][:, :, :], pick[k][:, :, :], rank, ALU.mult))
                step(dve.tensor_reduce(best[3][:, :], pick[k][:, :, :], AX.X, ALU.max))
                step(dve.tensor_tensor(pick[k][:, :, :], rank, wide(best[3]), ALU.is_equal))
                if k == 0:
                    step(dve.scalar_tensor_tensor(out=pick[3][:, :, :], in0=pick[0][:, :, :], scalar=OUT_OF_REACH, in1=logits,
                                                  op0=ALU.mult, op1=ALU.add))
            step(dve.tensor_tensor(best[2][:, :], best[1][:, :], best[0][:, :], ALU.subtract))
            dve.sem_inc(exp_in)
            dve.wait_ge(exp_out, 1)
            step(dve.tensor_scalar(best[0][:, :], best[2][:, :], 1.0, None, ALU.add))
            step(dve.reciprocal(best[0][:, :], best[0][:, :]))
            step(dve.tensor_tensor(best[1][:, :], best[0][:, :], best[2][:, :], ALU.mult))
            step(dve.tensor_tensor(pick[0][:, :, :], pick[0][:, :, :], wide(best[0]), ALU.mult))
            step(dve.tensor_tensor(pick[1][:, :, :], pick[1][:, :, :], wide(best[1]), ALU.mult))
            step(dve.tensor_tensor(pick[2][:, :, :], pick[0][:, :, :], pick[1][:, :, :], ALU.add))
            step(dve.tensor_tensor(hw[:, :, :].rearrange("p t (e r) -> p (t e) r", r=R),
                                   gate_h[:, :, E:].rearrange("p t (e r) -> p t e r", r=R),
                                   pick[2][:, :, :].rearrange("p t (e o) -> p t e o", o=1).to_broadcast([P, TILES, E, R]), ALU.mult))
            dve.sem_inc(hw_done)
            dve.wait_ge(loaded, 64)
            for t in range(TILES):
                step(dve.tensor_tensor(x2[:, t, :], x2[:, t, :], bias[:, :], ALU.add))
                dve.wait_ge(out_done, t + 1)
                if t >= 2:
                    dve.wait_ge(stored[t % 2], 16 * (t // 2))
                dve.tensor_tensor(done[:, t % 2, :], x2[:, t, :], out_bank(t), ALU.add).then_inc(added, 1)

        @block.tensor
        def _(pe):
            pe.wait_ge(mix_done, 1)
            pe.wait_ge(loaded, 64)

            def gate(t):
                pe.wait_ge(y_copied, t + 1)
                if t >= 2:
                    pe.wait_ge(g_copied, t - 1)
                for k in range(KC):
                    m = pe.matmul(ps_g[:, t % 2, 0:E + ER], y_t[:, t, k * P:(k + 1) * P], wga[:, k, :], start=(k == 0), stop=(k == KC - 1))
                m.then_inc(g_done, 1)

            for t in range(TILES):
                if t >= 2:
                    pe.wait_ge(y_copied, t - 1)
                for k in range(KC):
                    m = pe.matmul(ps_y[:, t % 2, k * P:(k + 1) * P], x2[:, t, k * P:(k + 1) * P], mix_bd[:, t, :], start=True, stop=True)
                m.then_inc(y_done, 1)
                if t > 0:
                    gate(t - 1)
            gate(TILES - 1)

            def base(t):
                if t >= 4:
                    pe.wait_ge(added, t - 3)
                for k in range(KC):
                    pe.matmul(out_bank(t), y_t[:, t, k * P:(k + 1) * P], wb[:, k, :], start=(k == 0), stop=False)

            base(0)
            base(1)
            for t in range(TILES):
                if t == 0:
                    pe.wait_ge(hw_done, 1)
                pe.transpose(ps_t[:, t % 2, 0:P], hw[:, t, :], c["ident"][:, :]).then_inc(t_done, 1)
                if t + 2 < TILES:
                    base(t + 2)
                pe.wait_ge(t_copied, t + 1)
                pe.matmul(out_bank(t), hw_t[:, t % 2, :], lb[:, :], start=False, stop=True).then_inc(out_done, 1)


def build(nc, a, out, scratch):
    with ExitStack() as opened:
        hold = opened.enter_context
        ident = hold(nc.sbuf_tensor("ident", [P, P], F32))
        tok_i = hold(nc.sbuf_tensor("tok_i", [P, 1], I32))
        tok_f = hold(nc.sbuf_tensor("tok_f", [P, 1], F32))
        subj = hold(nc.sbuf_tensor("subj", [P, TILES], I32))
        table = hold(nc.sbuf_tensor("table", [1, B * NPP], I32))
        causal = hold(nc.sbuf_tensor("causal", [P, S], F32))
        own_seq = hold(nc.sbuf_tensor("own_seq", [P, SEQ], F32))
        c = dict(ident=ident, tok_i=tok_i, tok_f=tok_f, subj=subj, table=table, causal=causal, own_seq=own_seq)
        with ExitStack() as parts:
            keep = parts.enter_context
            c.update(k_pool=keep(nc.sbuf_tensor("k_pool", [P, PAGES * HK * PSIZE], F32)),
                     pool_loaded=keep(nc.semaphore("pool_loaded")),
                     key_f=keep(nc.sbuf_tensor("key_f", [P, L], F32)),
                     vrow=keep(nc.sbuf_tensor("vrow", [P, B * 4], I32)),
                     len_all=keep(nc.sbuf_tensor("len_all", [P, B], I32)),
                     len_f=keep(nc.sbuf_tensor("len_f", [P, B], F32)))
            stage1(nc, c, a, scratch)
            stage2(nc, c, a, scratch)
        y = hold(nc.sbuf_tensor("y", [P, KC, TOK], F32))
        y_cleared = hold(nc.semaphore("y_cleared"))
        x2 = y[:, :, :].rearrange("p k n -> p (k n)").rearrange("p (t n) -> p t n", n=HID)
        x_loaded = hold(nc.semaphore("x2_loaded"))
        with ExitStack() as parts:
            y_hi = parts.enter_context(nc.sbuf_tensor("y_hi", [P, KC, TOK], F32R))
            y_lo = parts.enter_context(nc.sbuf_tensor("y_lo", [P, KC, TOK], F32R))
            w_raw = parts.enter_context(nc.sbuf_tensor("s4_w_raw", [P, KC, 5 * D], F32))
            w_loaded = parts.enter_context(nc.semaphore("s4_w_loaded"))
            over_heads(nc, "s3", a["wo"], scratch["oT"],
                       lambda span, j: y[:, j, span * SPAN:(span + 1) * SPAN], tokens_first=False,
                       ready=(y_cleared, 1), loads=lambda sp: None,
                       beside=lambda pool: pool.memset(y[:, :, :], 0.0).then_inc(y_cleared, 1))
            values_of_y(nc, a, scratch, y, y_hi, y_lo, (w_raw, w_loaded))
            stage4(nc, c, a, scratch, y_hi, y_lo, w_raw, w_loaded, (x2, x_loaded))
        mix = hold(nc.sbuf_tensor("s6_mix", [P, TILES, S], F32))
        mix_loaded = hold(nc.semaphore("s6_mix_loaded"))
        f = dict(mix_bd=hold(nc.sbuf_tensor("s6_mix_bd", [P, TILES, P], F32)),
                 wb=hold(nc.sbuf_tensor("s6_wb", [P, KC, HID], F32)),
                 wga=hold(nc.sbuf_tensor("s6_wga", [P, KC, E + ER], F32)),
                 lb=hold(nc.sbuf_tensor("s6_lb", [P, HID], F32)),
                 bias=hold(nc.sbuf_tensor("s6_bias", [P, HID], F32)),
                 order_i=hold(nc.sbuf_tensor("s6_order_i", [P, E], I32)),
                 loaded=hold(nc.semaphore("s6_loaded")), mix_done=hold(nc.semaphore("s6_mix_done")),
                 order_set=hold(nc.semaphore("s6_order_set")))

        def loads(sp):
            sp.dma_start(f["wga"][:, :, :].rearrange("p k n -> p (k n)"), a["wga"]).then_inc(f["loaded"], 16)
            sp.dma_start(f["wb"][:, :, :].rearrange("p k n -> p (k n)"), a["wb"]).then_inc(f["loaded"], 16)
            sp.dma_start(f["lb"][:, :], a["lb"]).then_inc(f["loaded"], 16)
            sp.dma_start(f["bias"][:, :], a["bias"].to_broadcast([P, HID])).then_inc(f["loaded"], 16)

        def mixes(pool):
            for t in range(TILES):
                pool.indirect_dma_start(out=mix[:, t, :], out_offset=None, in_=a["mix"],
                                        in_offset=bass.IndirectOffsetOnAxis(ap=c["subj"][:, t:t + 1], axis=0)
                                        ).then_inc(mix_loaded, 16)
            pool.iota(f["order_i"][:, :], pattern=[[-1, E]], base=E, channel_multiplier=0).then_inc(f["order_set"], 1)
            pool.wait_ge(mix_loaded, 16 * TILES)
            for s in range(SEQ):
                m = pool.tensor_tensor(f["mix_bd"][:, :, s * S:(s + 1) * S], mix[:, :, :],
                                       c["own_seq"][:, s:s + 1].rearrange("p (o q) -> p o q", o=1).to_broadcast([P, TILES, S]), ALU.mult)
            m.then_inc(f["mix_done"], 1)

        over_heads(nc, "s5", a["wd"], scratch["aT"], lambda span, j: x2[:, span * 4 + j, :], tokens_first=True,
                   ready=(x_loaded, 16), loads=loads, beside=mixes)
        stage6(nc, c, a, x2, f, out)


def kernel(x, itok_Bx16_0_63, itok_B_207_1644, itok_B_0_30, L0_cond_Wq, L0_cond_Wk, L0_cond_Wv, L0_cond_Wo,
           L0_cond_q_norm_w, L0_cond_k_norm_w, L0_cond_k_cache, L0_cond_v_cache, L0_attn_w_qkv, L0_attn_w_dense,
           L0_cond2_weights, L0_ffn_W_base, L0_ffn_b_base, L0_ffn_W_gate, L0_ffn_A, L0_ffn_B):
    import concourse.bacc as bacc
    from concourse.bass_utils import run_bass_kernel_spmd

    def laid(v):
        return np.ascontiguousarray(np.asarray(v))

    x = np.asarray(x).reshape(TOK, HID)
    w1 = np.concatenate([np.asarray(L0_cond_Wq), np.asarray(L0_cond_Wk), np.asarray(L0_cond_Wv)], 0)
    wqkv = np.asarray(L0_attn_w_qkv)
    w2 = np.concatenate([wqkv[:HQ * D].reshape(HK, G * D, HID), wqkv[HQ * D:(HQ + HK) * D].reshape(HK, D, HID)], 1)
    arrays = {
        "x": laid(x),
        "xT": laid(x.T),
        "w1": laid(w1.reshape(12, 512, KC, P).transpose(0, 3, 2, 1).reshape(12, P, KC * 512)),
        "freq": (np.float32(1.0) / np.float32(THETA) ** (np.arange(0, D, 2, dtype=np.float32) / np.float32(D))).astype(np.float32).reshape(1, HALF),
        "qw": laid(L0_cond_q_norm_w).reshape(1, D),
        "kw": laid(L0_cond_k_norm_w).reshape(1, D),
        "table": laid(itok_Bx16_0_63).reshape(1, B * NPP),
        "table_t": laid(np.asarray(itok_Bx16_0_63).reshape(B, 4, 4).transpose(2, 0, 1)).reshape(4, B * 4),
        "lens": laid(itok_B_207_1644).reshape(1, B),
        "lens_t": laid(np.asarray(itok_B_207_1644).reshape(TILES, SEQ).T),
        "subj_t": laid(np.asarray(itok_B_0_30).reshape(TILES, SEQ).T),
        "kpool": laid(np.asarray(L0_cond_k_cache).transpose(3, 0, 2, 1)).reshape(D, PAGES * HK * PSIZE),
        "vpool": laid(L0_cond_v_cache).reshape(PAGES * PSIZE, HK * D),
        "wo": laid(np.asarray(L0_cond_Wo).reshape(HID, HK, G, D).transpose(1, 3, 2, 0)).reshape(HK, D, G * HID),
        "w2": laid(w2.reshape(HK, 5 * D, KC, P).transpose(0, 3, 2, 1)).reshape(HK, P, KC * 5 * D),
        "wv2": laid(wqkv[(HQ + HK) * D:].reshape(HK * D, KC, P).transpose(2, 1, 0)).reshape(P, KC * HK * D),
        "wd": laid(np.asarray(L0_attn_w_dense).reshape(HID, HK, G, D).transpose(1, 3, 2, 0)).reshape(HK, D, G * HID),
        "mix": laid(L0_cond2_weights).reshape(S * S, S),
        "wb": laid(np.asarray(L0_ffn_W_base).reshape(HID, KC, P).transpose(2, 1, 0)).reshape(P, KC * HID),
        "wga": laid(np.concatenate([np.asarray(L0_ffn_W_gate), np.asarray(L0_ffn_A).reshape(ER, HID)], 0)
                    .reshape(E + ER, KC, P).transpose(2, 1, 0)).reshape(P, KC * (E + ER)),
        "lb": laid(np.asarray(L0_ffn_B).transpose(0, 2, 1)).reshape(ER, HID),
        "bias": laid(L0_ffn_b_base).reshape(1, HID),
    }
    nc = bacc.Bacc("TRN2", target_bir_lowering=False, num_devices=1)
    a = {k: nc.dram_tensor(k + "_in", v.shape, mybir.dt.from_np(v.dtype), kind="ExternalInput").ap() for k, v in arrays.items()}
    out = nc.dram_tensor("out", (TOK, HID), F32, kind="ExternalOutput").ap()
    scratch = {
        "qT": nc.dram_tensor("qT_scratch", (B, D, HK, GS), F32).ap(),
        "kT": nc.dram_tensor("kT_scratch", (B, D, 2, GS), F32).ap(),
        "v": nc.dram_tensor("v_scratch", (TOK, HK * D), F32).ap(),
        "oT": nc.dram_tensor("oT_scratch", (B, D, HK, GS), F32).ap(),
        "aT": nc.dram_tensor("aT_scratch", (B, D, HK, GS), F32).ap(),
    }
    build(nc, a, out, scratch)
    r = run_bass_kernel_spmd(nc, [{k + "_in": v for k, v in arrays.items()}], core_ids=[0])
    return r.results[0]["out"].reshape(B, S, HID)
```
